# Optimizing a Trainium2 kernel written in Bass

```python
import numpy as np
import jax
import jax.numpy as jnp

def _softmax(x, axis=-1):
    return jax.nn.softmax(x, axis=axis)

def _gelu(x):
    return jax.nn.gelu(x, approximate=True)

def _silu(x):
    return jax.nn.silu(x)

def _sigmoid(x):
    return jax.nn.sigmoid(x)

def _layernorm(x, axis=-1, eps=1e-05):
    m = jnp.mean(x, axis=axis, keepdims=True)
    v = jnp.var(x, axis=axis, keepdims=True)
    return (x - m) / jnp.sqrt(v + eps)

def _scatter_add(tgt, idx, src, axis=0):
    return tgt.at[idx].add(src)

def _segment_sum(src, seg, n):
    return jax.ops.segment_sum(src, seg, n)
kernel_name = 'mk_gnn_preln_d2_gnn_r32_c0e4cc'

def setup_inputs(seed: int=0):
    np.random.seed(seed)
    _w = jnp.asarray

    def _rec_inputs():
        import jax
        import jax.numpy as jnp
        _gk = jax.random.key(seed)
        x = -0.0002117 + 1 * jax.random.normal(jax.random.fold_in(_gk, 1), (3125, 256), jnp.float32)
        _s = jax.random.randint(jax.random.fold_in(_gk, 2), (25000,), 0, 3125, jnp.int32)
        _d = jax.random.randint(jax.random.fold_in(_gk, 3), (25000,), 0, 3125, jnp.int32)
        _loop = jnp.arange(3125, dtype=jnp.int32)
        src = jnp.concatenate([_s, _d, _loop])
        dst = jnp.concatenate([_d, _s, _loop])
        _o = jnp.argsort(dst, stable=True)
        src = src[_o]
        dst = dst[_o]
        edge_type_16 = jax.random.randint(jax.random.fold_in(_gk, 13), (53125,), 0, 16, jnp.int32)
        return (x, src, dst, edge_type_16)
    x, src, dst, edge_type_16 = _rec_inputs()

    def _L0_gnn_setup():
        import jax, jax.numpy as jnp
        import numpy as np
        N, D_DIM, K, R = (3125, 256, 4, 16)
        E_RAND = 50000
        ETA, LAM, C = (0.5, 0.1, 0.5)
        key = jax.random.key(seed)
        k1, k2, k3, k4 = jax.random.split(key, 4)
        Z = jax.random.normal(k1, (N, D_DIM), jnp.float32)
        U = jax.random.normal(k2, (K, D_DIM, R), jnp.float32) / np.float32(np.sqrt(D_DIM))
        Dmat = jax.random.normal(k3, (D_DIM, D_DIM), jnp.float32) / np.float32(np.sqrt(D_DIM))
        head_w = jnp.ones((K,), jnp.float32) / K
        rnd = jax.random.randint(k4, (2, E_RAND), 0, N)
        loops = jnp.stack([jnp.arange(N), jnp.arange(N)])
        edge_index = jnp.concatenate([rnd, loops], axis=1)
        return {'Z': Z, 'U': U, 'Dmat': Dmat, 'head_w': head_w, 'edge_index': edge_index}
    _L0_gnn_all = _L0_gnn_setup()
    _L0_gnn_in = {k: v for k, v in _L0_gnn_all.items() if k in ('U', 'Dmat', 'head_w')}
    del _L0_gnn_all

    def _L1_gnn_setup():
        import jax, jax.numpy as jnp
        import numpy as np
        N_NODES = 50000
        N_EDGES = 25000
        HDIM = 256
        NUMRELS = 16

        def _gru_cell(x, h, w_ih, w_hh, b_ih, b_hh):
            gi = x @ w_ih.T + b_ih
            gh = h @ w_hh.T + b_hh
            i_r, i_z, i_n = jnp.split(gi, 3, axis=-1)
            h_r, h_z, h_n = jnp.split(gh, 3, axis=-1)
            r = jax.nn.sigmoid(i_r + h_r)
            z = jax.nn.sigmoid(i_z + h_z)
            n = jnp.tanh(i_n + r * h_n)
            return (1.0 - z) * n + z * h
        key = jax.random.key(seed)
        ks = jax.random.split(key, 9)
        h = jax.random.normal(ks[0], (N_NODES, HDIM), dtype=jnp.float32)
        relvectors = jax.random.normal(ks[1], (NUMRELS, HDIM), dtype=jnp.float32)
        s = 1.0 / np.sqrt(HDIM)
        w_ih = jax.random.uniform(ks[2], (3 * HDIM, HDIM), minval=-s, maxval=s, dtype=jnp.float32)
        w_hh = jax.random.uniform(ks[3], (3 * HDIM, HDIM), minval=-s, maxval=s, dtype=jnp.float32)
        b_ih = jax.random.uniform(ks[4], (3 * HDIM,), minval=-s, maxval=s, dtype=jnp.float32)
        b_hh = jax.random.uniform(ks[5], (3 * HDIM,), minval=-s, maxval=s, dtype=jnp.float32)
        edge_src = jax.random.randint(ks[6], (N_EDGES,), 0, N_NODES, dtype=jnp.int32)
        edge_dst = jax.random.randint(ks[7], (N_EDGES,), 0, N_NODES, dtype=jnp.int32)
        edge_rel = jax.random.randint(ks[8], (N_EDGES,), 0, NUMRELS, dtype=jnp.int32)
        return {'h': h, 'relvectors': relvectors, 'w_ih': w_ih, 'w_hh': w_hh, 'b_ih': b_ih, 'b_hh': b_hh, 'edge_src': edge_src, 'edge_dst': edge_dst, 'edge_rel': edge_rel}
    _L1_gnn_all = _L1_gnn_setup()
    _L1_gnn_in = {k: v for k, v in _L1_gnn_all.items() if k in ('relvectors', 'w_ih', 'w_hh', 'b_ih', 'b_hh')}
    del _L1_gnn_all
    return {'x': x, 'src': src, 'dst': dst, 'edge_type_16': edge_type_16, 'L0_gnn_U': _L0_gnn_in['U'], 'L0_gnn_Dmat': _L0_gnn_in['Dmat'], 'L0_gnn_head_w': _L0_gnn_in['head_w'], 'L1_gnn_relvectors': _L1_gnn_in['relvectors'], 'L1_gnn_w_ih': _L1_gnn_in['w_ih'], 'L1_gnn_w_hh': _L1_gnn_in['w_hh'], 'L1_gnn_b_ih': _L1_gnn_in['b_ih'], 'L1_gnn_b_hh': _L1_gnn_in['b_hh']}

def reference(x, src, dst, edge_type_16, L0_gnn_U, L0_gnn_Dmat, L0_gnn_head_w, L1_gnn_relvectors, L1_gnn_w_ih, L1_gnn_w_hh, L1_gnn_b_ih, L1_gnn_b_hh):
    import jax
    import jax.numpy as jnp

    def _L0_gnn_ref(Z, U, Dmat, head_w, edge_index):
        import jax, jax.numpy as jnp
        import numpy as np
        N, D_DIM, K, R = (3125, 256, 4, 16)
        E_RAND = 50000
        ETA, LAM, C = (0.5, 0.1, 0.5)
        src, dst = (edge_index[0], edge_index[1])
        scale = np.float32(np.sqrt(R))
        ZU = jnp.einsum('nd,kdr->knr', Z, U)
        zs = ZU[:, src, :]
        zd = ZU[:, dst, :]
        logits = (zs * zd).sum(-1) / scale
        seg_max = jax.vmap(lambda l: jax.ops.segment_max(l, dst, num_segments=N))(logits)
        exp_l = jnp.exp(logits - seg_max[:, dst])
        seg_sum = jax.vmap(lambda e: jax.ops.segment_sum(e, dst, num_segments=N))(exp_l)
        alpha = exp_l / (seg_sum[:, dst] + 1e-16)
        weighted = alpha[..., None] * zs
        agg = jax.vmap(lambda w_: jax.ops.segment_sum(w_, dst, num_segments=N))(weighted)
        w = jax.nn.softmax(head_w)
        ssa = jnp.einsum('k,knr,kdr->nd', w, agg, U)
        Z_half = (1.0 - C) * Z + C * ssa
        DZ = Z_half @ Dmat.T
        residual = Z_half - DZ @ Dmat
        grad_step = Z_half + ETA * (residual @ Dmat)
        return jax.nn.relu(grad_step - ETA * LAM)

    def _L1_gnn_ref(h, relvectors, w_ih, w_hh, b_ih, b_hh, edge_src, edge_dst, edge_rel):
        import jax, jax.numpy as jnp
        import numpy as np
        N_NODES = 50000
        N_EDGES = 25000
        HDIM = 256
        NUMRELS = 16

        def _gru_cell(x, h, w_ih, w_hh, b_ih, b_hh):
            gi = x @ w_ih.T + b_ih
            gh = h @ w_hh.T + b_hh
            i_r, i_z, i_n = jnp.split(gi, 3, axis=-1)
            h_r, h_z, h_n = jnp.split(gh, 3, axis=-1)
            r = jax.nn.sigmoid(i_r + h_r)
            z = jax.nn.sigmoid(i_z + h_z)
            n = jnp.tanh(i_n + r * h_n)
            return (1.0 - z) * n + z * h
        msg = h[edge_src] + relvectors[edge_rel]
        red = jax.ops.segment_sum(msg, edge_dst, num_segments=h.shape[0])
        return _gru_cell(red, h, w_ih, w_hh, b_ih, b_hh)
    edge_index = jnp.stack([src, dst])
    h = jnp.maximum(_layernorm(x, axis=-1), 0.0)
    x = x + _L0_gnn_ref(h, L0_gnn_U, L0_gnn_Dmat, L0_gnn_head_w, edge_index)
    h = jnp.maximum(_layernorm(x, axis=-1), 0.0)
    x = x + _L1_gnn_ref(h, L1_gnn_relvectors, L1_gnn_w_ih, L1_gnn_w_hh, L1_gnn_b_ih, L1_gnn_b_hh, src, dst, edge_type_16)
    return x

_drawn_inputs = setup_inputs


def setup_inputs(seed=0):
    import zlib

    import numpy as np

    out = dict(_drawn_inputs(seed))
    spreads = {'L0_gnn_head_w': (0.25, 0.6)}
    factors = {'L1_gnn_b_ih': 8.0, 'L1_gnn_b_hh': 8.0}
    for name, (base, spread) in spreads.items():
        noise = np.random.default_rng([zlib.crc32(name.encode()), seed]).standard_normal(out[name].shape)
        drawn = base * np.exp(spread * noise) if base else spread * noise
        out[name] = jnp.asarray(drawn.astype(out[name].dtype))
    for name, factor in factors.items():
        out[name] = (out[name] * factor).astype(out[name].dtype)
    return out
```

```python
import concourse.bass as bass
from concourse import mybir
from contextlib import ExitStack

FRONT = 192
PAD_NODE = 1 << 20
WINDOW = 125
TILES = 18
BIG = 1.0e30


def gnn_kernel(nc, x, src, dst, kind, U, Dmat, head_w, rel, w_ih, w_hh, b_ih, b_hh, out):
    fp32, int32 = mybir.dt.float32, mybir.dt.int32
    ALU, ACT = mybir.AluOpType, mybir.ActivationFunctionType
    AXX = mybir.AxisListType.X

    N, D = x.shape
    K, _, R = U.shape
    KR = K * R
    RELS = rel.shape[0]
    G3 = w_ih.shape[0]
    W, C = WINDOW, TILES
    NW = N // W
    SPAN = C * 128
    E = src.shape[0] - FRONT - SPAN - 256
    EF = E // W
    CH = D // 128
    HALO = 386
    CHUNKS = [(0, 8), (8, 16), (16, 18)]
    PAIRS = NW // 2
    EPS, THRESH = 1e-5, 0.5 * 0.1
    assert N == NW * W and NW % 2 == 1 and E == EF * W and C == CHUNKS[-1][1]

    ctx = ExitStack()
    with ctx:
        def sb(name, shape, dt=fp32):
            return ctx.enter_context(nc.sbuf_tensor(name, shape, dt))

        def sem(name):
            return ctx.enter_context(nc.semaphore(name))

        zu_table = nc.dram_tensor("zu_table", [N, KR], fp32, kind="Internal").ap()
        h2_table = nc.dram_tensor("h2_table", [N, D], fp32, kind="Internal").ap()

        xs = sb("xs", [W, NW, D])
        zus = sb("zus", [W, NW, KR])
        base = sb("base", [W, NW, D])
        cnt_rows = sb("cnt_rows", [RELS + 1, N])
        src_col = sb("src_col", [128, NW, C], int32)
        dst_col = sb("dst_col", [128, NW, C])
        kind_col = sb("kind_col", [128, NW, C])
        ident = sb("ident", [128, 128])
        iota_w = sb("iota_w", [128, 128])
        iota_p = sb("iota_p", [128, 1])
        win_first = sb("win_first", [128, NW])
        node_id = sb("node_id", [128, NW])
        ones = sb("ones", [128, 1])
        eps_col = sb("eps_col", [128, 1])
        starts = sb("starts", [1, NW + 2], int32)
        wihT = sb("wihT", [128, CH, G3])
        whhT = sb("whhT", [128, CH, G3])
        relw = sb("relw", [RELS + 1, 4 * D])
        UV = sb("UV", [KR, D])

        shared = sb("shared", [128, 2 * C * D])
        SH = shared[:, :]

        def part(p, at, n, dt=fp32):
            v = SH[0:p, at:at + n]
            return v if dt == fp32 else v.bitcast(dt)

        rows_i = part(3 * C, 0, NW * 128, int32)
        rows_f = part(3 * C, NW * 128, NW * 128)
        at = 2 * NW * 128
        dcur = part(W, at, EF, int32)
        dnext = part(W, at + 512, EF, int32)
        dfar = part(W, at + 1024, EF, int32)
        dst_bc = [part(W, h * SPAN, SPAN, int32) for h in range(2)]
        ohT = part(W, 2 * SPAN, SPAN)
        zs = [part(128, 3 * SPAN + h * C * KR, C * KR) for h in range(2)]
        assert 3 * SPAN + 2 * C * KR <= 2 * C * D
        hg = [part(128, h * C * D, C * D).rearrange("p (j d) -> p j d", j=C) for h in range(2)]

        setup = sb("setup", [128, 3104])

        def carve(region, p, sizes):
            at, views = 0, []
            for q, size in zip(p, sizes):
                n = size if isinstance(size, int) else size[0] * size[1]
                v = region[0:q, at:at + n]
                views.append(v if isinstance(size, int) else v.rearrange("p (a b) -> p a b", a=size[0]))
                at += n
            return views

        Ds, DD, UVV, hn, hTs, junk = carve(setup, (128, 128, 128, W, 128, W),
                                           ((CH, D), (CH, D), (CH, KR + D), (2, D), (2, CH * W), EF))
        wrow, = carve(setup, (128,), ((2 * G3 // 128, D),))
        layer = sb("layer", [128, 3152])
        prod, V, cut = carve(layer, (128, 128, K * C), (C * KR, (C, KR + K), (2, HALO)))
        cntT, h2T, redT, rz, nn, dd, outs = carve(layer, (RELS + 1, 128, 128, W, W, W, W),
                                                  ((2, W), CH * W, CH * W, (2, 2 * D), D, D, (2, D)))
        cnt = sb("cnt", [W, NW + 2])
        tot = sb("tot", [1, NW + 3])
        tdiff = sb("tdiff", [1, NW])
        bad = sb("bad", [1, 2])
        hw = sb("hw", [KR, K])
        hwcol = sb("hwcol", [KR, 1])
        hst = sb("hst", [KR, 8])
        mv = sb("mv", [W, NW, 2])
        bst = sb("bst", [W, 2, 6])
        rstd = sb("rstd", [W, NW])
        nmr = sb("nmr", [W, NW])
        rels = sb("rels", [RELS, D])
        relT = sb("relT", [128, CH * RELS])
        brow = sb("brow", [1, 2, G3])
        bfull = sb("bfull", [1, 4 * D])

        halo_i = sb("halo_i", [K * C, 2, HALO], int32)
        cutf = sb("cutf", [K * C, 2, HALO])
        oh = sb("oh", [128, 2, C * W])
        ohk = sb("ohk", [128, C * RELS])
        sidx = sb("sidx", [128, 2, C], int32)
        L = sb("L", [128, C + 2, K])
        runs = sb("runs", [K * C, 2, 256])
        segmax = sb("segmax", [K * C, 128])
        dif = sb("dif", [128, C * K])
        den = sb("den", [W, 2 * K])
        aggn = sb("aggn", [W, KR])
        aggT = sb("aggT", [KR, W])
        stat = sb("stat", [W, 6])
        mvw = sb("mvw", [W, 2])
        rsw = sb("rsw", [W, 3])
        tmp = sb("tmp", [W, D])
        h2s = sb("h2s", [W, 2, D])


        banks = [ctx.enter_context(nc.psum_tensor(f"bank{i}", [128, 512], fp32)) for i in range(8)]

        def ps(i, p, a, b):
            return banks[i][0:p, a:b]

        l_dst = sem("l_dst")
        l_x = [sem(f"l_x{i}") for i in range(5)]
        l_small = sem("l_small")
        l_rows = sem("l_rows")
        l_gru = sem("l_gru")
        l_bc = [sem(f"l_bc{h}") for h in range(2)]
        l_halo = [sem(f"l_halo{h}") for h in range(2)]
        l_h2 = [sem(f"l_h2{h}") for h in range(2)]
        st_zu = sem("st_zu")
        st_h2 = sem("st_h2")
        st_out = sem("st_out")
        h2s_free = sem("h2s_free")
        outs_free = sem("outs_free")
        l_bias = sem("l_bias")
        a_relw = sem("a_relw")
        a_relT = sem("a_relT")
        p_relT = sem("p_relT")
        p_relw = sem("p_relw")
        g_zs = [[sem(f"g_zs{h}{c}") for c in range(3)] for h in range(2)]
        g_h = [[sem(f"g_h{h}{c}") for c in range(3)] for h in range(2)]
        c_pool = sem("c_pool")
        c_ident = sem("c_ident")
        c_const = sem("c_const")
        v_chk = sem("v_chk")
        v_cnt = sem("v_cnt")
        p_tot = sem("p_tot")
        starts_ready = sem("starts_ready")
        v_rowf = sem("v_rowf")
        p_col = sem("p_col")
        a_col = sem("a_col")
        p_gd = sem("p_gd")
        v_gd = sem("v_gd")
        v_head = sem("v_head")
        a_head = sem("a_head")
        v_bst = sem("v_bst")
        v_mv = sem("v_mv")
        a_rstd = sem("a_rstd")
        v_nmr = sem("v_nmr")
        a_hn = sem("a_hn")
        p_hT = sem("p_hT")
        v_hT = sem("v_hT")
        p_zub = sem("p_zub")
        v_zu = sem("v_zu")
        p_wT = sem("p_wT")
        a_wT = sem("a_wT")
        v_bias = sem("v_bias")
        oht_made = sem("oht_made")
        oh_made = sem("oh_made")
        ohk_made = sem("ohk_made")
        cut_raw = sem("cut_raw")
        cut_made = sem("cut_made")
        zd_made = [sem(f"zd_made{c}") for c in range(3)]
        cnt_made = sem("cnt_made")
        cnt_kept = sem("cnt_kept")
        prod_made = sem("prod_made")
        L_made = sem("L_made")
        LT_made = sem("LT_made")
        runs_made = sem("runs_made")
        segmax_made = sem("segmax_made")
        mT_made = sem("mT_made")
        dif_made = sem("dif_made")
        P_made = sem("P_made")
        V_made = sem("V_made")
        agg_made = sem("agg_made")
        den_made = sem("den_made")
        aggn_made = sem("aggn_made")
        aggT_made = sem("aggT_made")
        aggT_kept = sem("aggT_kept")
        grad_made = sem("grad_made")
        x1_made = sem("x1_made")
        stat_made = sem("stat_made")
        var_made = sem("var_made")
        ln_made = sem("ln_made")
        rsw_made = sem("rsw_made")
        h2_made = sem("h2_made")
        sidx_made = sem("sidx_made")
        oh2_made = sem("oh2_made")
        red_made = sem("red_made")
        red_kept = sem("red_kept")
        h2T_made = sem("h2T_made")
        h2T_kept = sem("h2T_kept")
        cntT_kept = sem("cntT_kept")
        gates_made = sem("gates_made")
        rz_made = sem("rz_made")
        nn_pre = sem("nn_pre")
        nn_made = sem("nn_made")
        mix = sem("mix")
        out_made = sem("out_made")

        CREDIT = 2
        GRP = 512 // (3 * C)
        GROUPS = [(a, min(a + GRP, NW)) for a in range(0, NW, GRP)]
        WC = G3 // 128
        block = ctx.enter_context(nc.Block())

        def flat(t3, t, n):
            f = t3.rearrange("p a b -> p (a b)") if len(t3.shape) == 3 else t3
            return f[:, bass.ds(t * n, n)]

        def windows(eng, body):
            with eng.Fori(0, PAIRS) as i:
                body(2 * i, i, 0)
                body(2 * i + 1, i, 1)
            body(NW - 1, PAIRS, 0)

        @block.sync
        def _(sp):
            dv = dst.rearrange("(a b) -> a b", a=1)
            for off, to in ((0, dcur), (1, dnext), (129, dfar)):
                sp.dma_start(to, dst[FRONT + off:FRONT + off + E].rearrange("(p f) -> p f", p=W)).then_inc(l_dst, 16)
            for i in range(5):
                a, b = i * NW // 5, (i + 1) * NW // 5
                sp.dma_start(xs[:, a:b, :], x[a * W:b * W, :].rearrange("(t p) d -> p t d", p=W)).then_inc(l_x[i], 16)
            sp.dma_start(Ds[:, :, :], Dmat.rearrange("(c p) d -> p c d", p=128)).then_inc(l_small, 16)
            for c in range(CH):
                for k in range(K):
                    sp.dma_start(UVV[:, c, k * R:(k + 1) * R], U[k, c * 128:(c + 1) * 128, :]).then_inc(l_small, 16)
            hrow = head_w.rearrange("(a k) -> a k", a=1)
            sp.dma_start(hw[:, :], bass.AP(hrow.tensor, 0, [[0, KR], [1, K]])).then_inc(l_small, 16)
            for k in range(K):
                sp.dma_start(hwcol[k * R:(k + 1) * R, :], bass.AP(hrow.tensor, k, [[0, R], [1, 1]])).then_inc(l_small, 16)
            sp.wait_ge(starts_ready, 1)
            with sp.Fori(0, NW) as t:
                first = sp.value_load(starts[0:1, bass.ds(t, 1)], min_val=0, max_val=E)
                for n, a in enumerate((src, dst, kind)):
                    row = a[bass.ds(first + FRONT, SPAN)].rearrange("(j p) -> j p", p=128)
                    sp.dma_start(rows_i[n * C:(n + 1) * C, bass.ds(t * 128, 128)], row).then_inc(l_rows, 16)

            def load_window(t, h):
                first = sp.value_load(starts[0:1, bass.ds(t, 1)], min_val=0, max_val=E)
                bc = bass.AP(dst.tensor, 0, [[0, W], [1, SPAN]])
                one = dst[bass.ds(first + FRONT, SPAN)]
                sp.dma_start(dst_bc[h], bass.AP(dst.tensor, one.offset, [[0, W], [1, SPAN]])).then_inc(l_bc[h], 16)
                for k in range(K):
                    hal = dst[bass.ds(first + FRONT - 129, (C - 1) * 128 + HALO)]
                    sp.dma_start(halo_i[k:k + K * (C - 1) + 1:K, h, :],
                                 bass.AP(dst.tensor, hal.offset, [[128, C], [1, HALO]])).then_inc(l_halo[h], 16)

            sp.wait_ge(a_col, 9)
            load_window(0, 0)
            load_window(1, 1)
            sp.wait_ge(v_zu, 2 * NW)
            sp.dma_start(zu_table.rearrange("(t p) d -> p t d", p=W), zus[:, :, :]).then_inc(st_zu, 16)
            for n, w in enumerate((w_ih, w_hh)):
                m = G3 // 128
                sp.dma_start(wrow[:, n * m:(n + 1) * m, :], w.rearrange("(c p) d -> p c d", p=128)).then_inc(l_gru, 16)
                sp.dma_start(brow[:, n, :], (b_ih, b_hh)[n].rearrange("(a d) -> a d", a=1)).then_inc(l_gru, 16)
            sp.dma_start(rels[:, :], rel).then_inc(l_gru, 16)

            def store_h2(t, h):
                sp.wait_ge(h2_made, t + 1)
                sp.dma_start(h2_table[bass.ds(t * W, W), :], h2s[:, h, :]).then_inc(st_h2, 16)
                sp.wait_ge(st_h2, 16 * (t + 1))
                sp.sem_inc(h2s_free, 1)

            def prefetch(t, h):
                sp.wait_ge(oht_made, t + 1)
                sp.wait_ge(cut_raw, t + 1)
                load_window(t + 2, h)
                store_h2(t, h)

            with sp.Fori(0, PAIRS - 1) as i:
                prefetch(2 * i, 0)
                prefetch(2 * i + 1, 1)
            prefetch(NW - 3, 0)
            store_h2(NW - 2, 1)
            store_h2(NW - 1, 0)
            sp.wait_ge(v_bias, 3)
            sp.wait_ge(a_relw, 2)
            sp.dma_start(relw[RELS:RELS + 1, :], bfull[:, :]).then_inc(l_bias, 16)

            def load_h2(t, h):
                sp.dma_start(h2s[:, h, :], h2_table[bass.ds(t * W, W), :]).then_inc(l_h2[h], 16)

            load_h2(0, 0)
            load_h2(1, 1)

            def out_window(t, h):
                sp.wait_ge(out_made, t + 1)
                sp.dma_start(out[bass.ds(t * W, W), :], outs[:, h, :]).then_inc(st_out, 16)
                sp.wait_ge(st_out, 16 * (t + 1))
                sp.sem_inc(outs_free, 1)

            def turn(t, h):
                out_window(t, h)
                load_h2(t + 2, h)

            with sp.Fori(0, PAIRS - 1) as i:
                turn(2 * i, 0)
                turn(2 * i + 1, 1)
            turn(NW - 3, 0)
            out_window(NW - 2, 1)
            out_window(NW - 1, 0)
            sp.wait_ge(st_out, 16 * NW)

        @block.gpsimd
        def _(pool):
            nc.gpsimd.memset(ident[:, :], 0.0).then_inc(c_pool, 1)
            nc.gpsimd.iota(iota_w[:, :], pattern=[[1, 128]], base=0, channel_multiplier=0,
                           allow_small_or_imprecise_dtypes=True).then_inc(c_const, 1)
            nc.gpsimd.iota(iota_p[:, :], pattern=[[0, 1]], base=0, channel_multiplier=1,
                           allow_small_or_imprecise_dtypes=True).then_inc(c_const, 1)
            nc.gpsimd.iota(win_first[:, :], pattern=[[W, NW]], base=0, channel_multiplier=0,
                           allow_small_or_imprecise_dtypes=True).then_inc(c_const, 1)
            nc.gpsimd.iota(node_id[:, :], pattern=[[W, NW]], base=0, channel_multiplier=1,
                           allow_small_or_imprecise_dtypes=True).then_inc(c_const, 1)
            nc.gpsimd.memset(ones[:, :], 1.0).then_inc(c_const, 1)
            nc.gpsimd.memset(eps_col[:, :], EPS).then_inc(c_const, 1)
            nc.gpsimd.memset(cnt_rows[:, :], 1.0).then_inc(c_const, 1)
            nc.gpsimd.memset(relw[:, :], 0.0).then_inc(c_const, 1)
            nc.gpsimd.memset(L[:, :, :], -BIG).then_inc(c_const, 1)
            pool.wait_ge(c_pool, 1)
            nc.gpsimd.affine_select(out=ident[:, :], in_=ident[:, :], compare_op=ALU.not_equal, fill=1.0,
                                    base=0, pattern=[[-1, 128]], channel_multiplier=1).then_inc(c_ident, 1)

            def gather(t, i, h, table, to, width, done, layer):
                if layer == 0:
                    pool.wait_ge(V_made, t + 1)
                else:
                    pool.wait_ge(red_made, t + 1)
                pool.nop(nofuse=True)
                nc.gpsimd.tensor_copy(sidx[:, h, :], flat(src_col[:, :, :], t, C)).then_inc(sidx_made, 1)
                pool.wait_ge(sidx_made, layer * NW + t + 1)
                pool.nop(nofuse=True)
                for c, (a, b) in enumerate(CHUNKS):
                    for j in range(a, b):
                        nc.gpsimd.indirect_dma_start(
                            out=to(h, j), out_offset=None, in_=table,
                            in_offset=bass.IndirectOffsetOnAxis(ap=sidx[:, h, j:j + 1], axis=0),
                        ).then_inc(done[h][c], 16)

            pool.wait_ge(st_zu, 16)
            pool.wait_ge(a_col, 9)
            windows(pool, lambda t, i, h: gather(
                t, i, h, zu_table, lambda h, j: zs[h][:, j * KR:(j + 1) * KR], KR, g_zs, 0))
            pool.wait_ge(st_h2, 16 * NW)
            windows(pool, lambda t, i, h: gather(
                t, i, h, h2_table, lambda h, j: hg[h][:, j, :], D, g_h, 1))

        @block.vector
        def _(dve):
            dve.sem_inc(V_made, CREDIT)

            dve.wait_ge(l_dst, 48)
            for t in range(NW):
                if t:
                    dve.wait_ge(v_cnt, t)
                nc.vector.tensor_scalar(junk[:, 0:EF], dcur, float(W * t), 0.0, ALU.is_lt, ALU.add,
                                        accum_out=cnt[:, t:t + 1]).then_inc(v_cnt, 1)
            dve.wait_ge(v_cnt, NW)
            nc.vector.tensor_tensor(junk[:, 0:EF], dcur, dnext, ALU.is_gt).then_inc(v_chk, 1)
            dve.wait_ge(v_chk, 1)
            nc.vector.reduce_sum(cnt[:, NW:NW + 1], junk[:, 0:EF], axis=AXX).then_inc(v_cnt, 1)
            dve.wait_ge(v_cnt, NW + 1)
            nc.vector.tensor_tensor(junk[:, 0:EF], dcur, dfar, ALU.is_equal).then_inc(v_chk, 1)
            dve.wait_ge(v_chk, 2)
            nc.vector.reduce_sum(cnt[:, NW + 1:NW + 2], junk[:, 0:EF], axis=AXX).then_inc(v_cnt, 1)
            dve.wait_ge(p_tot, 1)
            nc.vector.tensor_copy(tot[:, 0:NW + 2], ps(7, 1, 0, NW + 2)).then_inc(v_chk, 1)
            dve.wait_ge(v_chk, 3)
            nc.vector.tensor_copy(starts[:, 0:NW], tot[:, 0:NW]).then_inc(starts_ready, 1)

            dve.wait_ge(l_small, 16 * (2 + CH * K + K))
            nc.vector.reduce_max(hst[:, 0:1], hw[:, :], axis=AXX).then_inc(v_head, 1)
            dve.wait_ge(v_head, 1)
            nc.vector.tensor_scalar(hst[:, 1:2], hst[:, 0:1], -1.0, None, ALU.mult).then_inc(v_head, 1)

            for i in range(5):
                dve.wait_ge(l_x[i], 16)
                for t in range(i * NW // 5, (i + 1) * NW // 5):
                    if t >= 2:
                        dve.wait_ge(v_mv, t - 1)
                    nc.vector.bn_stats(bst[:, t % 2, :], xs[:, t, :]).then_inc(v_bst, 1)
                    dve.wait_ge(v_bst, t + 1)
                    nc.vector.bn_aggr(mv[:, t, :], bst[:, t % 2, :]).then_inc(v_mv, 1)
            dve.wait_ge(a_rstd, 2)
            nc.vector.scalar_tensor_tensor(nmr[:, :], mv[:, :, 0], -1.0, rstd[:, :], ALU.mult, ALU.mult).then_inc(v_nmr, 1)

            dve.wait_ge(p_gd, 1)
            nc.vector.tensor_copy(DD[:, :, :].rearrange("p c d -> p (c d)"), ps(4, 128, 0, CH * D)).then_inc(v_gd, 1)
            dve.wait_ge(l_small, 16 * (2 + CH * K + K))
            for c in range(CH):
                dve.wait_ge(p_gd, 2 + c)
                nc.vector.tensor_tensor(UVV[:, c, KR:KR + D], Ds[:, c, :], ps(5 + c, 128, 0, D), ALU.subtract).then_inc(v_gd, 1)
            dve.wait_ge(v_gd, 3)
            nc.vector.tensor_scalar(UVV[:, :, KR:KR + D], UVV[:, :, KR:KR + D], 0.25, None, ALU.mult).then_inc(v_gd, 1)
            dve.wait_ge(v_gd, 4)
            dve.wait_ge(c_ident, 1)
            for c in range(CH):
                d = UVV[:, c, KR + c * 128:KR + (c + 1) * 128]
                nc.vector.scalar_tensor_tensor(d, ident[:, :], 0.5, d, ALU.mult, ALU.add).then_inc(v_gd, 1)
            dve.wait_ge(a_head, 2)
            nc.vector.reduce_sum(hst[:, 3:4], hw[:, :], axis=AXX).then_inc(v_head, 1)
            dve.wait_ge(v_head, 3)
            nc.vector.reciprocal(hst[:, 4:5], hst[:, 3:4]).then_inc(v_head, 1)
            dve.wait_ge(v_head, 4)
            nc.vector.tensor_tensor(hst[:, 5:6], hst[:, 4:5], hst[:, 2:3], ALU.mult).then_inc(v_head, 1)
            dve.wait_ge(v_head, 5)
            dve.wait_ge(p_gd, 4)
            nc.vector.tensor_scalar(UV[:, :], ps(4, KR, 0, D), hst[:, 5:6], None, ALU.mult).then_inc(v_head, 1)

            def project(t, i, h):
                dve.wait_ge(p_hT, t + 1 + CREDIT)
                nc.vector.tensor_copy(hTs[:, h, :], ps(h, 128, 0, CH * W)).then_inc(v_hT, 1)
                dve.wait_ge(p_zub, t + 1)
                dve.nop(nofuse=True)
                nc.vector.tensor_copy(flat(zus[:, :, :], t, KR), ps(2 + h, W, 0, KR)).then_inc(v_zu, 1)
                nc.vector.tensor_scalar(flat(base[:, :, :], t, D), ps(2 + h, W, KR, KR + D), -THRESH, None, ALU.add).then_inc(v_zu, 1)

            windows(dve, project)

            dve.wait_ge(l_rows, 16 * 3 * NW)
            nc.vector.tensor_copy(rows_f, rows_i).then_inc(v_rowf, 1)

            dve.wait_ge(l_gru, 16 * 5)
            nc.vector.tensor_tensor(bfull[:, 0:2 * D], brow[:, 0, 0:2 * D], brow[:, 1, 0:2 * D], ALU.add).then_inc(v_bias, 1)
            nc.vector.tensor_copy(bfull[:, 2 * D:3 * D], brow[:, 0, 2 * D:3 * D]).then_inc(v_bias, 1)
            nc.vector.tensor_copy(bfull[:, 3 * D:4 * D], brow[:, 1, 2 * D:3 * D]).then_inc(v_bias, 1)

            def one_hots(t, h, layer):
                in0 = iota_w[:, 0:W].unsqueeze(1).broadcast_to([128, C, W])
                col = flat(dst_col[:, :, :], t, C).unsqueeze(2).broadcast_to([128, C, W])
                o = oh[:, h, :].rearrange("p (j w) -> p j w", j=C)
                nc.vector.scalar_tensor_tensor(o, in0, win_first[:, bass.ds(t, 1)], col, ALU.add,
                                               ALU.is_equal).then_inc((oh_made, oh2_made)[layer], 1)

            def prepare(t, i, h):
                dve.wait_ge(l_bc[h], 16 * (i + 1))
                nc.vector.tensor_scalar(ohT, dst_bc[h], node_id[0:W, bass.ds(t, 1)], None, ALU.is_equal).then_inc(oht_made, 1)
                one_hots(t, h, 0)
                kc = flat(kind_col[:, :, :], t, C).unsqueeze(2).broadcast_to([128, C, RELS])
                io = iota_w[:, 0:RELS].unsqueeze(1).broadcast_to([128, C, RELS])
                if not (isinstance(t, int) and t == 0):
                    dve.wait_ge(cnt_made, t)
                nc.vector.tensor_tensor(ohk[:, :].rearrange("p (j r) -> p j r", j=C), io, kc, ALU.is_equal).then_inc(ohk_made, 1)
                dve.wait_ge(l_halo[h], 16 * K * (i + 1))
                nc.vector.tensor_tensor(cut[:, h, 1:HALO], halo_i[:, h, 1:HALO], halo_i[:, h, 0:HALO - 1],
                                        ALU.not_equal).then_inc(cut_raw, 1)

            def attend(t, i, h, ahead):
                for c, (a, b) in enumerate(CHUNKS):
                    n = (b - a) * KR
                    dve.wait_ge(g_zs[h][c], 16 * (b - a) * (i + 1))
                    dve.wait_ge(zd_made[c], t + 1)
                    nc.vector.tensor_tensor(prod[:, a * KR:b * KR], zs[h][:, a * KR:b * KR], ps(c, 128, 0, n),
                                            ALU.mult).then_inc(prod_made, 1)
                    dve.wait_ge(prod_made, 3 * t + c + 1)
                    nc.vector.tensor_reduce(L[:, 1 + a:1 + b, :],
                                            prod[:, a * KR:b * KR].rearrange("p (j k r) -> p j k r", k=K, r=R),
                                            AXX, ALU.add).then_inc(L_made, 1)
                dve.wait_ge(LT_made, t + 1)
                dve.wait_ge(cut_made, t + 1)
                nc.vector.tensor_tensor_scan(runs[:, 0, :], cutf[:, h, 1:257], ps(3, K * C, 0, 256), -BIG,
                                             ALU.add, ALU.max).then_inc(runs_made, 1)
                nc.vector.tensor_tensor_scan(runs[:, 1, ::-1], cutf[:, h, 130:386][:, ::-1], ps(3, K * C, 128, 384)[:, ::-1],
                                             -BIG, ALU.add, ALU.max).then_inc(runs_made, 1)
                dve.wait_ge(runs_made, 2 * t + 2)
                nc.vector.tensor_tensor(segmax[:, :], runs[:, 0, 128:256], runs[:, 1, 0:128], ALU.max).then_inc(segmax_made, 1)
                dve.wait_ge(mT_made, t + 1)
                nc.vector.tensor_tensor(dif[:, :], L[:, 1:C + 1, :].rearrange("p j k -> p (j k)"),
                                        ps(4, 128, 0, K * C), ALU.subtract).then_inc(dif_made, 1)
                dve.wait_ge(P_made, t + 1)
                nc.vector.tensor_tensor(V[:, :, 0:KR].rearrange("p j (k r) -> p j k r", k=K),
                                        zs[h].rearrange("p (j k r) -> p j k r", k=K, r=R),
                                        V[:, :, KR:KR + K].unsqueeze(3).broadcast_to([128, C, K, R]),
                                        ALU.mult).then_inc(V_made, 1)
                if ahead:
                    prepare(t + 1, i + h, 1 - h)
                dve.wait_ge(agg_made, t + 1)
                nc.vector.tensor_scalar(den[:, 0:K], ps(5, W, KR, KR + K), 1e-16, None, ALU.add).then_inc(den_made, 1)
                dve.wait_ge(den_made, 2 * t + 1)
                nc.vector.reciprocal(den[:, K:2 * K], den[:, 0:K]).then_inc(den_made, 1)
                dve.wait_ge(den_made, 2 * t + 2)
                nc.vector.tensor_tensor(aggn[:, :].rearrange("p (k r) -> p k r", k=K),
                                        ps(5, W, 0, KR).rearrange("p (k r) -> p k r", k=K),
                                        den[:, K:2 * K].unsqueeze(2).broadcast_to([W, K, R]), ALU.mult).then_inc(aggn_made, 1)
                dve.wait_ge(grad_made, t + 1)
                nc.vector.tensor_tensor(tmp[:, :], ps(5, W, 0, D), flat(base[:, :, :], t, D), ALU.add).then_inc(x1_made, 1)
                dve.wait_ge(x1_made, 2 * t + 1)
                xt = flat(xs[:, :, :], t, D)
                nc.vector.scalar_tensor_tensor(xt, tmp[:, :], 0.0, xt, ALU.max, ALU.add).then_inc(x1_made, 1)
                dve.wait_ge(x1_made, 2 * t + 2)
                dve.nop(nofuse=True)
                nc.vector.bn_stats(stat[:, :], xt).then_inc(stat_made, 1)
                dve.wait_ge(stat_made, t + 1)
                dve.nop(nofuse=True)
                nc.vector.bn_aggr(mvw[:, :], stat[:, :]).then_inc(var_made, 1)
                dve.wait_ge(ln_made, 2 * t + 2)
                nc.vector.scalar_tensor_tensor(rsw[:, 2:3], mvw[:, 0:1], -1.0, rsw[:, 1:2], ALU.mult, ALU.mult).then_inc(rsw_made, 1)

            dve.wait_ge(c_const, 9)
            dve.wait_ge(a_col, 9)
            prepare(0, 0, 0)
            with dve.Fori(0, PAIRS) as i:
                attend(2 * i, i, 0, True)
                attend(2 * i + 1, i, 1, True)
            attend(NW - 1, PAIRS, 0, False)

            def gru(t, i, h, ahead):
                if ahead:
                    dve.wait_ge(red_made, t + CREDIT)
                    one_hots(t + 1, 1 - h, 1)
                gate = (5, 3)[h]
                dve.wait_ge(rz_made, t + 1)
                nc.vector.tensor_tensor(nn[:, :], rz[:, h, 0:D], ps(gate, W, D, 2 * D), ALU.mult).then_inc(nn_pre, 1)
                dve.wait_ge(nn_pre, 2 * t + 1)
                nc.vector.tensor_tensor(nn[:, :], nn[:, :], ps(gate, W, 0, D), ALU.add).then_inc(nn_pre, 1)
                dve.wait_ge(nn_made, t + 1)
                nc.vector.tensor_tensor(dd[:, :], h2s[:, h, :], nn[:, :], ALU.subtract).then_inc(mix, 1)
                dve.wait_ge(mix, 3 * t + 1)
                nc.vector.tensor_tensor(dd[:, :], dd[:, :], rz[:, h, D:2 * D], ALU.mult).then_inc(mix, 1)
                dve.wait_ge(mix, 3 * t + 2)
                nc.vector.tensor_tensor(dd[:, :], dd[:, :], nn[:, :], ALU.add).then_inc(mix, 1)
                dve.wait_ge(mix, 3 * t + 3)
                dve.wait_ge(outs_free, t + 1)
                nc.vector.tensor_tensor(outs[:, h, :], dd[:, :], flat(xs[:, :, :], t, D), ALU.add).then_inc(out_made, 1)

            dve.sem_inc(outs_free, CREDIT)
            one_hots(0, 0, 1)
            with dve.Fori(0, PAIRS) as i:
                gru(2 * i, i, 0, True)
                gru(2 * i + 1, i, 1, True)
            gru(NW - 1, PAIRS, 0, False)

        @block.scalar
        def _(act):
            act.wait_ge(v_head, 2)
            nc.scalar.activation(hw[:, :], hw[:, :], ACT.Exp, bias=hst[:, 1:2]).then_inc(a_head, 1)
            nc.scalar.activation(hst[:, 2:3], hwcol[:, :], ACT.Exp, bias=hst[:, 1:2]).then_inc(a_head, 1)
            act.wait_ge(v_mv, NW)
            act.wait_ge(c_const, 9)
            nc.scalar.activation(rstd[:, :], mv[:, :, 1], ACT.Ln, bias=eps_col[0:W, :]).then_inc(a_rstd, 1)
            act.wait_ge(a_rstd, 1)
            nc.scalar.activation(rstd[:, :], rstd[:, :], ACT.Exp, scale=-0.5).then_inc(a_rstd, 1)
            act.wait_ge(a_rstd, 2)
            act.wait_ge(v_nmr, 1)

            def normalise(t, i, h):
                act.wait_ge(p_hT, t + 1)
                act.nop(nofuse=True)
                nc.scalar.activation(hn[:, h, :], flat(xs[:, :, :], t, D), ACT.Relu, bias=nmr[:, bass.ds(t, 1)],
                                     scale=rstd[:, bass.ds(t, 1)]).then_inc(a_hn, 1)

            windows(act, normalise)

            for g, (a, b) in enumerate(GROUPS):
                act.wait_ge(p_col, g + 1)
                for n, to in enumerate((src_col, dst_col, kind_col)):
                    v = ps(6, 128, 0, (b - a) * 3 * C).rearrange("p (t n j) -> p t n j", n=3, j=C)
                    nc.scalar.activation(to[:, a:b, :], v[:, :, n, :], ACT.Copy).then_inc(a_col, 1)

            for g in range(8):
                n, c, half = g // 4, g // 2 % 2, g % 2
                act.wait_ge(p_wT, g + 1)
                to = (wihT, whhT)[n]
                nc.scalar.activation(to[:, c, half * G3 // 2:(half + 1) * G3 // 2], ps(6 + g % 2, 128, 0, G3 // 2),
                                     ACT.Copy).then_inc(a_wT, 1)
            act.wait_ge(p_relT, 1)
            nc.scalar.activation(relT[:, :], ps(5, 128, 0, CH * RELS), ACT.Copy).then_inc(a_relT, 1)
            act.wait_ge(p_relw, 1)
            nc.scalar.activation(relw[0:RELS, 0:2 * D], ps(6, RELS, 0, 2 * D), ACT.Copy).then_inc(a_relw, 1)
            nc.scalar.activation(relw[0:RELS, 2 * D:3 * D], ps(7, RELS, 0, D), ACT.Copy).then_inc(a_relw, 1)

            act.sem_inc(h2s_free, CREDIT)

            def cuts(t, h):
                act.wait_ge(cut_raw, t + 1)
                nc.scalar.activation(cutf[:, h, 1:HALO], cut[:, h, 1:HALO], ACT.Copy, scale=-BIG).then_inc(cut_made, 1)

            def attend(t, i, h, ahead):
                act.wait_ge(cnt_made, t + 1)
                act.nop(nofuse=True)
                nc.scalar.activation(cnt_rows[0:RELS, bass.ds(t * W, W)], ps(7, RELS, 0, W), ACT.Copy).then_inc(cnt_kept, 1)
                act.wait_ge(dif_made, t + 1)
                nc.scalar.activation(V[:, :, KR:KR + K], dif[:, :].rearrange("p (j k) -> p j k", k=K), ACT.Exp,
                                     scale=float(R) ** -0.5).then_inc(P_made, 1)
                if ahead:
                    cuts(t + 1, 1 - h)
                act.wait_ge(aggT_made, t + 1)
                nc.scalar.activation(aggT[:, :], ps(4, KR, 0, W), ACT.Copy).then_inc(aggT_kept, 1)
                act.wait_ge(var_made, t + 1)
                nc.scalar.activation(rsw[:, 0:1], mvw[:, 1:2], ACT.Ln, bias=eps_col[0:W, :]).then_inc(ln_made, 1)
                act.wait_ge(ln_made, 2 * t + 1)
                nc.scalar.activation(rsw[:, 1:2], rsw[:, 0:1], ACT.Exp, scale=-0.5).then_inc(ln_made, 1)
                act.wait_ge(h2s_free, t + 1)
                act.wait_ge(rsw_made, t + 1)
                act.nop(nofuse=True)
                nc.scalar.activation(h2s[:, h, :], flat(xs[:, :, :], t, D), ACT.Relu, bias=rsw[:, 2:3],
                                     scale=rsw[:, 1:2]).then_inc(h2_made, 1)

            cuts(0, 0)
            with act.Fori(0, PAIRS) as i:
                attend(2 * i, i, 0, True)
                attend(2 * i + 1, i, 1, True)
            attend(NW - 1, PAIRS, 0, False)

            def gru(t, i, h):
                act.wait_ge(cnt_kept, NW)
                nc.scalar.activation(cntT[:, h, :], cnt_rows[:, bass.ds(t * W, W)], ACT.Copy).then_inc(cntT_kept, 1)
                act.wait_ge(h2T_made, t + 1)
                nc.scalar.activation(h2T[:, :], ps(6, 128, 0, CH * W), ACT.Copy).then_inc(h2T_kept, 1)
                act.wait_ge(red_made, t + 1 + CREDIT)
                for c in range(CH):
                    nc.scalar.activation(redT[:, c * W:(c + 1) * W], ps(c, 128, 0, W), ACT.Copy).then_inc(red_kept, 1)
                act.wait_ge(gates_made, t + 1)
                nc.scalar.activation(rz[:, h, :], ps((4, 2)[h], W, 0, 2 * D), ACT.Sigmoid).then_inc(rz_made, 1)
                act.wait_ge(nn_pre, 2 * t + 2)
                nc.scalar.activation(nn[:, :], nn[:, :], ACT.Tanh).then_inc(nn_made, 1)

            windows(act, gru)

        @block.tensor
        def _(pe):
            pe.sem_inc(p_hT, CREDIT)
            mm, tr = nc.tensor.matmul, nc.tensor.transpose
            pe.wait_ge(v_cnt, NW + 2)
            pe.wait_ge(c_const, 9)
            mm(ps(7, 1, 0, NW + 2), ones[0:W, :], cnt[:, :], start=True, stop=True).then_inc(p_tot, 1)
            pe.wait_ge(l_small, 16 * (2 + CH * K + K))
            for a in range(CH):
                for c in range(CH):
                    last = mm(ps(4, 128, a * D, (a + 1) * D), Ds[:, c, a * 128:(a + 1) * 128], Ds[:, c, :],
                              start=c == 0, stop=c == CH - 1)
            last.then_inc(p_gd, 1)
            pe.wait_ge(v_gd, 1)
            for a in range(CH):
                for c in range(CH):
                    last = mm(ps(5 + a, 128, 0, D), DD[:, c, a * 128:(a + 1) * 128], Ds[:, c, :],
                              start=c == 0, stop=c == CH - 1)
                last.then_inc(p_gd, 1)
            pe.wait_ge(v_gd, 6)
            for c in range(CH):
                last = mm(ps(4, KR, 0, D), UVV[:, c, 0:KR], UVV[:, c, KR:KR + D], start=c == 0, stop=c == CH - 1)
            last.then_inc(p_gd, 1)

            def project(t, i, h):
                pe.wait_ge(a_hn, t + 1)
                for c in range(CH):
                    last = tr(ps(h, 128, c * W, (c + 1) * W), hn[:, h, c * 128:(c + 1) * 128], ident[0:W, 0:W])
                last.then_inc(p_hT, 1)
                pe.wait_ge(v_hT, t + 1)
                for c in range(CH):
                    last = mm(ps(2 + h, W, 0, KR + D), hTs[:, h, c * W:(c + 1) * W], UVV[:, c, :],
                              start=c == 0, stop=c == CH - 1)
                last.then_inc(p_zub, 1)

            windows(pe, project)

            pe.wait_ge(v_rowf, 1)
            for g, (a, b) in enumerate(GROUPS):
                if g:
                    pe.wait_ge(a_col, 3 * g)
                for t in range(a, b):
                    last = tr(ps(6, 128, (t - a) * 3 * C, (t - a + 1) * 3 * C), rows_f[:, t * 128:(t + 1) * 128],
                              ident[0:3 * C, 0:3 * C])
                last.then_inc(p_col, 1)

            pe.wait_ge(l_gru, 16 * 5)
            pe.wait_ge(a_col, 9)
            for g in range(8):
                n, c, half = g // 4, g // 2 % 2, g % 2
                if g >= 2:
                    pe.wait_ge(a_wT, g - 1)
                for m in range(WC // 2):
                    last = tr(ps(6 + g % 2, 128, m * 128, (m + 1) * 128),
                              wrow[:, n * WC + half * WC // 2 + m, c * 128:(c + 1) * 128], ident[:, :])
                last.then_inc(p_wT, 1)
            for c in range(CH):
                last = tr(ps(5, 128, c * RELS, (c + 1) * RELS), rels[:, c * 128:(c + 1) * 128], ident[0:RELS, 0:RELS])
            last.then_inc(p_relT, 1)
            pe.wait_ge(a_relT, 1)
            pe.wait_ge(a_wT, 8)
            for b, lo, hi in ((6, 0, 2 * D), (7, 2 * D, 3 * D)):
                for c in range(CH):
                    last = mm(ps(b, RELS, 0, hi - lo), relT[:, c * RELS:(c + 1) * RELS], wihT[:, c, lo:hi],
                              start=c == 0, stop=c == CH - 1)
            last.then_inc(p_relw, 1)
            pe.wait_ge(a_relw, 2)

            def attend(t, i, h):
                pe.wait_ge(oht_made, t + 1)
                for c, (a, b) in enumerate(CHUNKS):
                    for j in range(a, b):
                        last = mm(ps(c, 128, (j - a) * KR, (j - a + 1) * KR), ohT[:, j * 128:(j + 1) * 128],
                                  flat(zus[:, :, :], t, KR), start=True, stop=True)
                    last.then_inc(zd_made[c], 1)
                pe.wait_ge(oh_made, t + 1)
                pe.wait_ge(ohk_made, t + 1)
                for j in range(C):
                    last = mm(ps(7, RELS, 0, W), ohk[:, j * RELS:(j + 1) * RELS], oh[:, h, j * W:(j + 1) * W],
                              start=j == 0, stop=j == C - 1)
                last.then_inc(cnt_made, 1)
                pe.wait_ge(L_made, 3 * t + 3)
                for s in range(3):
                    last = tr(ps(3, K * C, s * 128, (s + 1) * 128), L[:, s:s + C, :].rearrange("p j k -> p (j k)"), ident[:, :])
                last.then_inc(LT_made, 1)
                pe.wait_ge(segmax_made, t + 1)
                tr(ps(4, 128, 0, K * C), segmax[:, :], ident[0:K * C, 0:K * C]).then_inc(mT_made, 1)
                pe.wait_ge(V_made, t + 1 + CREDIT)
                for j in range(C):
                    last = mm(ps(5, W, 0, KR + K), oh[:, h, j * W:(j + 1) * W], V[:, j, :], start=j == 0, stop=j == C - 1)
                last.then_inc(agg_made, 1)
                pe.wait_ge(aggn_made, t + 1)
                pe.nop(nofuse=True)
                tr(ps(4, KR, 0, W), aggn[:, :], ident[0:W, 0:W]).then_inc(aggT_made, 1)
                pe.wait_ge(aggT_kept, t + 1)
                mm(ps(5, W, 0, D), aggT[:, :], UV[:, :], start=True, stop=True).then_inc(grad_made, 1)

            windows(pe, attend)

            pe.sem_inc(red_made, CREDIT)
            pe.wait_ge(l_bias, 16)

            def gru(t, i, h):
                pe.wait_ge(l_h2[h], 16 * (i + 1))
                for c in range(CH):
                    last = tr(ps(6, 128, c * W, (c + 1) * W), h2s[:, h, c * 128:(c + 1) * 128], ident[0:W, 0:W])
                last.then_inc(h2T_made, 1)
                pe.wait_ge(oh2_made, t + 1)
                for q, (a, b) in enumerate(CHUNKS):
                    pe.wait_ge(g_h[h][q], 16 * (b - a) * (i + 1))
                    for j in range(a, b):
                        for c in range(CH):
                            last = mm(ps(c, 128, 0, W), hg[h][:, j, c * 128:(c + 1) * 128], oh[:, h, j * W:(j + 1) * W],
                                      start=j == 0, stop=j == C - 1)
                last.then_inc(red_made, 1)
                rzb, nb = ((4, 5), (2, 3))[h]
                pe.wait_ge(cntT_kept, t + 1)
                mm(ps(rzb, W, 0, 2 * D), cntT[:, h, :], relw[:, 0:2 * D], start=True, stop=False)
                mm(ps(nb, W, 0, 2 * D), cntT[:, h, :], relw[:, 2 * D:4 * D], start=True, stop=False)
                pe.wait_ge(h2T_kept, t + 1)
                for c in range(CH):
                    mm(ps(rzb, W, 0, 2 * D), h2T[:, c * W:(c + 1) * W], whhT[:, c, 0:2 * D], start=False, stop=False)
                    mm(ps(nb, W, D, 2 * D), h2T[:, c * W:(c + 1) * W], whhT[:, c, 2 * D:3 * D], start=False, stop=False)
                pe.wait_ge(red_kept, 2 * t + 2)
                for c in range(CH):
                    mm(ps(rzb, W, 0, 2 * D), redT[:, c * W:(c + 1) * W], wihT[:, c, 0:2 * D], start=False, stop=c == CH - 1)
                    last = mm(ps(nb, W, 0, D), redT[:, c * W:(c + 1) * W], wihT[:, c, 2 * D:3 * D], start=False, stop=c == CH - 1)
                last.then_inc(gates_made, 1)

            windows(pe, gru)


def kernel(**inputs):
    import numpy as _np
    import concourse.bacc as _bacc
    from concourse import mybir as _mybir
    from concourse.bass_utils import run_bass_kernel_spmd as _run

    names = ["x", "src", "dst", "edge_type_16", "L0_gnn_U", "L0_gnn_Dmat", "L0_gnn_head_w", "L1_gnn_relvectors",
             "L1_gnn_w_ih", "L1_gnn_w_hh", "L1_gnn_b_ih", "L1_gnn_b_hh"]
    nc = _bacc.Bacc("TRN2", target_bir_lowering=False, num_devices=1)
    behind = TILES * 128 + 256
    pads = {"src": (0, 0), "dst": (-1, PAD_NODE), "edge_type_16": (0, 0)}
    arrays, args = {}, []
    for name in names:
        a = _np.ascontiguousarray(inputs[name])
        if name in pads:
            before, after = pads[name]
            a = _np.concatenate([_np.full(FRONT, before, a.dtype), a, _np.full(behind, after, a.dtype)])
        arrays[f"in_{name}"] = a
        args.append(nc.dram_tensor(f"in_{name}", a.shape, _mybir.dt.from_np(a.dtype), kind="ExternalInput").ap())
    shape = inputs["x"].shape
    args.append(nc.dram_tensor("out_dram", shape, _mybir.dt.float32, kind="ExternalOutput").ap())
    gnn_kernel(nc, *args)
    return _run(nc, [arrays], core_ids=[0]).results[0]["out_dram"]
```

```python
import concourse.bass as bass
from concourse import mybir
from contextlib import ExitStack

FRONT = 192
PAD_NODE = 1 << 20
WINDOW = 125
TILES = 18
BIG = 1.0e30
HALO_EDGES = 128


def gnn_kernel(nc, x, edges, U, Dmat, head_w, rel, w_ih, w_hh, b_ih, b_hh, out):
    fp32, int32, bf16 = mybir.dt.float32, mybir.dt.int32, mybir.dt.bfloat16
    ALU, ACT = mybir.AluOpType, mybir.ActivationFunctionType
    AXX = mybir.AxisListType.X

    N, D = x.shape
    K, _, R = U.shape
    KR = K * R
    RELS = rel.shape[0]
    G3 = w_ih.shape[0]
    W, C = WINDOW, TILES
    NW = N // W
    SPAN = C * 128
    EP = edges.shape[1]
    E = EP - FRONT - SPAN - 256
    EF = E // W
    CH = D // 128
    HALO = 3 * HALO_EDGES + 2
    BLOCKS = -(-E // SPAN)
    CHUNKS = [(0, 8), (8, 16), (16, 18)]
    PAIRS = NW // 2
    EPS, THRESH = 1e-5, 0.5 * 0.1
    assert N == NW * W and NW % 2 == 1 and BLOCKS <= NW and E == EF * W and C == CHUNKS[-1][1]

    ctx = ExitStack()
    with ctx:
        def sb(name, shape, dt=fp32):
            return ctx.enter_context(nc.sbuf_tensor(name, shape, dt))

        def sem(name):
            return ctx.enter_context(nc.semaphore(name))

        zu_table = nc.dram_tensor("zu_table", [N, KR], fp32, kind="Internal").ap()
        h2_table = nc.dram_tensor("h2_table", [N, D], fp32, kind="Internal").ap()
        logit_table = nc.dram_tensor("logit_table", [K, BLOCKS * SPAN], fp32, kind="Internal").ap()
        most_table = nc.dram_tensor("most_table", [N, K], fp32, kind="Internal").ap()

        xs = sb("xs", [W, NW, D])
        zus = sb("zus", [W, NW, KR])
        base_all = sb("base", [128, NW * D])
        base = base_all[0:W, :].rearrange("p (t d) -> p t d", t=NW)
        cnt_rows = sb("cnt_rows", [RELS + 1, N])
        src_col = sb("src_col", [128, NW, C], int32)
        dst_col = sb("dst_col", [128, NW, C])
        kind_col = sb("kind_col", [128, NW, C])
        ident = sb("ident", [128, 128])
        iota_w = sb("iota_w", [128, 128])
        iota_p = sb("iota_p", [128, 1])
        win_first = sb("win_first", [128, NW])
        node_id = sb("node_id", [128, NW])
        ones = sb("ones", [128, 1])
        eps_col = sb("eps_col", [128, 1])
        minus_thresh = sb("minus_thresh", [128, 1])
        starts = sb("starts", [1, NW + 2], int32)
        wihT = sb("wihT", [128, CH, G3])
        whhT = sb("whhT", [128, CH, G3])
        relw = sb("relw", [RELS + 1, 4 * D])
        UV = sb("UV", [KR, D])

        shared = sb("shared", [128, 2 * C * D])
        SH = shared[:, :]

        def part(p, at, n, dt=fp32):
            v = SH[0:p, at:at + n]
            return v if dt == fp32 else v.bitcast(dt)

        rows_i = part(3 * C, 0, NW * 128, int32)
        rows_f = part(3 * C, NW * 128, NW * 128)
        at = 2 * NW * 128
        dcur = part(W, at, EF, int32)
        dnext = part(W, at + 512, EF, int32)
        dfar = part(W, at + 1024, EF, int32)
        dst_bc = [part(W, h * SPAN, SPAN, int32) for h in range(2)]
        ohT = part(W, 2 * SPAN, SPAN // 2).bitcast(bf16)
        zs = [part(128, 3 * SPAN + h * C * KR, C * KR) for h in range(2)]
        assert 3 * SPAN + 2 * C * KR <= 2 * C * D
        any_dst_row, any_row, any_mask, any_masked = (part(W, n * SPAN, SPAN, dt) for n, dt in
                                                      enumerate((int32, fp32, fp32, fp32)))
        any_dst_i = part(128, 0, BLOCKS * C, int32).rearrange("p (q j) -> p q j", j=C)
        any_kind_i = part(128, BLOCKS * C, BLOCKS * C, int32).rearrange("p (q j) -> p q j", j=C)
        any_near = part(128, 2 * BLOCKS * C, BLOCKS * C)
        hg = [part(128, h * C * D, C * D).rearrange("p (j d) -> p j d", j=C) for h in range(2)]

        setup = sb("setup", [128, 3536])

        def carve(region, p, sizes):
            at, views = 0, []
            for q, size in zip(p, sizes):
                n = size if isinstance(size, int) else size[0] * size[1]
                v = region[0:q, at:at + n]
                views.append(v if isinstance(size, int) else v.rearrange("p (a b) -> p a b", a=size[0]))
                at += n
            return views

        Ds, DD, UVV, hn, hTs, junk, junk2 = carve(setup, (128, 128, 128, W, 128, W, W),
                                                  ((CH, D), (CH, D), (CH, KR + D), (2, D), (2, CH * W), EF, EF))
        wrow, = carve(setup, (128,), ((2 * G3 // 128, D),))
        layer = sb("layer", [128, 3152])
        zu3 = sb("zu3", [W, 3, KR], bf16)
        rest = sb("rest", [W, 2, KR])
        prod, V, cut = carve(layer, (128, 128, K * C), (C * KR, (C, KR + K), (2, HALO)))
        cntT, h2T, redT, rz, nn, dd, outs = carve(layer, (RELS + 1, 128, 128, W, W, W, W),
                                                  ((2, W), CH * W, CH * W, (2, 2 * D), D, D, (2, D)))
        cnt = sb("cnt", [W, NW + 1])
        unfit = sb("unfit", [W, 2, EF])
        half_below = sb("half_below", [W, NW])
        tot = sb("tot", [1, NW + 2])
        tdiff = sb("tdiff", [1, NW])
        bad = sb("bad", [1, 3])
        general = sb("general", [1, 1], int32)
        hw = sb("hw", [KR, K])
        hwcol = sb("hwcol", [KR, 1])
        hst = sb("hst", [KR, 8])
        mv = sb("mv", [W, NW, 2])
        bst = sb("bst", [W, 2, 6])
        rstd = sb("rstd", [W, NW])
        nmr = sb("nmr", [W, NW])
        rels = sb("rels", [RELS, D])
        relT = sb("relT", [128, CH * RELS])
        brow = sb("brow", [1, 2, G3])
        bfull = sb("bfull", [1, 4 * D])

        halo_i = sb("halo_i", [K * C, 2, HALO], int32)
        cutf = sb("cutf", [K * C, 2, HALO])
        oh = sb("oh", [128, 2, C * W])
        any_L = oh[:, 1, 0:BLOCKS * K * C]
        any_near_i = oh[:, 1, BLOCKS * K * C:BLOCKS * (K + 1) * C].bitcast(int32)
        any_agg = setup[0:KR + K, 0:N]
        any_red = base_all[:, 0:CH * N]
        any_most = sb("any_most", [W, NW, K])
        any_top = sb("any_top", [W, 1])
        most_e = sb("most_e", [128, C * K])
        ohk = sb("ohk", [128, C * RELS])
        sidx = sb("sidx", [128, 2, C], int32)
        L = sb("L", [128, C + 2, K])
        runs = sb("runs", [K * C, 2, 256])
        segmax = sb("segmax", [K * C, 128])
        dif = sb("dif", [128, C * K])
        den = sb("den", [KR + K, 2, W])
        aggraw = sb("aggraw", [KR, W])
        head_rows = sb("head_rows", [KR + K, KR])
        aggT = sb("aggT", [KR, W])
        stat = sb("stat", [W, 6])
        mvw = sb("mvw", [W, 2])
        rsw = sb("rsw", [W, 3])
        tmp = sb("tmp", [W, D])
        h2s = sb("h2s", [W, 2, D])


        banks = [ctx.enter_context(nc.psum_tensor(f"bank{i}", [128, 512], fp32)) for i in range(8)]

        def ps(i, p, a, b):
            return banks[i][0:p, a:b]

        l_dst = sem("l_dst")
        l_x = [sem(f"l_x{i}") for i in range(5)]
        l_small = sem("l_small")
        l_rows = sem("l_rows")
        l_gru = sem("l_gru")
        l_bc = [sem(f"l_bc{h}") for h in range(2)]
        l_halo = [sem(f"l_halo{h}") for h in range(2)]
        l_h2 = [sem(f"l_h2{h}") for h in range(2)]
        st_zu = sem("st_zu")
        st_h2 = sem("st_h2")
        st_out = sem("st_out")
        h2s_free = sem("h2s_free")
        outs_free = sem("outs_free")
        l_bias = sem("l_bias")
        a_relw = sem("a_relw")
        a_relT = sem("a_relT")
        p_relT = sem("p_relT")
        p_relw = sem("p_relw")
        g_zs = [[sem(f"g_zs{h}{c}") for c in range(3)] for h in range(2)]
        g_h = [[sem(f"g_h{h}{c}") for c in range(3)] for h in range(2)]
        c_pool = sem("c_pool")
        c_ident = sem("c_ident")
        v_half = sem("v_half")
        a_cnt = sem("a_cnt")
        c_const = sem("c_const")
        c_first = sem("c_first")
        v_chk = sem("v_chk")
        l_next = sem("l_next")
        v_unfit = sem("v_unfit")
        flag_ready = sem("flag_ready")
        v_cnt = sem("v_cnt")
        p_tot = sem("p_tot")
        starts_ready = sem("starts_ready")
        v_rowf = sem("v_rowf")
        p_col = sem("p_col")
        a_col = sem("a_col")
        p_gd = sem("p_gd")
        v_gd = sem("v_gd")
        v_head = sem("v_head")
        a_head = sem("a_head")
        v_bst = sem("v_bst")
        v_mv = sem("v_mv")
        a_rstd = sem("a_rstd")
        v_nmr = sem("v_nmr")
        a_hn = sem("a_hn")
        p_hT = sem("p_hT")
        v_hT = sem("v_hT")
        p_zub = sem("p_zub")
        v_zu = sem("v_zu")
        a_base = sem("a_base")
        p_wT = sem("p_wT")
        a_wT = sem("a_wT")
        v_bias = sem("v_bias")
        oht_made = sem("oht_made")
        oh_made = sem("oh_made")
        zu3_made = sem("zu3_made")
        rec_made = sem("rec_made")
        wide_made = sem("wide_made")
        agg_kept = sem("agg_kept")
        ohk_made = sem("ohk_made")
        cut_raw = sem("cut_raw")
        cut_made = sem("cut_made")
        zd_made = [sem(f"zd_made{c}") for c in range(3)]
        cnt_made = sem("cnt_made")
        cnt_kept = sem("cnt_kept")
        prod_made = sem("prod_made")
        L_made = sem("L_made")
        LT_made = sem("LT_made")
        runs_made = sem("runs_made")
        segmax_made = sem("segmax_made")
        mT_made = sem("mT_made")
        dif_made = sem("dif_made")
        P_made = sem("P_made")
        V_made = sem("V_made")
        agg_made = sem("agg_made")
        den_made = sem("den_made")
        aggT_made = sem("aggT_made")
        grad_made = sem("grad_made")
        x1_made = sem("x1_made")
        stat_made = sem("stat_made")
        var_made = sem("var_made")
        ln_made = sem("ln_made")
        rsw_made = sem("rsw_made")
        h2_made = sem("h2_made")
        sidx_made = sem("sidx_made")
        oh2_made = sem("oh2_made")
        red_made = sem("red_made")
        red_kept = sem("red_kept")
        h2T_made = sem("h2T_made")
        h2T_kept = sem("h2T_kept")
        cntT_kept = sem("cntT_kept")
        gates_made = sem("gates_made")
        rz_made = sem("rz_made")
        nn_pre = sem("nn_pre")
        nn_made = sem("nn_made")
        mix = sem("mix")
        out_made = sem("out_made")

        any_in = sem("any_in")
        any_cast = sem("any_cast")
        any_zero = sem("any_zero")
        any_idx = sem("any_idx")
        any_g = sem("any_g")
        any_prod = sem("any_prod")
        any_L_made = sem("any_L_made")
        any_L_out = sem("any_L_out")
        l_any_dst = sem("l_any_dst")
        l_any_row = sem("l_any_row")
        any_masks = sem("any_masks")
        any_tops = sem("any_tops")
        any_most_made = sem("any_most_made")
        any_row_used = sem("any_row_used")
        any_most_out = sem("any_most_out")
        any_dif = sem("any_dif")
        any_P = sem("any_P")
        any_V = sem("any_V")
        any_ohk = sem("any_ohk")
        any_oh = sem("any_oh")
        any_agg_made = sem("any_agg_made")
        any_agg_kept = sem("any_agg_kept")
        any_red_made = sem("any_red_made")
        any_red_kept = sem("any_red_kept")

        COUNTS = (4, 12, C)
        CREDIT = 2
        FREE = 1
        SPLIT = 11
        GRP = 512 // (3 * C)
        GROUPS = [(a, min(a + GRP, NW)) for a in range(0, NW, GRP)]
        WC = G3 // 128
        block = ctx.enter_context(nc.Block())

        def flat(t3, t, n):
            f = t3.rearrange("p a b -> p (a b)") if len(t3.shape) == 3 else t3
            return f[:, bass.ds(t * n, n)]

        def windows(eng, body):
            with eng.Fori(0, PAIRS) as i:
                body(2 * i, i, 0)
                body(2 * i + 1, i, 1)
            body(NW - 1, PAIRS, 0)

        def overlapped(eng, step):
            step(0, 0, 0, True, False)
            with eng.Fori(0, PAIRS - 1) as i:
                step(2 * i + 1, i, 1, False, False)
                step(2 * i + 2, i + 1, 0, False, False)
            step(NW - 2, PAIRS - 1, 1, False, False)
            step(NW - 1, PAIRS, 0, False, True)

        def way(eng, windowed, by_blocks):
            eng.wait_ge(flag_ready, 1)
            eng.nop(nofuse=True)
            unsuited = eng.value_load(general[0:1, 0:1], min_val=0, max_val=1)
            with eng.If(unsuited < 1):
                windowed()
            with eng.Else():
                by_blocks()

        @block.sync
        def _(sp):
            for off, to, loaded in ((0, dcur, l_dst), (1, dnext, l_next), (HALO_EDGES + 1, dfar, l_next)):
                sp.dma_start(to, edges[1, FRONT + off:FRONT + off + E].rearrange("(p f) -> p f", p=W)).then_inc(loaded, 16)
            for i in range(5):
                a, b = i * NW // 5, (i + 1) * NW // 5
                sp.dma_start(xs[:, a:b, :], x[a * W:b * W, :].rearrange("(t p) d -> p t d", p=W)).then_inc(l_x[i], 16)
            sp.wait_ge(starts_ready, 1)
            with sp.Fori(0, NW) as t:
                first = sp.value_load(starts[0:1, bass.ds(t, 1)], min_val=0, max_val=E)
                rows = edges[0, bass.ds(first + FRONT, SPAN)]
                sp.dma_start(rows_i[:, bass.ds(t * 128, 128)],
                             bass.AP(edges.tensor, rows.offset, [[EP, 3], [128, C], [1, 128]])).then_inc(l_rows, 16)

            def load_window(t, h):
                first = sp.value_load(starts[0:1, bass.ds(t, 1)], min_val=0, max_val=E)
                one = edges[1, bass.ds(first + FRONT, SPAN)]
                sp.dma_start(dst_bc[h], bass.AP(edges.tensor, one.offset, [[0, W], [1, SPAN]])).then_inc(l_bc[h], 16)
                hal = edges[1, bass.ds(first + FRONT - 129, (C - 1) * 128 + HALO)]
                sp.dma_start(halo_i[:, h, :], bass.AP(edges.tensor, hal.offset,
                                                      [[128, C], [0, K], [1, HALO]])).then_inc(l_halo[h], 16)

            for i in range(5):
                a, b = i * NW // 5, (i + 1) * NW // 5
                sp.wait_ge(v_zu, b)
                sp.dma_start(zu_table[a * W:b * W, :].rearrange("(t p) d -> p t d", p=W), zus[:, a:b, :]).then_inc(st_zu, 16)
            sp.wait_ge(a_base, NW + CREDIT)
            for n, w in enumerate((w_ih, w_hh)):
                sp.dma_start(wrow[:, n * WC:(n + 1) * WC, :], w.rearrange("(c p) d -> p c d", p=128)).then_inc(l_gru, 16)
                sp.dma_start(brow[:, n, :], (b_ih, b_hh)[n].rearrange("(a d) -> a d", a=1)).then_inc(l_gru, 16)
            sp.dma_start(rels[:, :], rel).then_inc(l_gru, 16)

            def store_h2(t, h):
                sp.wait_ge(h2_made, t + 1)
                sp.dma_start(h2_table[bass.ds(t * W, W), :], h2s[:, h, :]).then_inc(st_h2, 16)
                sp.wait_ge(st_h2, 16 * (t + 1))
                sp.sem_inc(h2s_free, 1)

            def prefetch(t, h):
                sp.wait_ge(oht_made, t + 1)
                sp.wait_ge(cut_raw, t + 1)
                load_window(t + 2, h)
                store_h2(t, h)

            def load_h2(t, h):
                sp.dma_start(h2s[:, h, :], h2_table[bass.ds(t * W, W), :]).then_inc(l_h2[h], 16)

            def out_window(t, h):
                sp.wait_ge(out_made, t + 1)
                sp.dma_start(out[bass.ds(t * W, W), :], outs[:, h, :]).then_inc(st_out, 16)
                sp.wait_ge(st_out, 16 * (t + 1))
                sp.sem_inc(outs_free, 1)

            def turn(t, h):
                out_window(t, h)
                load_h2(t + 2, h)

            def second_layer():
                sp.wait_ge(v_bias, 3)
                sp.wait_ge(a_relw, 2)
                sp.dma_start(relw[RELS:RELS + 1, :], bfull[:, :]).then_inc(l_bias, 16)
                load_h2(0, 0)
                load_h2(1, 1)
                with sp.Fori(0, PAIRS - 1) as i:
                    turn(2 * i, 0)
                    turn(2 * i + 1, 1)
                turn(NW - 3, 0)
                out_window(NW - 2, 1)
                out_window(NW - 1, 0)
                sp.wait_ge(st_out, 16 * NW)

            def windowed():
                load_window(0, 0)
                load_window(1, 1)
                with sp.Fori(0, PAIRS - 1) as i:
                    prefetch(2 * i, 0)
                    prefetch(2 * i + 1, 1)
                prefetch(NW - 3, 0)
                store_h2(NW - 2, 1)
                store_h2(NW - 1, 0)
                second_layer()

            def by_blocks():
                for n, to in enumerate((src_col[:, 0:BLOCKS, :], any_dst_i, any_kind_i)):
                    sp.dma_start(to, edges[n, FRONT:FRONT + BLOCKS * SPAN].rearrange(
                        "(q p j) -> p q j", p=128, j=C)).then_inc(any_in, 16)
                with sp.Fori(0, BLOCKS) as q:
                    sp.wait_ge(any_L_made, q + 1 + FREE)
                    sp.dma_start(logit_table[:, bass.ds(q * SPAN, SPAN)].rearrange("k (p j) -> p k j", j=C),
                                 any_L[:, bass.ds(q * K * C, K * C)].rearrange("p (k j) -> p k j", k=K)).then_inc(any_L_out, 16)
                sp.wait_ge(any_L_out, 16 * BLOCKS)
                with sp.Fori(0, BLOCKS) as q:
                    sp.wait_ge(any_row_used, q * K + FREE)
                    one = edges[1, bass.ds(q * SPAN + FRONT, SPAN)]
                    sp.dma_start(any_dst_row, bass.AP(edges.tensor, one.offset, [[0, W], [1, SPAN]])).then_inc(l_any_dst, 16)
                    for k in range(K):
                        if k:
                            sp.wait_ge(any_row_used, q * K + k + FREE)
                        one = logit_table[k, bass.ds(q * SPAN, SPAN)]
                        sp.dma_start(any_row, bass.AP(logit_table.tensor, one.offset, [[0, W], [1, SPAN]])).then_inc(l_any_row, 16)
                sp.wait_ge(any_most_made, BLOCKS * K * NW + FREE)
                sp.dma_start(most_table.rearrange("(t p) k -> p t k", p=W), any_most[:, :, :]).then_inc(any_most_out, 16)
                with sp.Fori(0, PAIRS) as i:
                    store_h2(2 * i, 0)
                    store_h2(2 * i + 1, 1)
                store_h2(NW - 1, 0)
                second_layer()

            sp.wait_ge(a_col, 9)
            way(sp, windowed, by_blocks)

        @block.gpsimd
        def _(pool):
            nc.gpsimd.iota(win_first[:, :], pattern=[[W, NW]], base=0, channel_multiplier=0,
                           allow_small_or_imprecise_dtypes=True).then_inc(c_first, 1)
            nc.gpsimd.memset(ident[:, :], 0.0).then_inc(c_pool, 1)
            nc.gpsimd.iota(iota_w[:, :], pattern=[[1, 128]], base=0, channel_multiplier=0,
                           allow_small_or_imprecise_dtypes=True).then_inc(c_const, 1)
            nc.gpsimd.iota(iota_p[:, :], pattern=[[0, 1]], base=0, channel_multiplier=1,
                           allow_small_or_imprecise_dtypes=True).then_inc(c_const, 1)
            nc.gpsimd.iota(node_id[:, :], pattern=[[W, NW]], base=0, channel_multiplier=1,
                           allow_small_or_imprecise_dtypes=True).then_inc(c_const, 1)
            nc.gpsimd.memset(ones[:, :], 1.0).then_inc(c_const, 1)
            nc.gpsimd.memset(eps_col[:, :], EPS).then_inc(c_const, 1)
            nc.gpsimd.memset(minus_thresh[:, :], -THRESH).then_inc(c_const, 1)
            nc.gpsimd.memset(cnt_rows[:, :], 1.0).then_inc(c_const, 1)
            nc.gpsimd.memset(head_rows[:, :], 1.0).then_inc(c_pool, 1)
            pool.wait_ge(c_pool, 2)
            nc.gpsimd.affine_select(out=head_rows[:, :], in_=head_rows[:, :], compare_op=ALU.is_ge, fill=0.0,
                                    base=R * KR, pattern=[[1, KR]], channel_multiplier=-R).then_inc(c_pool, 1)
            pool.wait_ge(c_pool, 3)
            nc.gpsimd.affine_select(out=head_rows[:, :], in_=head_rows[:, :], compare_op=ALU.is_ge, fill=0.0,
                                    base=-R * KR + R - 1, pattern=[[-1, KR]], channel_multiplier=R).then_inc(c_const, 1)
            nc.gpsimd.memset(relw[:, :], 0.0).then_inc(c_const, 1)
            nc.gpsimd.memset(L[:, :, :], -BIG).then_inc(c_const, 1)
            pool.wait_ge(c_pool, 1)
            nc.gpsimd.affine_select(out=ident[:, :], in_=ident[:, :], compare_op=ALU.not_equal, fill=1.0,
                                    base=0, pattern=[[-1, 128]], channel_multiplier=1).then_inc(c_ident, 1)

            def gather(t, i, h, table, to, width, done, layer):
                if layer == 0:
                    pool.wait_ge(V_made, t + 1)
                else:
                    pool.wait_ge(red_made, t + 1)
                pool.nop(nofuse=True)
                nc.gpsimd.tensor_copy(sidx[:, h, :], flat(src_col[:, :, :], t, C)).then_inc(sidx_made, 1)
                pool.wait_ge(sidx_made, layer * NW + t + 1)
                pool.nop(nofuse=True)
                for c, (a, b) in enumerate(CHUNKS):
                    for j in range(a, b):
                        nc.gpsimd.indirect_dma_start(
                            out=to(h, j), out_offset=None, in_=table,
                            in_offset=bass.IndirectOffsetOnAxis(ap=sidx[:, h, j:j + 1], axis=0),
                        ).then_inc(done[h][c], 16)

            def windowed():
                pool.wait_ge(a_col, len(GROUPS))
                windows(pool, lambda t, i, h: gather(
                    t, i, h, zu_table, lambda h, j: zs[h][:, j * KR:(j + 1) * KR], KR, g_zs, 0))
                pool.wait_ge(st_h2, 16 * NW)
                windows(pool, lambda t, i, h: gather(
                    t, i, h, h2_table, lambda h, j: hg[h][:, j, :], D, g_h, 1))

            def block_gather(q, n, index, table, to):
                nc.gpsimd.tensor_copy(sidx[:, n % 2, :], index[:, bass.ds(q * C, C)]).then_inc(any_idx, 1)

                def rows():
                    for j in range(C):
                        nc.gpsimd.indirect_dma_start(
                            out=to(j), out_offset=None, in_=table,
                            in_offset=bass.IndirectOffsetOnAxis(ap=sidx[:, n % 2, j:j + 1], axis=0),
                        ).then_inc(any_g, 16)
                return rows

            def by_blocks():
                sources = src_col[:, :, :].rearrange("p q j -> p (q j)")
                pool.wait_ge(any_in, 48)
                pool.wait_ge(any_cast, 4)
                with pool.Fori(0, BLOCKS) as q:
                    pool.wait_ge(any_L_made, q + FREE)
                    pool.nop(nofuse=True)
                    a = block_gather(q, 0, sources, zu_table, lambda j: zs[0][:, j * KR:(j + 1) * KR])
                    b = block_gather(q, 1, any_near_i, zu_table, lambda j: zs[1][:, j * KR:(j + 1) * KR])
                    pool.wait_ge(any_idx, 2 * q + 2)
                    pool.nop(nofuse=True)
                    a()
                    b()
                pool.wait_ge(any_most_out, 16)
                with pool.Fori(0, BLOCKS) as q:
                    pool.wait_ge(any_agg_made, q * NW + FREE)
                    pool.nop(nofuse=True)
                    a = block_gather(q, 0, sources, zu_table, lambda j: zs[0][:, j * KR:(j + 1) * KR])
                    b = block_gather(q, 1, any_near_i, most_table, lambda j: most_e[:, j * K:(j + 1) * K])
                    pool.wait_ge(any_idx, 2 * BLOCKS + 2 * q + 2)
                    pool.nop(nofuse=True)
                    a()
                    b()
                pool.wait_ge(st_h2, 16 * NW)
                with pool.Fori(0, BLOCKS) as q:
                    pool.wait_ge(any_red_made, q * NW + FREE)
                    pool.nop(nofuse=True)
                    a = block_gather(q, 0, sources, h2_table, lambda j: hg[0][:, j, :])
                    pool.wait_ge(any_idx, 4 * BLOCKS + q + 1)
                    pool.nop(nofuse=True)
                    a()

            pool.wait_ge(st_zu, 16 * 5)
            way(pool, windowed, by_blocks)

        @block.vector
        def _(dve):
            dve.sem_inc(V_made, CREDIT)

            dve.wait_ge(c_first, 1)
            nc.vector.tensor_scalar(half_below[:, :], win_first[0:W, :], -0.5, None, ALU.add).then_inc(v_half, 1)
            dve.wait_ge(l_dst, 16)
            for t in range(SPLIT):
                if t:
                    dve.wait_ge(v_cnt, t)
                nc.vector.tensor_scalar(junk[:, 0:EF], dcur, float(W * t), 0.0, ALU.is_lt, ALU.add,
                                        accum_out=cnt[:, t:t + 1]).then_inc(v_cnt, 1)
            dve.wait_ge(l_next, 32)
            nc.vector.tensor_tensor(unfit[:, 0, :], dcur, dnext, ALU.is_gt).then_inc(v_unfit, 1)
            nc.vector.tensor_tensor(unfit[:, 1, :], dcur, dfar, ALU.is_equal).then_inc(v_unfit, 1)

            dve.wait_ge(p_gd, 1)
            nc.vector.tensor_copy(DD[:, :, :].rearrange("p c d -> p (c d)"), ps(4, 128, 0, CH * D)).then_inc(v_gd, 1)
            dve.wait_ge(l_small, 16 * (3 + CH))
            for c in range(CH):
                dve.wait_ge(p_gd, 2 + c)
                nc.vector.tensor_tensor(UVV[:, c, KR:KR + D], Ds[:, c, :], ps(5 + c, 128, 0, D), ALU.subtract).then_inc(v_gd, 1)
            dve.wait_ge(v_gd, 3)
            nc.vector.tensor_scalar(UVV[:, :, KR:KR + D], UVV[:, :, KR:KR + D], 0.25, None, ALU.mult).then_inc(v_gd, 1)
            dve.wait_ge(v_gd, 4)
            dve.wait_ge(c_ident, 1)
            for c in range(CH):
                d = UVV[:, c, KR + c * 128:KR + (c + 1) * 128]
                nc.vector.scalar_tensor_tensor(d, ident[:, :], 0.5, d, ALU.mult, ALU.add).then_inc(v_gd, 1)
            dve.wait_ge(l_small, 16 * (3 + CH))
            nc.vector.reduce_max(hst[:, 0:1], hw[:, :], axis=AXX).then_inc(v_head, 1)
            dve.wait_ge(v_head, 1)
            nc.vector.tensor_scalar(hst[:, 1:2], hst[:, 0:1], -1.0, None, ALU.mult).then_inc(v_head, 1)

            dve.wait_ge(p_tot, 1)
            nc.vector.tensor_copy(tot[:, 0:NW], ps(7, 1, 0, NW)).then_inc(v_chk, 1)
            nc.vector.tensor_copy(bad[:, 0:1], ps(7, 1, NW, NW + 1)).then_inc(v_chk, 1)
            dve.wait_ge(v_chk, 1)
            nc.vector.tensor_scalar(tot[:, SPLIT:NW], tot[:, SPLIT:NW], float(E), 0.5, ALU.add, ALU.mult).then_inc(v_chk, 1)
            dve.wait_ge(v_chk, 3)
            nc.vector.tensor_copy(starts[:, 0:NW], tot[:, 0:NW]).then_inc(starts_ready, 1)
            nc.vector.memset(tot[:, NW:NW + 1], float(E)).then_inc(v_chk, 1)
            dve.wait_ge(v_chk, 4)
            nc.vector.tensor_tensor(tdiff[:, :], tot[:, 1:NW + 1], tot[:, 0:NW], ALU.subtract).then_inc(v_chk, 1)
            dve.wait_ge(v_chk, 5)
            nc.vector.reduce_max(bad[:, 1:2], tdiff[:, :], axis=AXX).then_inc(v_chk, 1)
            dve.wait_ge(v_chk, 6)
            nc.vector.scalar_tensor_tensor(bad[:, 2:3], bad[:, 1:2], float(SPAN), bad[:, 0:1], ALU.is_gt, ALU.add).then_inc(v_chk, 1)
            dve.wait_ge(v_chk, 7)
            nc.vector.tensor_scalar(general[:, :], bad[:, 2:3], 0.5, None, ALU.is_gt).then_inc(flag_ready, 1)

            for i in range(5):
                dve.wait_ge(l_x[i], 16)
                for t in range(i * NW // 5, (i + 1) * NW // 5):
                    if t >= 2:
                        dve.wait_ge(v_mv, t - 1)
                    nc.vector.bn_stats(bst[:, t % 2, :], xs[:, t, :]).then_inc(v_bst, 1)
                    dve.wait_ge(v_bst, t + 1)
                    nc.vector.bn_aggr(mv[:, t, :], bst[:, t % 2, :]).then_inc(v_mv, 1)
            dve.wait_ge(a_rstd, 2)
            nc.vector.scalar_tensor_tensor(nmr[:, :], mv[:, :, 0], -1.0, rstd[:, :], ALU.mult, ALU.mult).then_inc(v_nmr, 1)

            dve.wait_ge(a_head, 2)
            nc.vector.reduce_sum(hst[:, 3:4], hw[:, :], axis=AXX).then_inc(v_head, 1)
            dve.wait_ge(v_head, 3)
            nc.vector.reciprocal(hst[:, 4:5], hst[:, 3:4]).then_inc(v_head, 1)
            dve.wait_ge(v_head, 4)
            nc.vector.tensor_tensor(hst[:, 5:6], hst[:, 4:5], hst[:, 2:3], ALU.mult).then_inc(v_head, 1)
            dve.wait_ge(v_head, 5)
            dve.wait_ge(p_gd, 4)
            nc.vector.tensor_scalar(UV[:, :], ps(4, KR, 0, D), hst[:, 5:6], None, ALU.mult).then_inc(v_head, 1)

            def turn_h(t, h):
                dve.wait_ge(p_hT, t + 1 + CREDIT)
                nc.vector.tensor_copy(hTs[:, h, :], ps(h, 128, 0, CH * W)).then_inc(v_hT, 1)

            def project(t, h, ahead=True):
                if ahead:
                    turn_h(t + 1, 1 - h)
                dve.wait_ge(p_zub, t + 1)
                dve.nop(nofuse=True)
                nc.vector.tensor_copy(flat(zus[:, :, :], t, KR), ps(2 + h, W, 0, KR)).then_inc(v_zu, 1)

            turn_h(0, 0)
            with dve.Fori(0, PAIRS) as i:
                project(2 * i, 0)
                project(2 * i + 1, 1)
            project(NW - 1, 0, False)

            dve.wait_ge(l_rows, 16 * NW)
            nc.vector.tensor_copy(rows_f, rows_i).then_inc(v_rowf, 1)

            dve.wait_ge(l_gru, 16 * 5)
            nc.vector.tensor_tensor(bfull[:, 0:2 * D], brow[:, 0, 0:2 * D], brow[:, 1, 0:2 * D], ALU.add).then_inc(v_bias, 1)
            nc.vector.tensor_copy(bfull[:, 2 * D:3 * D], brow[:, 0, 2 * D:3 * D]).then_inc(v_bias, 1)
            nc.vector.tensor_copy(bfull[:, 3 * D:4 * D], brow[:, 1, 2 * D:3 * D]).then_inc(v_bias, 1)

            def one_hots(t, h, layer):
                in0 = iota_w[:, 0:W].unsqueeze(1).broadcast_to([128, C, W])
                col = flat(dst_col[:, :, :], t, C).unsqueeze(2).broadcast_to([128, C, W])
                o = oh[:, h, :].rearrange("p (j w) -> p j w", j=C)
                nc.vector.scalar_tensor_tensor(o, in0, win_first[:, bass.ds(t, 1)], col, ALU.add,
                                               ALU.is_equal).then_inc((oh_made, oh2_made)[layer], 1)

            def target_one_hots(t, i, h):
                dve.wait_ge(l_bc[h], 16 * (i + 1))
                nc.vector.tensor_scalar(ohT, dst_bc[h], node_id[0:W, bass.ds(t, 1)], None, ALU.is_equal).then_inc(oht_made, 1)

            def split_rows(t):
                zt = flat(zus[:, :, :], t, KR)
                nc.vector.tensor_copy(zu3[:, 0, :], zt).then_inc(zu3_made, 1)
                dve.wait_ge(zu3_made, 5 * t + 1)
                nc.vector.tensor_tensor(rest[:, 0, :], zt, zu3[:, 0, :], ALU.subtract).then_inc(zu3_made, 1)
                dve.wait_ge(zu3_made, 5 * t + 2)
                nc.vector.tensor_copy(zu3[:, 1, :], rest[:, 0, :]).then_inc(zu3_made, 1)
                dve.wait_ge(zu3_made, 5 * t + 3)
                nc.vector.tensor_tensor(rest[:, 1, :], rest[:, 0, :], zu3[:, 1, :], ALU.subtract).then_inc(zu3_made, 1)
                dve.wait_ge(zu3_made, 5 * t + 4)
                nc.vector.tensor_copy(zu3[:, 2, :], rest[:, 1, :]).then_inc(zu3_made, 1)

            def find_cuts(i, h):
                dve.wait_ge(l_halo[h], 16 * (i + 1))
                nc.vector.tensor_tensor(cut[:, h, 1:HALO], halo_i[:, h, 1:HALO], halo_i[:, h, 0:HALO - 1],
                                        ALU.not_equal).then_inc(cut_raw, 1)

            def relation_one_hots(t, first):
                kc = flat(kind_col[:, :, :], t, C).unsqueeze(2).broadcast_to([128, C, RELS])
                io = iota_w[:, 0:RELS].unsqueeze(1).broadcast_to([128, C, RELS])
                if not first:
                    dve.wait_ge(cnt_made, t)
                nc.vector.tensor_tensor(ohk[:, :].rearrange("p (j r) -> p j r", j=C), io, kc, ALU.is_equal).then_inc(ohk_made, 1)

            def logits(t, i, h, c):
                a, b = CHUNKS[c]
                dve.wait_ge(g_zs[h][c], 16 * (b - a) * (i + 1))
                dve.wait_ge(zd_made[c], t + 1)
                nc.vector.tensor_tensor(prod[:, a * KR:b * KR], zs[h][:, a * KR:b * KR], ps(c, 128, 0, (b - a) * KR),
                                        ALU.mult).then_inc(prod_made, 1)
                dve.wait_ge(prod_made, 3 * t + c + 1)
                nc.vector.tensor_reduce(L[:, 1 + a:1 + b, :],
                                        prod[:, a * KR:b * KR].rearrange("p (j k r) -> p j k r", k=K, r=R),
                                        AXX, ALU.add).then_inc(L_made, 1)

            def attend(t, i, h, first, last):
                logits(t, i, h, 0)
                if not first:
                    renew(t - 1)
                logits(t, i, h, 1)
                if not first:
                    shift(t - 1)
                logits(t, i, h, 2)
                dve.wait_ge(LT_made, t + 1)
                dve.wait_ge(cut_made, t + 1)
                nc.vector.tensor_tensor_scan(runs[:, 0, :], cutf[:, h, 1:2 * HALO_EDGES + 1], ps(3, K * C, 0, 256), -BIG,
                                             ALU.add, ALU.max).then_inc(runs_made, 1)
                nc.vector.tensor_tensor_scan(runs[:, 1, ::-1], cutf[:, h, HALO_EDGES + 2:HALO][:, ::-1],
                                             ps(3, K * C, 128, 384)[:, ::-1],
                                             -BIG, ALU.add, ALU.max).then_inc(runs_made, 1)
                dve.wait_ge(runs_made, 2 * t + 2)
                nc.vector.tensor_tensor(segmax[:, :], runs[:, 0, 128:256], runs[:, 1, 0:128], ALU.max).then_inc(segmax_made, 1)
                ahead = (t + 1, i + h, 1 - h)
                if not last:
                    target_one_hots(*ahead)
                dve.wait_ge(mT_made, t + 1)
                nc.vector.tensor_tensor(dif[:, :], L[:, 1:C + 1, :].rearrange("p j k -> p (j k)"),
                                        ps(4, 128, 0, K * C), ALU.subtract).then_inc(dif_made, 1)
                if not last:
                    split_rows(t + 1)
                dve.wait_ge(P_made, t + 1)
                nc.vector.tensor_tensor(V[:, :, 0:KR].rearrange("p j (k r) -> p j k r", k=K),
                                        zs[h].rearrange("p (j k r) -> p j k r", k=K, r=R),
                                        V[:, :, KR:KR + K].unsqueeze(3).broadcast_to([128, C, K, R]),
                                        ALU.mult).then_inc(V_made, 1)
                if not last:
                    find_cuts(i + h, 1 - h)
                    one_hots(t + 1, 1 - h, 0)
                dve.wait_ge(agg_made, t + 1)
                weigh(t, banks[5][KR:KR + K, 0:W])
                if not last:
                    relation_one_hots(t + 1, False)

            def weigh(t, sums):
                nc.vector.tensor_scalar(den[KR:KR + K, 0, :], sums, 1e-16, None, ALU.add).then_inc(den_made, 1)
                dve.wait_ge(den_made, t + 1)
                nc.vector.reciprocal(den[KR:KR + K, 1, :], den[KR:KR + K, 0, :]).then_inc(rec_made, 1)
                dve.wait_ge(wide_made, t + 1)
                dve.wait_ge(agg_kept, t + 1)
                nc.vector.tensor_tensor(aggT[:, :], aggraw[:, :], ps(4, KR, 0, W), ALU.mult).then_inc(aggT_made, 1)

            def renew(t):
                dve.wait_ge(grad_made, t + 1)
                nc.vector.tensor_tensor(tmp[:, :], ps(5, W, 0, D), base_all[0:W, bass.ds(t * D, D)], ALU.add).then_inc(x1_made, 1)
                dve.wait_ge(x1_made, 2 * t + 1)
                xt = flat(xs[:, :, :], t, D)
                nc.vector.scalar_tensor_tensor(xt, tmp[:, :], 0.0, xt, ALU.max, ALU.add).then_inc(x1_made, 1)
                dve.wait_ge(x1_made, 2 * t + 2)
                dve.nop(nofuse=True)
                nc.vector.bn_stats(stat[:, :], xt).then_inc(stat_made, 1)
                dve.wait_ge(stat_made, t + 1)
                dve.nop(nofuse=True)
                nc.vector.bn_aggr(mvw[:, :], stat[:, :]).then_inc(var_made, 1)

            def shift(t):
                dve.wait_ge(ln_made, 2 * t + 2)
                nc.vector.scalar_tensor_tensor(rsw[:, 2:3], mvw[:, 0:1], -1.0, rsw[:, 1:2], ALU.mult, ALU.mult).then_inc(rsw_made, 1)

            def gru(t, i, h, ahead):
                if ahead:
                    dve.wait_ge(red_made, t + CREDIT)
                    one_hots(t + 1, 1 - h, 1)
                mix_gates(t, h)

            def mix_gates(t, h):
                gate = (5, 3)[h]
                dve.wait_ge(rz_made, t + 1)
                nc.vector.tensor_tensor(nn[:, :], rz[:, h, 0:D], ps(gate, W, D, 2 * D), ALU.mult).then_inc(nn_pre, 1)
                dve.wait_ge(nn_pre, 2 * t + 1)
                nc.vector.tensor_tensor(nn[:, :], nn[:, :], ps(gate, W, 0, D), ALU.add).then_inc(nn_pre, 1)
                dve.wait_ge(nn_made, t + 1)
                nc.vector.tensor_tensor(dd[:, :], h2s[:, h, :], nn[:, :], ALU.subtract).then_inc(mix, 1)
                dve.wait_ge(mix, 3 * t + 1)
                nc.vector.tensor_tensor(dd[:, :], dd[:, :], rz[:, h, D:2 * D], ALU.mult).then_inc(mix, 1)
                dve.wait_ge(mix, 3 * t + 2)
                nc.vector.tensor_tensor(dd[:, :], dd[:, :], nn[:, :], ALU.add).then_inc(mix, 1)
                dve.wait_ge(mix, 3 * t + 3)
                dve.wait_ge(outs_free, t + 1)
                nc.vector.tensor_tensor(outs[:, h, :], dd[:, :], flat(xs[:, :, :], t, D), ALU.add).then_inc(out_made, 1)

            def windowed():
                target_one_hots(0, 0, 0)
                split_rows(0)
                find_cuts(0, 0)
                one_hots(0, 0, 0)
                relation_one_hots(0, True)
                overlapped(dve, attend)
                renew(NW - 1)
                shift(NW - 1)
                one_hots(0, 0, 1)
                with dve.Fori(0, PAIRS) as i:
                    gru(2 * i, i, 0, True)
                    gru(2 * i + 1, i, 1, True)
                gru(NW - 1, PAIRS, 0, False)

            def block_one_hots(q, t):
                in0 = iota_w[:, 0:W].unsqueeze(1).broadcast_to([128, C, W])
                col = flat(dst_col[:, :, :], q, C).unsqueeze(2).broadcast_to([128, C, W])
                nc.vector.scalar_tensor_tensor(oh[:, 0, :].rearrange("p (j w) -> p j w", j=C), in0,
                                               win_first[:, bass.ds(t, 1)], col, ALU.add, ALU.is_equal).then_inc(any_oh, 1)

            def by_blocks():
                for counted in (any_row_used, any_L_made, any_agg_kept, any_red_kept, any_most_made):
                    dve.sem_inc(counted, FREE)
                dve.wait_ge(any_in, 48)
                nc.vector.tensor_copy(dst_col[:, 0:BLOCKS, :], any_dst_i).then_inc(any_cast, 1)
                nc.vector.tensor_copy(kind_col[:, 0:BLOCKS, :], any_kind_i).then_inc(any_cast, 1)
                dve.wait_ge(any_cast, 2)
                nc.vector.tensor_scalar(any_near, dst_col[:, 0:BLOCKS, :].rearrange("p q j -> p (q j)"), float(N - 1),
                                        None, ALU.min).then_inc(any_cast, 1)
                dve.wait_ge(any_cast, 3)
                nc.vector.tensor_copy(any_near_i, any_near).then_inc(any_cast, 1)
                nc.vector.memset(any_most[:, :, :], -BIG).then_inc(any_zero, 1)
                dve.wait_ge(a_wT, 8)
                nc.vector.memset(any_agg, 0.0).then_inc(any_zero, 1)
                nc.vector.memset(cnt_rows[0:RELS, :], 0.0).then_inc(any_zero, 1)

                with dve.Fori(0, BLOCKS) as q:
                    dve.wait_ge(any_g, 16 * 2 * C * (q + 1))
                    nc.vector.tensor_tensor(prod[:, :], zs[0], zs[1], ALU.mult).then_inc(any_prod, 1)
                    dve.wait_ge(any_prod, q + 1)
                    nc.vector.tensor_reduce(any_L[:, bass.ds(q * K * C, K * C)].rearrange("p (k j) -> p j k", k=K),
                                            prod[:, :].rearrange("p (j k r) -> p j k r", k=K, r=R),
                                            AXX, ALU.add).then_inc(any_L_made, 1)

                dve.wait_ge(any_zero, 3)
                with dve.Fori(0, BLOCKS) as q:
                    dve.wait_ge(l_any_dst, 16 * (q + 1))
                    for k in range(K):
                        dve.wait_ge(l_any_row, 16 * (q * K + k + 1))
                        dve.nop(nofuse=True)
                        with dve.Fori(0, NW) as t:
                            n = (q * K + k) * NW + t
                            nc.vector.tensor_scalar(any_mask, any_dst_row, node_id[0:W, bass.ds(t, 1)], BIG,
                                                    ALU.is_equal, ALU.mult).then_inc(any_masks, 1)
                            dve.wait_ge(any_masks, 2 * n + 1)
                            nc.vector.scalar_tensor_tensor(any_masked, any_mask, BIG, any_row, ALU.subtract,
                                                           ALU.add).then_inc(any_masks, 1)
                            dve.wait_ge(any_masks, 2 * n + 2)
                            nc.vector.reduce_max(any_top[:, :], any_masked, axis=AXX).then_inc(any_tops, 1)
                            dve.wait_ge(any_tops, n + 1)
                            dve.wait_ge(any_most_made, n + FREE)
                            dve.nop(nofuse=True)
                            most = any_most[:, :, :].rearrange("p t k -> p (t k)")[:, bass.ds(t * K + k, 1)]
                            nc.vector.tensor_tensor(most, most, any_top[:, :], ALU.max).then_inc(any_most_made, 1)
                        dve.sem_inc(any_row_used, 1)

                with dve.Fori(0, BLOCKS) as q:
                    dve.wait_ge(any_g, 16 * 2 * C * (q + 1 + BLOCKS))
                    dve.nop(nofuse=True)
                    nc.vector.tensor_tensor(dif[:, :].rearrange("p (k j) -> p k j", k=K),
                                            any_L[:, bass.ds(q * K * C, K * C)].rearrange("p (k j) -> p k j", k=K),
                                            most_e[:, :].rearrange("p (j k) -> p k j", k=K), ALU.subtract).then_inc(any_dif, 1)
                    dve.wait_ge(any_dif, 2 * q + 1)
                    nc.vector.tensor_scalar(dif[:, :], dif[:, :], 0.0, None, ALU.min).then_inc(any_dif, 1)
                    dve.wait_ge(any_P, q + 1)
                    nc.vector.tensor_tensor(V[:, :, 0:KR].rearrange("p j (k r) -> p j k r", k=K),
                                            zs[0].rearrange("p (j k r) -> p j k r", k=K, r=R),
                                            V[:, :, KR:KR + K].unsqueeze(3).broadcast_to([128, C, K, R]),
                                            ALU.mult).then_inc(any_V, 1)
                    kc = flat(kind_col[:, :, :], q, C).unsqueeze(2).broadcast_to([128, C, RELS])
                    io = iota_w[:, 0:RELS].unsqueeze(1).broadcast_to([128, C, RELS])
                    nc.vector.tensor_tensor(ohk[:, :].rearrange("p (j r) -> p j r", j=C), io, kc, ALU.is_equal).then_inc(any_ohk, 1)
                    dve.nop(nofuse=True)
                    with dve.Fori(0, NW) as t:
                        n = q * NW + t
                        dve.wait_ge(any_agg_made, n + FREE)
                        dve.nop(nofuse=True)
                        block_one_hots(q, t)
                        dve.wait_ge(any_agg_made, n + 1 + FREE)
                        dve.wait_ge(any_agg_kept, 2 * n + FREE)
                        dve.nop(nofuse=True)
                        a = any_agg[:, bass.ds(t * W, W)]
                        nc.vector.tensor_tensor(a, a, ps(5, KR + K, 0, W), ALU.add).then_inc(any_agg_kept, 1)
                        a = cnt_rows[0:RELS, bass.ds(t * W, W)]
                        nc.vector.tensor_tensor(a, a, ps(7, RELS, 0, W), ALU.add).then_inc(any_agg_kept, 1)
                dve.wait_ge(any_agg_kept, 2 * BLOCKS * NW + FREE)

                def finish(t, i, h):
                    weigh(t, any_agg[KR:KR + K, bass.ds(t * W, W)])
                    renew(t)
                    shift(t)

                windows(dve, finish)

                dve.wait_ge(rsw_made, NW)
                nc.vector.memset(any_red, 0.0).then_inc(any_zero, 1)
                dve.wait_ge(any_zero, 4)
                with dve.Fori(0, BLOCKS) as q:
                    dve.nop(nofuse=True)
                    with dve.Fori(0, NW) as t:
                        n = q * NW + t
                        dve.wait_ge(any_red_made, n + FREE)
                        dve.nop(nofuse=True)
                        block_one_hots(q, t)
                        dve.wait_ge(any_red_made, n + 1 + FREE)
                        dve.wait_ge(any_red_kept, CH * n + FREE)
                        dve.nop(nofuse=True)
                        for c in range(CH):
                            a = any_red[:, bass.ds(t * W + c * N, W)]
                            nc.vector.tensor_tensor(a, a, ps(c, 128, 0, W), ALU.add).then_inc(any_red_kept, 1)
                windows(dve, lambda t, i, h: mix_gates(t, h))

            dve.sem_inc(outs_free, CREDIT)
            dve.wait_ge(c_const, 10)
            dve.wait_ge(a_col, 9)
            way(dve, windowed, by_blocks)

        @block.scalar
        def _(act):
            nc.scalar.preload_act_table_set("natural_log_exp_and_others")
            act.dma_start(Ds[:, :, :], Dmat.rearrange("(c p) d -> p c d", p=128)).then_inc(l_small, 16)
            for c in range(CH):
                act.dma_start(UVV[:, c, 0:KR].rearrange("p (k r) -> p k r", k=K),
                              U[:, c * 128:(c + 1) * 128, :].rearrange("k d r -> d k r")).then_inc(l_small, 16)
            hrow = head_w.rearrange("(a k) -> a k", a=1)
            act.dma_start(hw[:, :], bass.AP(hrow.tensor, 0, [[0, KR], [1, K]])).then_inc(l_small, 16)
            act.dma_start(hwcol[:, :], bass.AP(hrow.tensor, 0, [[1, K], [0, R], [1, 1]])).then_inc(l_small, 16)

            act.wait_ge(l_dst, 16)
            act.wait_ge(v_half, 1)
            for t in range(SPLIT, NW):
                nc.scalar.activation(junk2, dcur, ACT.Sign, bias=half_below[:, t:t + 1], scale=-1.0,
                                     accum_out=cnt[:, t:t + 1]).then_inc(a_cnt, 1)
                act.wait_ge(a_cnt, t - SPLIT + 1)
            act.wait_ge(v_unfit, 2)
            nc.scalar.activation(unfit[:, :, :], unfit[:, :, :], ACT.Relu, accum_out=cnt[:, NW:NW + 1]).then_inc(a_cnt, 1)
            act.wait_ge(v_head, 2)
            nc.scalar.activation(hw[:, :], hw[:, :], ACT.Exp, bias=hst[:, 1:2]).then_inc(a_head, 1)
            nc.scalar.activation(hst[:, 2:3], hwcol[:, :], ACT.Exp, bias=hst[:, 1:2]).then_inc(a_head, 1)
            act.wait_ge(v_mv, NW)
            act.wait_ge(c_const, 10)
            nc.scalar.activation(rstd[:, :], mv[:, :, 1], ACT.Ln, bias=eps_col[0:W, :]).then_inc(a_rstd, 1)
            act.wait_ge(a_rstd, 1)
            nc.scalar.activation(rstd[:, :], rstd[:, :], ACT.Exp, scale=-0.5).then_inc(a_rstd, 1)
            act.wait_ge(a_rstd, 2)
            act.wait_ge(v_nmr, 1)

            def normalise(t, h):
                act.wait_ge(p_hT, t + 1)
                act.nop(nofuse=True)
                nc.scalar.activation(hn[:, h, :], flat(xs[:, :, :], t, D), ACT.Relu, bias=nmr[:, bass.ds(t, 1)],
                                     scale=rstd[:, bass.ds(t, 1)]).then_inc(a_hn, 1)

            def dense_part(t, h, ahead=True):
                if ahead:
                    normalise(t + 2, h)
                act.wait_ge(v_zu, t + 1)
                act.nop(nofuse=True)
                nc.scalar.activation(base_all[0:W, bass.ds(t * D, D)], ps(2 + h, W, KR, KR + D), ACT.Identity,
                                     bias=minus_thresh[0:W, :]).then_inc(a_base, 1)

            normalise(0, 0)
            normalise(1, 1)
            with act.Fori(0, PAIRS - 1) as i:
                dense_part(2 * i, 0)
                dense_part(2 * i + 1, 1)
            dense_part(NW - 3, 0)
            dense_part(NW - 2, 1, False)
            dense_part(NW - 1, 0, False)

            for n, to in enumerate((src_col, dst_col, kind_col)):
                for g, (a, b) in enumerate(GROUPS):
                    act.wait_ge(p_col, g + 1)
                    v = ps(5 + g, 128, 0, (b - a) * 3 * C).rearrange("p (t n j) -> p t n j", n=3, j=C)
                    nc.scalar.activation(to[:, a:b, :], v[:, :, n, :], ACT.Copy).then_inc(a_col, 1)

            for g in range(8):
                n, c, half = g // 4, g // 2 % 2, g % 2
                act.wait_ge(p_wT, g + 1)
                to = (wihT, whhT)[n]
                nc.scalar.activation(to[:, c, half * G3 // 2:(half + 1) * G3 // 2], ps(6 + g % 2, 128, 0, G3 // 2),
                                     ACT.Copy).then_inc(a_wT, 1)
            act.wait_ge(p_relT, 1)
            nc.scalar.activation(relT[:, :], ps(5, 128, 0, CH * RELS), ACT.Copy).then_inc(a_relT, 1)
            act.wait_ge(p_relw, 1)
            nc.scalar.activation(relw[0:RELS, 0:2 * D], ps(6, RELS, 0, 2 * D), ACT.Copy).then_inc(a_relw, 1)
            nc.scalar.activation(relw[0:RELS, 2 * D:3 * D], ps(7, RELS, 0, D), ACT.Copy).then_inc(a_relw, 1)

            act.sem_inc(h2s_free, CREDIT)

            def cuts(t, h):
                act.wait_ge(cut_raw, t + 1)
                nc.scalar.activation(cutf[:, h, 1:HALO], cut[:, h, 1:HALO], ACT.Copy, scale=-BIG).then_inc(cut_made, 1)

            def attend(t, i, h, first, last):
                if not first:
                    normalise_rows(t - 1, 1 - h)
                act.wait_ge(dif_made, t + 1)
                nc.scalar.activation(V[:, :, KR:KR + K], dif[:, :].rearrange("p (j k) -> p j k", k=K), ACT.Exp,
                                     scale=float(R) ** -0.5).then_inc(P_made, 1)
                if not last:
                    cuts(t + 1, 1 - h)
                keep_sums(t, ps(5, KR, 0, W))
                act.wait_ge(cnt_made, t + 1)
                act.nop(nofuse=True)
                nc.scalar.activation(cnt_rows[0:RELS, bass.ds(t * W, W)], ps(7, RELS, 0, W), ACT.Copy).then_inc(cnt_kept, 1)

            def keep_sums(t, sums):
                act.wait_ge(den_made, t + 1)
                act.nop(nofuse=True)
                nc.scalar.activation(aggraw[:, :], sums, ACT.Copy).then_inc(agg_kept, 1)

            def normalise_rows(t, h):
                act.wait_ge(var_made, t + 1)
                nc.scalar.activation(rsw[:, 0:1], mvw[:, 1:2], ACT.Ln, bias=eps_col[0:W, :]).then_inc(ln_made, 1)
                act.wait_ge(ln_made, 2 * t + 1)
                nc.scalar.activation(rsw[:, 1:2], rsw[:, 0:1], ACT.Exp, scale=-0.5).then_inc(ln_made, 1)
                act.wait_ge(h2s_free, t + 1)
                act.wait_ge(rsw_made, t + 1)
                act.nop(nofuse=True)
                nc.scalar.activation(h2s[:, h, :], flat(xs[:, :, :], t, D), ACT.Relu, bias=rsw[:, 2:3],
                                     scale=rsw[:, 1:2]).then_inc(h2_made, 1)

            def gru(t, i, h):
                update(t, h, [ps(c, 128, 0, W) for c in range(CH)])

            def update(t, h, sums):
                nc.scalar.activation(cntT[:, h, :], cnt_rows[:, bass.ds(t * W, W)], ACT.Copy).then_inc(cntT_kept, 1)
                act.wait_ge(h2T_made, t + 1)
                nc.scalar.activation(h2T[:, :], ps(6, 128, 0, CH * W), ACT.Copy).then_inc(h2T_kept, 1)
                act.wait_ge(red_made, t + 1 + CREDIT)
                act.nop(nofuse=True)
                for c in range(CH):
                    nc.scalar.activation(redT[:, c * W:(c + 1) * W], sums[c], ACT.Copy).then_inc(red_kept, 1)
                act.wait_ge(gates_made, t + 1)
                nc.scalar.activation(rz[:, h, :], ps((4, 2)[h], W, 0, 2 * D), ACT.Sigmoid).then_inc(rz_made, 1)
                act.wait_ge(nn_pre, 2 * t + 2)
                nc.scalar.activation(nn[:, :], nn[:, :], ACT.Tanh).then_inc(nn_made, 1)

            def windowed():
                cuts(0, 0)
                act.sem_inc(cnt_kept, 1)
                overlapped(act, attend)
                normalise_rows(NW - 1, 0)
                act.wait_ge(cnt_kept, NW + 1)
                windows(act, gru)

            def by_blocks():
                with act.Fori(0, BLOCKS) as q:
                    act.wait_ge(any_dif, 2 * q + 2)
                    nc.scalar.activation(V[:, :, KR:KR + K].rearrange("p j k -> p k j"),
                                         dif[:, :].rearrange("p (k j) -> p k j", k=K), ACT.Exp,
                                         scale=float(R) ** -0.5).then_inc(any_P, 1)

                def finish(t, i, h):
                    keep_sums(t, any_agg[0:KR, bass.ds(t * W, W)])
                    normalise_rows(t, h)

                windows(act, finish)
                act.wait_ge(any_red_kept, CH * BLOCKS * NW + FREE)
                windows(act, lambda t, i, h: update(t, h, [any_red[:, bass.ds(t * W + c * N, W)] for c in range(CH)]))

            way(act, windowed, by_blocks)

        @block.tensor
        def _(pe):
            pe.sem_inc(p_hT, CREDIT)
            pe.sem_inc(a_base, CREDIT)
            mm, tr = nc.tensor.matmul, nc.tensor.transpose
            pe.wait_ge(l_small, 16 * (3 + CH))
            for a in range(CH):
                for c in range(CH):
                    last = mm(ps(4, 128, a * D, (a + 1) * D), Ds[:, c, a * 128:(a + 1) * 128], Ds[:, c, :],
                              start=c == 0, stop=c == CH - 1)
            last.then_inc(p_gd, 1)
            pe.wait_ge(v_gd, 1)
            for a in range(CH):
                for c in range(CH):
                    last = mm(ps(5 + a, 128, 0, D), DD[:, c, a * 128:(a + 1) * 128], Ds[:, c, :],
                              start=c == 0, stop=c == CH - 1)
                last.then_inc(p_gd, 1)
            pe.wait_ge(v_gd, 6)
            for c in range(CH):
                last = mm(ps(4, KR, 0, D), UVV[:, c, 0:KR], UVV[:, c, KR:KR + D], start=c == 0, stop=c == CH - 1)
            last.then_inc(p_gd, 1)
            pe.wait_ge(v_cnt, SPLIT)
            pe.wait_ge(a_cnt, NW - SPLIT + 1)
            pe.wait_ge(c_const, 10)
            mm(ps(7, 1, 0, NW + 1), ones[0:W, :], cnt[:, :], start=True, stop=True).then_inc(p_tot, 1)

            def turn_h(t, h):
                pe.wait_ge(a_hn, t + 1)
                for c in range(CH):
                    last = tr(ps(h, 128, c * W, (c + 1) * W), hn[:, h, c * 128:(c + 1) * 128], ident[0:W, 0:W])
                last.then_inc(p_hT, 1)

            def project(t, h, ahead=True):
                if ahead:
                    turn_h(t + 1, 1 - h)
                pe.wait_ge(v_hT, t + 1)
                pe.wait_ge(a_base, t + 1)
                for c in range(CH):
                    last = mm(ps(2 + h, W, 0, KR + D), hTs[:, h, c * W:(c + 1) * W], UVV[:, c, :],
                              start=c == 0, stop=c == CH - 1)
                last.then_inc(p_zub, 1)

            turn_h(0, 0)
            with pe.Fori(0, PAIRS) as i:
                project(2 * i, 0)
                project(2 * i + 1, 1)
            project(NW - 1, 0, False)

            pe.wait_ge(v_rowf, 1)
            for g, (a, b) in enumerate(GROUPS):
                for t in range(a, b):
                    last = tr(ps(5 + g, 128, (t - a) * 3 * C, (t - a + 1) * 3 * C), rows_f[:, t * 128:(t + 1) * 128],
                              ident[0:3 * C, 0:3 * C])
                last.then_inc(p_col, 1)

            pe.wait_ge(l_gru, 16 * 5)
            pe.wait_ge(a_col, 9)
            for g in range(8):
                n, c, half = g // 4, g // 2 % 2, g % 2
                if g >= 2:
                    pe.wait_ge(a_wT, g - 1)
                for m in range(WC // 2):
                    last = tr(ps(6 + g % 2, 128, m * 128, (m + 1) * 128),
                              wrow[:, n * WC + half * WC // 2 + m, c * 128:(c + 1) * 128], ident[:, :])
                last.then_inc(p_wT, 1)
            for c in range(CH):
                last = tr(ps(5, 128, c * RELS, (c + 1) * RELS), rels[:, c * 128:(c + 1) * 128], ident[0:RELS, 0:RELS])
            last.then_inc(p_relT, 1)
            pe.wait_ge(a_relT, 1)
            pe.wait_ge(a_wT, 8)
            for b, lo, hi in ((6, 0, 2 * D), (7, 2 * D, 3 * D)):
                for c in range(CH):
                    last = mm(ps(b, RELS, 0, hi - lo), relT[:, c * RELS:(c + 1) * RELS], wihT[:, c, lo:hi],
                              start=c == 0, stop=c == CH - 1)
            last.then_inc(p_relw, 1)
            pe.wait_ge(a_relw, 2)

            def target_rows(t):
                pe.wait_ge(oht_made, t + 1)
                pe.wait_ge(zu3_made, 5 * t + 5)
                for c, (a, b) in enumerate(CHUNKS):
                    for j in range(a, b):
                        for m in range(3):
                            last = mm(ps(c, 128, (j - a) * KR, (j - a + 1) * KR), ohT[:, j * 128:(j + 1) * 128],
                                      zu3[:, m, :], start=m == 0, stop=m == 2)
                    last.then_inc(zd_made[c], 1)

            def relation_counts(h, a, b):
                for j in range(a, b):
                    last = mm(ps(7, RELS, 0, W), ohk[:, j * RELS:(j + 1) * RELS], oh[:, h, j * W:(j + 1) * W],
                              start=j == 0, stop=j == C - 1)
                return last

            def attend(t, h, ahead):
                pe.wait_ge(L_made, 3 * t + 3)
                for s in range(3):
                    last = tr(ps(3, K * C, s * 128, (s + 1) * 128), L[:, s:s + C, :].rearrange("p j k -> p (j k)"), ident[:, :])
                last.then_inc(LT_made, 1)
                pe.wait_ge(oh_made, t + 1)
                pe.wait_ge(ohk_made, t + 1)
                pe.wait_ge(cnt_kept, t + 1)
                relation_counts(h, 0, COUNTS[0])
                pe.wait_ge(segmax_made, t + 1)
                tr(ps(4, 128, 0, K * C), segmax[:, :], ident[0:K * C, 0:K * C]).then_inc(mT_made, 1)
                relation_counts(h, *COUNTS[0:2])
                if ahead:
                    target_rows(t + 1)
                pe.wait_ge(V_made, t + 1 + CREDIT)
                for j in range(C):
                    last = mm(ps(5, KR + K, 0, W), V[:, j, :], oh[:, h, j * W:(j + 1) * W], start=j == 0, stop=j == C - 1)
                last.then_inc(agg_made, 1)
                relation_counts(h, *COUNTS[1:3]).then_inc(cnt_made, 1)
                step_rows(t)

            def step_rows(t):
                pe.wait_ge(rec_made, t + 1)
                mm(ps(4, KR, 0, W), head_rows[KR:KR + K, :], den[KR:KR + K, 1, :], start=True, stop=True).then_inc(wide_made, 1)
                pe.wait_ge(aggT_made, t + 1)
                mm(ps(5, W, 0, D), aggT[:, :], UV[:, :], start=True, stop=True).then_inc(grad_made, 1)

            pe.sem_inc(red_made, CREDIT)

            def gru(t, i, h):
                turn_rows(t, i, h)
                pe.wait_ge(oh2_made, t + 1)
                for q, (a, b) in enumerate(CHUNKS):
                    pe.wait_ge(g_h[h][q], 16 * (b - a) * (i + 1))
                    for j in range(a, b):
                        for c in range(CH):
                            last = mm(ps(c, 128, 0, W), hg[h][:, j, c * 128:(c + 1) * 128], oh[:, h, j * W:(j + 1) * W],
                                      start=j == 0, stop=j == C - 1)
                last.then_inc(red_made, 1)
                gates(t, h)

            def turn_rows(t, i, h):
                pe.wait_ge(l_h2[h], 16 * (i + 1))
                for c in range(CH):
                    last = tr(ps(6, 128, c * W, (c + 1) * W), h2s[:, h, c * 128:(c + 1) * 128], ident[0:W, 0:W])
                last.then_inc(h2T_made, 1)

            def gates(t, h):
                rzb, nb = ((4, 5), (2, 3))[h]
                pe.wait_ge(cntT_kept, t + 1)
                mm(ps(rzb, W, 0, 2 * D), cntT[:, h, :], relw[:, 0:2 * D], start=True, stop=False)
                mm(ps(nb, W, 0, 2 * D), cntT[:, h, :], relw[:, 2 * D:4 * D], start=True, stop=False)
                pe.wait_ge(h2T_kept, t + 1)
                for c in range(CH):
                    mm(ps(rzb, W, 0, 2 * D), h2T[:, c * W:(c + 1) * W], whhT[:, c, 0:2 * D], start=False, stop=False)
                    mm(ps(nb, W, D, 2 * D), h2T[:, c * W:(c + 1) * W], whhT[:, c, 2 * D:3 * D], start=False, stop=False)
                pe.wait_ge(red_kept, 2 * t + 2)
                for c in range(CH):
                    mm(ps(rzb, W, 0, 2 * D), redT[:, c * W:(c + 1) * W], wihT[:, c, 0:2 * D], start=False, stop=c == CH - 1)
                    last = mm(ps(nb, W, 0, D), redT[:, c * W:(c + 1) * W], wihT[:, c, 2 * D:3 * D], start=False, stop=c == CH - 1)
                last.then_inc(gates_made, 1)

            def windowed():
                target_rows(0)
                with pe.Fori(0, PAIRS) as i:
                    attend(2 * i, 0, True)
                    attend(2 * i + 1, 1, True)
                attend(NW - 1, 0, False)
                pe.wait_ge(l_bias, 16)
                windows(pe, gru)

            def block_gru(t, i, h):
                turn_rows(t, i, h)
                pe.sem_inc(red_made, 1)
                gates(t, h)

            def by_blocks():
                for counted in (any_agg_made, any_red_made):
                    pe.sem_inc(counted, FREE)
                with pe.Fori(0, BLOCKS) as q:
                    pe.wait_ge(any_V, q + 1)
                    pe.wait_ge(any_ohk, q + 1)
                    pe.nop(nofuse=True)
                    with pe.Fori(0, NW) as t:
                        n = q * NW + t
                        pe.wait_ge(any_oh, n + 1)
                        pe.wait_ge(any_agg_kept, 2 * n + FREE)
                        for j in range(C):
                            mm(ps(5, KR + K, 0, W), V[:, j, :], oh[:, 0, j * W:(j + 1) * W], start=j == 0, stop=j == C - 1)
                        relation_counts(0, 0, C).then_inc(any_agg_made, 1)
                windows(pe, lambda t, i, h: step_rows(t))
                with pe.Fori(0, BLOCKS) as q:
                    pe.wait_ge(any_g, 16 * C * (4 * BLOCKS + q + 1))
                    pe.nop(nofuse=True)
                    with pe.Fori(0, NW) as t:
                        n = q * NW + t
                        pe.wait_ge(any_oh, BLOCKS * NW + n + 1)
                        pe.wait_ge(any_red_kept, CH * n + FREE)
                        for j in range(C):
                            for c in range(CH):
                                last = mm(ps(c, 128, 0, W), hg[0][:, j, c * 128:(c + 1) * 128], oh[:, 0, j * W:(j + 1) * W],
                                          start=j == 0, stop=j == C - 1)
                        last.then_inc(any_red_made, 1)
                pe.wait_ge(any_red_kept, CH * BLOCKS * NW + FREE)
                pe.wait_ge(l_bias, 16)
                windows(pe, block_gru)

            way(pe, windowed, by_blocks)


def kernel(**inputs):
    import numpy as _np
    import concourse.bacc as _bacc
    from concourse import mybir as _mybir
    from concourse.bass_utils import run_bass_kernel_spmd as _run

    names = ["x", "edges", "L0_gnn_U", "L0_gnn_Dmat", "L0_gnn_head_w", "L1_gnn_relvectors",
             "L1_gnn_w_ih", "L1_gnn_w_hh", "L1_gnn_b_ih", "L1_gnn_b_hh"]
    nc = _bacc.Bacc("TRN2", target_bir_lowering=False, num_devices=1)
    behind = TILES * 128 + 256
    rows = []
    for name, before, after in (("src", 0, 0), ("dst", -1, PAD_NODE), ("edge_type_16", 0, 0)):
        a = _np.asarray(inputs[name])
        rows.append(_np.concatenate([_np.full(FRONT, before, a.dtype), a, _np.full(behind, after, a.dtype)]))
    arrays, args = {}, []
    for name in names:
        a = _np.stack(rows) if name == "edges" else _np.ascontiguousarray(inputs[name])
        arrays[f"in_{name}"] = a
        args.append(nc.dram_tensor(f"in_{name}", a.shape, _mybir.dt.from_np(a.dtype), kind="ExternalInput").ap())
    shape = inputs["x"].shape
    args.append(nc.dram_tensor("out_dram", shape, _mybir.dt.float32, kind="ExternalOutput").ap())
    gnn_kernel(nc, *args)
    return _run(nc, [arrays], core_ids=[0]).results[0]["out_dram"]
```

```python
import concourse.bass as bass
from concourse import mybir
from contextlib import ExitStack

FRONT = 192
PAD_NODE = 1 << 20
WINDOW = 125
TILES = 18
BIG = 1.0e30
HALO_EDGES = 128


def gnn_kernel(nc, x, edges, U, Dmat, head_w, rel, w_ih, w_hh, b_ih, b_hh, out):
    fp32, int32, bf16 = mybir.dt.float32, mybir.dt.int32, mybir.dt.bfloat16
    ALU, ACT = mybir.AluOpType, mybir.ActivationFunctionType
    AXX = mybir.AxisListType.X

    N, D = x.shape
    K, _, R = U.shape
    KR = K * R
    RELS = rel.shape[0]
    G3 = w_ih.shape[0]
    W, C = WINDOW, TILES
    NW = N // W
    SPAN = C * 128
    EP = edges.shape[1]
    E = EP - FRONT - SPAN - 256
    EF = E // W
    CH = D // 128
    HALO = 3 * HALO_EDGES + 2
    BLOCKS = -(-E // SPAN)
    CHUNKS = [(0, 8), (8, 16), (16, 18)]
    CHUNKS2 = [(0, 8), (8, 16), (16, 18)]
    PAIRS = NW // 2
    EPS, THRESH = 1e-5, 0.5 * 0.1
    assert N == NW * W and NW % 4 == 1 and BLOCKS <= NW and E == EF * W and C == CHUNKS[-1][1]

    ctx = ExitStack()
    with ctx:
        def sb(name, shape, dt=fp32):
            return ctx.enter_context(nc.sbuf_tensor(name, shape, dt))

        def sem(name):
            return ctx.enter_context(nc.semaphore(name))

        zu_table = nc.dram_tensor("zu_table", [N, KR], fp32, kind="Internal").ap()
        h2_table = nc.dram_tensor("h2_table", [N, D], fp32, kind="Internal").ap()
        logit_table = nc.dram_tensor("logit_table", [K, BLOCKS * SPAN], fp32, kind="Internal").ap()
        most_table = nc.dram_tensor("most_table", [N, K], fp32, kind="Internal").ap()

        xs = sb("xs", [W, NW, D])
        zus = sb("zus", [W, NW, KR])
        wide = sb("wide", [128, NW * D])
        cnt_rows = sb("cnt_rows", [KR + RELS + 1, N])
        src_col = sb("src_col", [128, NW, C], int32)
        dst_col = sb("dst_col", [128, NW, C])
        kind_col = sb("kind_col", [128, NW, C])
        ident = sb("ident", [128, 128])
        iota_w = sb("iota_w", [128, 128])
        iota_p = sb("iota_p", [128, 1])
        win_first = sb("win_first", [128, NW])
        node_id = sb("node_id", [128, NW])
        ones = sb("ones", [128, 1])
        eps_col = sb("eps_col", [128, 1])
        starts = sb("starts", [1, NW + 2], int32)
        wihT = sb("wihT", [128, CH, G3])
        whhT = sb("whhT", [128, CH, G3])
        relw = sb("relw", [KR + RELS + 1, 4 * D])
        UV = sb("UV", [KR, D])
        VV = sb("VV", [128, CH, D])

        shared = sb("shared", [128, 2 * C * D])
        SH = shared[:, :]

        def part(p, at, n, dt=fp32):
            v = SH[0:p, at:at + n]
            return v if dt == fp32 else v.bitcast(dt)

        rows_i = part(3 * C, 0, NW * 128, int32)
        rows_f = part(3 * C, NW * 128, NW * 128)
        at = 2 * NW * 128
        dcur = part(W, at, EF, int32)
        dnext = part(W, at + 512, EF, int32)
        dfar = part(W, at + 1024, EF, int32)
        dst_bc = [part(W, h * SPAN, SPAN, int32) for h in range(2)]
        ohT = part(W, 2 * SPAN, SPAN // 2).bitcast(bf16)
        zs = [part(128, 3 * SPAN + h * C * KR, C * KR) for h in range(2)]
        assert 3 * SPAN + 2 * C * KR <= 2 * C * D
        any_dst_row, any_row, any_mask, any_masked = (part(W, n * SPAN, SPAN, dt) for n, dt in
                                                      enumerate((int32, fp32, fp32, fp32)))
        any_dst_i = part(128, 0, BLOCKS * C, int32).rearrange("p (q j) -> p q j", j=C)
        any_kind_i = part(128, BLOCKS * C, BLOCKS * C, int32).rearrange("p (q j) -> p q j", j=C)
        any_near = part(128, 2 * BLOCKS * C, BLOCKS * C)
        hg = [part(128, h * C * D, C * D).rearrange("p (j d) -> p j d", j=C) for h in range(2)]

        setup = sb("setup", [128, 3536])

        def carve(region, p, sizes):
            at, views = 0, []
            for q, size in zip(p, sizes):
                n = size if isinstance(size, int) else size[0] * size[1]
                v = region[0:q, at:at + n]
                views.append(v if isinstance(size, int) else v.rearrange("p (a b) -> p a b", a=size[0]))
                at += n
            return views

        Ds, DD, Us, hn, hTs, junk, junk2 = carve(setup, (128, 128, 128, W, 128, W, W),
                                                  ((CH, D), (CH, D), (CH, KR), (2, D), (2, CH * W), EF, EF))
        wrow, = carve(setup, (128,), ((2 * G3 // 128, D),))
        SUMS = KR + K + RELS
        layer = sb("layer", [128, 3440])
        zu3 = sb("zu3", [W, 3, KR], bf16)
        rest = sb("rest", [W, 2, KR])
        prod, V, cut = carve(layer, (128, 128, K * C), (C * KR, (C, SUMS), (2, HALO)))
        cntT, h2T, redT, rz, nn, dd, outs = carve(layer, (KR + RELS + 1, 128, 128, W, W, W, W),
                                                  ((2, W), CH * W, CH * W, (2, 2 * D), D, D, (2, D)))
        cnt = sb("cnt", [W, NW])
        misfits = sb("misfits", [W, 1])
        unfit = sb("unfit", [W, 2, EF])
        half_below = sb("half_below", [W, NW])
        tot = sb("tot", [1, NW + 2])
        tdiff = sb("tdiff", [1, NW])
        bad = sb("bad", [1, 3])
        general = sb("general", [1, 1], int32)
        hw = sb("hw", [KR, K])
        hwcol = sb("hwcol", [KR, 1])
        hst = sb("hst", [KR, 8])
        mv = sb("mv", [W, NW, 2])
        bst = sb("bst", [W, NW, 6])
        rstd = sb("rstd", [W, NW])
        nmr = sb("nmr", [W, NW])
        rels = sb("rels", [RELS, D])
        relT = sb("relT", [128, CH * RELS])

        halo_i = sb("halo_i", [K * C, 2, HALO], int32)
        cutf = sb("cutf", [K * C, 2, HALO])
        oh = sb("oh", [128, 2, C * W])
        any_L = oh[:, 1, 0:BLOCKS * K * C]
        any_near_i = oh[:, 1, BLOCKS * K * C:BLOCKS * (K + 1) * C].bitcast(int32)
        any_agg = setup[0:W, 0:NW * SUMS]
        any_red = wide[:, 0:CH * N]
        hrow = wide[0:W, 0:D]
        hTw = wide[:, D:D + CH * W]
        relw_low = wide[0:RELS, 2 * D:6 * D]
        brow = wide[0:1, 6 * D:6 * D + 2 * G3].rearrange("p (a b) -> p a b", a=2)
        bfull = wide[0:1, 12 * D:16 * D]
        any_most = sb("any_most", [W, NW, K])
        any_top = sb("any_top", [W, 1])
        most_e = sb("most_e", [128, C * K])
        sidx = sb("sidx", [128, 2, C], int32)
        L = sb("L", [128, C + 2, K])
        runs = sb("runs", [K * C, 2, 256])
        segmax = sb("segmax", [K * C, 128])
        dif = sb("dif", [128, C * K])
        den = sb("den", [W, 2, K])
        means = sb("means", [W, KR + RELS])
        meansT = sb("meansT", [KR + RELS, W])
        stat = sb("stat", [W, 6])
        mvw = sb("mvw", [W, 2])
        rsw = sb("rsw", [W, 3])
        tmp = sb("tmp", [W, D])
        h2s = sb("h2s", [W, 2, D])


        banks = [ctx.enter_context(nc.psum_tensor(f"bank{i}", [128, 512], fp32)) for i in range(8)]

        def ps(i, p, a, b):
            return banks[i][0:p, a:b]

        l_dst = sem("l_dst")
        l_x = [sem(f"l_x{i}") for i in range(5)]
        l_small = sem("l_small")
        l_rows = [sem(f"l_rows{g}") for g in range(3)]
        l_gru = sem("l_gru")
        l_bc = [sem(f"l_bc{h}") for h in range(2)]
        l_halo = [sem(f"l_halo{h}") for h in range(2)]
        l_h2 = [sem(f"l_h2{h}") for h in range(2)]
        st_zu = sem("st_zu")
        st_h2 = sem("st_h2")
        st_out = sem("st_out")
        h2s_free = sem("h2s_free")
        outs_free = sem("outs_free")
        l_bias = sem("l_bias")
        a_relw = sem("a_relw")
        a_relT = sem("a_relT")
        p_relT = sem("p_relT")
        p_relw = sem("p_relw")
        g_zs = [[sem(f"g_zs{h}{c}") for c in range(3)] for h in range(2)]
        g_h = [[sem(f"g_h{h}{c}") for c in range(4)] for h in range(2)]
        c_pool = sem("c_pool")
        c_ident = sem("c_ident")
        v_half = sem("v_half")
        a_cnt = sem("a_cnt")
        c_const = sem("c_const")
        c_first = sem("c_first")
        v_chk = sem("v_chk")
        l_next = sem("l_next")
        v_unfit = sem("v_unfit")
        flag_ready = sem("flag_ready")
        v_cnt = sem("v_cnt")
        p_tot = sem("p_tot")
        starts_ready = sem("starts_ready")
        v_rowf = sem("v_rowf")
        p_col = sem("p_col")
        a_col = sem("a_col")
        a_rowf = sem("a_rowf")
        p_gd = sem("p_gd")
        v_gd = sem("v_gd")
        v_head = sem("v_head")
        a_head = sem("a_head")
        v_bst = sem("v_bst")
        v_mv = sem("v_mv")
        a_rstd = sem("a_rstd")
        v_nmr = sem("v_nmr")
        a_hn = sem("a_hn")
        p_hT = sem("p_hT")
        v_hT = sem("v_hT")
        p_zub = sem("p_zub")
        v_zu = sem("v_zu")
        p_flag = sem("p_flag")
        a_misfit = sem("a_misfit")
        l_dense = sem("l_dense")
        hrow_made = sem("hrow_made")
        hrow_turned = sem("hrow_turned")
        hTw_kept = sem("hTw_kept")
        p_wT = sem("p_wT")
        a_wT = sem("a_wT")
        v_bias = sem("v_bias")
        oht_made = sem("oht_made")
        oh_made = sem("oh_made")
        zu3_made = sem("zu3_made")
        ohk_made = sem("ohk_made")
        cut_raw = sem("cut_raw")
        cut_made = sem("cut_made")
        zd_made = [sem(f"zd_made{c}") for c in range(3)]
        means_made = sem("means_made")
        turned_made = sem("turned_made")
        cnt_kept = sem("cnt_kept")
        prod_made = sem("prod_made")
        L_made = sem("L_made")
        LT_made = sem("LT_made")
        runs_made = sem("runs_made")
        segmax_made = sem("segmax_made")
        mT_made = sem("mT_made")
        dif_made = sem("dif_made")
        P_made = sem("P_made")
        V_made = sem("V_made")
        agg_made = sem("agg_made")
        den_made = sem("den_made")
        meansT_made = sem("meansT_made")
        grad_made = sem("grad_made")
        x1_made = sem("x1_made")
        stat_made = sem("stat_made")
        var_made = sem("var_made")
        ln_made = sem("ln_made")
        rsw_made = sem("rsw_made")
        h2_made = sem("h2_made")
        sidx_made = [sem(f"sidx_made{h}") for h in range(2)]
        oh2_made = sem("oh2_made")
        red_made = sem("red_made")
        red_kept = sem("red_kept")
        h2T_made = sem("h2T_made")
        h2T_kept = sem("h2T_kept")
        cntT_kept = sem("cntT_kept")
        gates_made = sem("gates_made")
        rz_made = sem("rz_made")
        nn_pre = sem("nn_pre")
        nn_made = sem("nn_made")
        mix = sem("mix")
        out_made = sem("out_made")

        any_in = sem("any_in")
        any_cast = sem("any_cast")
        any_zero = sem("any_zero")
        any_idx = sem("any_idx")
        any_g = sem("any_g")
        any_prod = sem("any_prod")
        any_L_made = sem("any_L_made")
        any_L_out = sem("any_L_out")
        l_any_dst = sem("l_any_dst")
        l_any_row = sem("l_any_row")
        any_masks = sem("any_masks")
        any_tops = sem("any_tops")
        any_most_made = sem("any_most_made")
        any_row_used = sem("any_row_used")
        any_most_out = sem("any_most_out")
        any_dif = sem("any_dif")
        any_P = sem("any_P")
        any_V = sem("any_V")
        any_ohk = sem("any_ohk")
        any_oh = sem("any_oh")
        any_agg_made = sem("any_agg_made")
        any_agg_kept = sem("any_agg_kept")
        any_red_made = sem("any_red_made")
        any_red_kept = sem("any_red_kept")

        CREDIT = 2
        FREE = 1
        SPLIT = 6
        GRP = 512 // (3 * C)
        GROUPS = [(a, min(a + GRP, NW)) for a in range(0, NW, GRP)]
        WC = G3 // 128
        block = ctx.enter_context(nc.Block())

        def flat(t3, t, n):
            f = t3.rearrange("p a b -> p (a b)") if len(t3.shape) == 3 else t3
            return f[:, bass.ds(t * n, n)]

        def windows(eng, body):
            with eng.Fori(0, PAIRS) as i:
                body(2 * i, i, 0)
                body(2 * i + 1, i, 1)
            body(NW - 1, PAIRS, 0)

        def load_rows(eng, a, b, loaded):
            with eng.Fori(a, b) as t:
                first = eng.value_load(starts[0:1, bass.ds(t, 1)], min_val=0, max_val=E)
                rows = edges[0, bass.ds(first + FRONT, SPAN)]
                eng.dma_start(rows_i[:, bass.ds(t * 128, 128)],
                              bass.AP(edges.tensor, rows.offset, [[EP, 3], [128, C], [1, 128]])).then_inc(loaded, 16)

        def overlapped(eng, step):
            step(0, 0, 0, True, False)
            with eng.Fori(0, PAIRS - 1) as i:
                step(2 * i + 1, i, 1, False, False)
                step(2 * i + 2, i + 1, 0, False, False)
            step(NW - 2, PAIRS - 1, 1, False, False)
            step(NW - 1, PAIRS, 0, False, True)

        def way(eng, windowed, by_blocks):
            eng.wait_ge(flag_ready, 1)
            eng.nop(nofuse=True)
            unsuited = eng.value_load(general[0:1, 0:1], min_val=0, max_val=1)
            with eng.If(unsuited < 1):
                windowed()
            with eng.Else():
                by_blocks()

        @block.sync
        def _(sp):
            for off, to, loaded in ((0, dcur, l_dst), (1, dnext, l_next), (HALO_EDGES + 1, dfar, l_next)):
                sp.dma_start(to, edges[1, FRONT + off:FRONT + off + E].rearrange("(p f) -> p f", p=W)).then_inc(loaded, 16)
            for i in range(5):
                a, b = i * NW // 5, (i + 1) * NW // 5
                sp.dma_start(xs[:, a:b, :], x[a * W:b * W, :].rearrange("(t p) d -> p t d", p=W)).then_inc(l_x[i], 16)
            sp.dma_start(Ds[:, :, :], Dmat.rearrange("(c p) d -> p c d", p=128)).then_inc(l_dense, 16)
            hrow_w = head_w.rearrange("(a k) -> a k", a=1)
            sp.dma_start(hw[:, :], bass.AP(hrow_w.tensor, 0, [[0, KR], [1, K]])).then_inc(l_dense, 16)
            sp.dma_start(hwcol[:, :], bass.AP(hrow_w.tensor, 0, [[1, K], [0, R], [1, 1]])).then_inc(l_dense, 16)
            sp.wait_ge(starts_ready, 1)
            load_rows(sp, *GROUPS[0], l_rows[0])

            def load_window(t, h):
                first = sp.value_load(starts[0:1, bass.ds(t, 1)], min_val=0, max_val=E)
                one = edges[1, bass.ds(first + FRONT, SPAN)]
                sp.dma_start(dst_bc[h], bass.AP(edges.tensor, one.offset, [[0, W], [1, SPAN]])).then_inc(l_bc[h], 16)
                hal = edges[1, bass.ds(first + FRONT - 129, (C - 1) * 128 + HALO)]
                sp.dma_start(halo_i[:, h, :], bass.AP(edges.tensor, hal.offset,
                                                      [[128, C], [0, K], [1, HALO]])).then_inc(l_halo[h], 16)

            for i in range(5):
                a, b = i * NW // 5, (i + 1) * NW // 5
                sp.wait_ge(v_zu, b + CREDIT)
                sp.dma_start(zu_table[a * W:b * W, :].rearrange("(t p) d -> p t d", p=W), zus[:, a:b, :]).then_inc(st_zu, 16)
            def load_gru():
                sp.wait_ge(v_head, 6)
                for n, w in enumerate((w_ih, w_hh)):
                    sp.dma_start(wrow[:, n * WC:(n + 1) * WC, :], w.rearrange("(c p) d -> p c d", p=128)).then_inc(l_gru, 16)
                    sp.dma_start(brow[:, n, :], (b_ih, b_hh)[n].rearrange("(a d) -> a d", a=1)).then_inc(l_gru, 16)
                sp.dma_start(rels[:, :], rel).then_inc(l_gru, 16)

            def store_h2(t, h):
                sp.wait_ge(h2_made, t + 1)
                sp.dma_start(h2_table[bass.ds(t * W, W), :], h2s[:, h, :]).then_inc(st_h2, 16)
                sp.wait_ge(st_h2, 16 * (t + 1))
                sp.sem_inc(h2s_free, 1)

            def prefetch(t, h):
                sp.wait_ge(oht_made, t + 1)
                sp.wait_ge(cut_raw, t + 1)
                load_window(t + 2, h)
                store_h2(t, h)

            def load_h2(t, h):
                sp.dma_start(h2s[:, h, :], h2_table[bass.ds(t * W, W), :]).then_inc(l_h2[h], 16)

            def out_window(t, h):
                sp.wait_ge(out_made, t + 1)
                sp.dma_start(out[bass.ds(t * W, W), :], outs[:, h, :]).then_inc(st_out, 16)
                sp.wait_ge(st_out, 16 * (t + 1))
                sp.sem_inc(outs_free, 1)

            def turn(t, h):
                out_window(t, h)
                load_h2(t + 2, h)

            def place_relations():
                sp.wait_ge(v_bias, 3)
                sp.wait_ge(a_relw, 2)
                sp.dma_start(relw[KR:KR + RELS, :], relw_low[:, :]).then_inc(l_bias, 16)
                sp.dma_start(relw[KR + RELS:KR + RELS + 1, :], bfull[:, :]).then_inc(l_bias, 16)

            def second_layer():
                load_h2(0, 0)
                load_h2(1, 1)
                with sp.Fori(0, PAIRS - 1) as i:
                    turn(2 * i, 0)
                    turn(2 * i + 1, 1)
                turn(NW - 3, 0)
                out_window(NW - 2, 1)
                out_window(NW - 1, 0)
                sp.wait_ge(st_out, 16 * NW)

            def windowed():
                load_window(0, 0)
                load_window(1, 1)
                load_gru()
                with sp.Fori(0, PAIRS - 1) as i:
                    prefetch(2 * i, 0)
                    prefetch(2 * i + 1, 1)
                prefetch(NW - 3, 0)
                store_h2(NW - 2, 1)
                store_h2(NW - 1, 0)
                place_relations()
                second_layer()

            def by_blocks():
                load_gru()
                place_relations()
                for n, to in enumerate((src_col[:, 0:BLOCKS, :], any_dst_i, any_kind_i)):
                    sp.dma_start(to, edges[n, FRONT:FRONT + BLOCKS * SPAN].rearrange(
                        "(q p j) -> p q j", p=128, j=C)).then_inc(any_in, 16)
                with sp.Fori(0, BLOCKS) as q:
                    sp.wait_ge(any_L_made, q + 1 + FREE)
                    sp.dma_start(logit_table[:, bass.ds(q * SPAN, SPAN)].rearrange("k (p j) -> p k j", j=C),
                                 any_L[:, bass.ds(q * K * C, K * C)].rearrange("p (k j) -> p k j", k=K)).then_inc(any_L_out, 16)
                sp.wait_ge(any_L_out, 16 * BLOCKS)
                with sp.Fori(0, BLOCKS) as q:
                    sp.wait_ge(any_row_used, q * K + FREE)
                    one = edges[1, bass.ds(q * SPAN + FRONT, SPAN)]
                    sp.dma_start(any_dst_row, bass.AP(edges.tensor, one.offset, [[0, W], [1, SPAN]])).then_inc(l_any_dst, 16)
                    for k in range(K):
                        if k:
                            sp.wait_ge(any_row_used, q * K + k + FREE)
                        one = logit_table[k, bass.ds(q * SPAN, SPAN)]
                        sp.dma_start(any_row, bass.AP(logit_table.tensor, one.offset, [[0, W], [1, SPAN]])).then_inc(l_any_row, 16)
                sp.wait_ge(any_most_made, BLOCKS * K * NW + FREE)
                sp.dma_start(most_table.rearrange("(t p) k -> p t k", p=W), any_most[:, :, :]).then_inc(any_most_out, 16)
                with sp.Fori(0, PAIRS) as i:
                    store_h2(2 * i, 0)
                    store_h2(2 * i + 1, 1)
                store_h2(NW - 1, 0)
                second_layer()

            load_rows(sp, *GROUPS[2], l_rows[2])
            sp.wait_ge(a_col, 9)
            way(sp, windowed, by_blocks)

        @block.gpsimd
        def _(pool):
            nc.gpsimd.iota(win_first[:, :], pattern=[[W, NW]], base=0, channel_multiplier=0,
                           allow_small_or_imprecise_dtypes=True).then_inc(c_first, 1)
            nc.gpsimd.memset(ident[:, :], 0.0).then_inc(c_pool, 1)
            nc.gpsimd.iota(iota_w[:, :], pattern=[[1, 128]], base=0, channel_multiplier=0,
                           allow_small_or_imprecise_dtypes=True).then_inc(c_const, 1)
            nc.gpsimd.iota(iota_p[:, :], pattern=[[0, 1]], base=0, channel_multiplier=1,
                           allow_small_or_imprecise_dtypes=True).then_inc(c_const, 1)
            nc.gpsimd.iota(node_id[:, :], pattern=[[W, NW]], base=0, channel_multiplier=1,
                           allow_small_or_imprecise_dtypes=True).then_inc(c_const, 1)
            nc.gpsimd.memset(ones[:, :], 1.0).then_inc(c_const, 1)
            nc.gpsimd.memset(eps_col[:, :], EPS).then_inc(c_const, 1)
            nc.gpsimd.memset(cnt_rows[:, :], 1.0).then_inc(c_const, 1)
            nc.gpsimd.memset(relw_low[:, :], 0.0).then_inc(c_const, 1)
            nc.gpsimd.memset(L[:, :, :], -BIG).then_inc(c_const, 1)
            pool.wait_ge(c_pool, 1)
            nc.gpsimd.affine_select(out=ident[:, :], in_=ident[:, :], compare_op=ALU.not_equal, fill=1.0,
                                    base=0, pattern=[[-1, 128]], channel_multiplier=1).then_inc(c_ident, 1)

            def gather(i, h, table, to, done, layer):
                pool.wait_ge(sidx_made[h], layer * (PAIRS + 1 - h) + i + 1)
                pool.nop(nofuse=True)
                for c, (a, b) in enumerate((CHUNKS, CHUNKS2)[layer]):
                    for j in range(a, b):
                        nc.gpsimd.indirect_dma_start(
                            out=to(h, j), out_offset=None, in_=table,
                            in_offset=bass.IndirectOffsetOnAxis(ap=sidx[:, h, j:j + 1], axis=0),
                        ).then_inc(done[h][c], 16)

            def windowed():
                pool.wait_ge(a_col, 1)
                for h in range(2):
                    nc.gpsimd.tensor_copy(sidx[:, h, :], src_col[:, h, :]).then_inc(sidx_made[h], 1)
                pool.wait_ge(st_zu, 16 * 5)
                windows(pool, lambda t, i, h: gather(
                    i, h, zu_table, lambda h, j: zs[h][:, j * KR:(j + 1) * KR], g_zs, 0))
                pool.wait_ge(st_h2, 16 * NW)
                windows(pool, lambda t, i, h: gather(
                    i, h, h2_table, lambda h, j: hg[h][:, j, :], g_h, 1))

            def block_gather(q, n, index, table, to):
                nc.gpsimd.tensor_copy(sidx[:, n % 2, :], index[:, bass.ds(q * C, C)]).then_inc(any_idx, 1)

                def rows():
                    for j in range(C):
                        nc.gpsimd.indirect_dma_start(
                            out=to(j), out_offset=None, in_=table,
                            in_offset=bass.IndirectOffsetOnAxis(ap=sidx[:, n % 2, j:j + 1], axis=0),
                        ).then_inc(any_g, 16)
                return rows

            def by_blocks():
                sources = src_col[:, :, :].rearrange("p q j -> p (q j)")
                pool.wait_ge(st_zu, 16 * 5)
                pool.wait_ge(any_in, 48)
                pool.wait_ge(any_cast, 4)
                with pool.Fori(0, BLOCKS) as q:
                    pool.wait_ge(any_L_made, q + FREE)
                    pool.nop(nofuse=True)
                    a = block_gather(q, 0, sources, zu_table, lambda j: zs[0][:, j * KR:(j + 1) * KR])
                    b = block_gather(q, 1, any_near_i, zu_table, lambda j: zs[1][:, j * KR:(j + 1) * KR])
                    pool.wait_ge(any_idx, 2 * q + 2)
                    pool.nop(nofuse=True)
                    a()
                    b()
                pool.wait_ge(any_most_out, 16)
                with pool.Fori(0, BLOCKS) as q:
                    pool.wait_ge(any_agg_made, q * NW + FREE)
                    pool.nop(nofuse=True)
                    a = block_gather(q, 0, sources, zu_table, lambda j: zs[0][:, j * KR:(j + 1) * KR])
                    b = block_gather(q, 1, any_near_i, most_table, lambda j: most_e[:, j * K:(j + 1) * K])
                    pool.wait_ge(any_idx, 2 * BLOCKS + 2 * q + 2)
                    pool.nop(nofuse=True)
                    a()
                    b()
                pool.wait_ge(st_h2, 16 * NW)
                with pool.Fori(0, BLOCKS) as q:
                    pool.wait_ge(any_red_made, q * NW + FREE)
                    pool.nop(nofuse=True)
                    a = block_gather(q, 0, sources, h2_table, lambda j: hg[0][:, j, :])
                    pool.wait_ge(any_idx, 4 * BLOCKS + q + 1)
                    pool.nop(nofuse=True)
                    a()

            pool.wait_ge(starts_ready, 1)
            load_rows(pool, *GROUPS[1], l_rows[1])
            way(pool, windowed, by_blocks)

        @block.vector
        def _(dve):
            dve.sem_inc(V_made, CREDIT)
            dve.sem_inc(v_zu, CREDIT)

            dve.wait_ge(c_first, 1)
            nc.vector.tensor_scalar(half_below[:, :], win_first[0:W, :], -0.5, None, ALU.add).then_inc(v_half, 1)
            dve.wait_ge(l_dst, 16)
            for t in range(SPLIT):
                if t:
                    dve.wait_ge(v_cnt, t)
                nc.vector.tensor_scalar(junk[:, 0:EF], dcur, float(W * t), 0.0, ALU.is_lt, ALU.add,
                                        accum_out=cnt[:, t:t + 1]).then_inc(v_cnt, 1)
            dve.wait_ge(l_next, 32)
            nc.vector.tensor_tensor(unfit[:, 0, :], dcur, dnext, ALU.is_gt).then_inc(v_unfit, 1)
            nc.vector.tensor_tensor(unfit[:, 1, :], dcur, dfar, ALU.is_equal).then_inc(v_unfit, 1)

            for i in range(5):
                a, b = i * NW // 5, (i + 1) * NW // 5
                dve.wait_ge(l_x[i], 16)
                for t in range(a, b):
                    nc.vector.bn_stats(bst[:, t, :], xs[:, t, :]).then_inc(v_bst, 1)
                for t in range(a, b):
                    dve.wait_ge(v_bst, t + 1)
                    nc.vector.bn_aggr(mv[:, t, :], bst[:, t, :]).then_inc(v_mv, 1)
            dve.wait_ge(p_tot, 1)
            nc.vector.tensor_copy(tot[:, 0:NW], ps(7, 1, 0, NW)).then_inc(v_chk, 1)
            dve.wait_ge(v_chk, 1)
            nc.vector.tensor_scalar(tot[:, SPLIT:NW], tot[:, SPLIT:NW], float(E), 0.5, ALU.add, ALU.mult).then_inc(v_chk, 1)
            dve.wait_ge(v_chk, 2)
            nc.vector.tensor_copy(starts[:, 0:NW], tot[:, 0:NW]).then_inc(starts_ready, 1)
            nc.vector.memset(tot[:, NW:NW + 1], float(E)).then_inc(v_chk, 1)
            dve.wait_ge(p_flag, 1)
            nc.vector.tensor_copy(bad[:, 0:1], ps(5, 1, 0, 1)).then_inc(v_chk, 1)
            dve.wait_ge(a_rstd, 2)
            nc.vector.scalar_tensor_tensor(nmr[:, :], mv[:, :, 0], -1.0, rstd[:, :], ALU.mult, ALU.mult).then_inc(v_nmr, 1)

            def turn_h(t, h):
                dve.wait_ge(p_hT, t + 1 + CREDIT)
                nc.vector.tensor_copy(hTs[:, h, :], ps(h, 128, 0, CH * W)).then_inc(v_hT, 1)

            def project(t, h, ahead=True):
                if ahead:
                    turn_h(t + 1, 1 - h)
                dve.wait_ge(p_zub, t + 1)
                dve.nop(nofuse=True)
                nc.vector.tensor_copy(flat(zus[:, :, :], t, KR), ps(2 + h, W, 0, KR)).then_inc(v_zu, 1)

            turn_h(0, 0)
            with dve.Fori(0, PAIRS // 2) as i:
                for n in range(4):
                    project(4 * i + n, n % 2)
            project(NW - 1, 0, False)

            dve.wait_ge(v_chk, 4)
            nc.vector.tensor_tensor(tdiff[:, :], tot[:, 1:NW + 1], tot[:, 0:NW], ALU.subtract).then_inc(v_chk, 1)
            dve.wait_ge(v_chk, 5)
            nc.vector.reduce_max(bad[:, 1:2], tdiff[:, :], axis=AXX).then_inc(v_chk, 1)
            dve.wait_ge(v_chk, 6)
            nc.vector.scalar_tensor_tensor(bad[:, 2:3], bad[:, 1:2], float(SPAN), bad[:, 0:1], ALU.is_gt, ALU.add).then_inc(v_chk, 1)
            dve.wait_ge(v_chk, 7)
            nc.vector.tensor_scalar(general[:, :], bad[:, 2:3], 0.5, None, ALU.is_gt).then_inc(flag_ready, 1)

            dve.wait_ge(l_dense, 48)
            nc.vector.reduce_max(hst[:, 0:1], hw[:, :], axis=AXX).then_inc(v_head, 1)
            dve.wait_ge(v_head, 1)
            nc.vector.tensor_scalar(hst[:, 1:2], hst[:, 0:1], -1.0, None, ALU.mult).then_inc(v_head, 1)
            dve.wait_ge(p_gd, 1)
            nc.vector.tensor_copy(DD[:, :, :].rearrange("p c d -> p (c d)"), ps(4, 128, 0, CH * D)).then_inc(v_gd, 1)
            for c in range(CH):
                dve.wait_ge(p_gd, 2 + c)
                nc.vector.tensor_tensor(VV[:, c, :], Ds[:, c, :], ps(2 + c, 128, 0, D), ALU.subtract).then_inc(v_gd, 1)
            dve.wait_ge(v_gd, 3)
            nc.vector.tensor_scalar(VV[:, :, :], VV[:, :, :], 0.25, None, ALU.mult).then_inc(v_gd, 1)
            dve.wait_ge(v_gd, 4)
            dve.wait_ge(c_ident, 1)
            for c in range(CH):
                d = VV[:, c, c * 128:(c + 1) * 128]
                nc.vector.scalar_tensor_tensor(d, ident[:, :], 0.5, d, ALU.mult, ALU.add).then_inc(v_gd, 1)
            for g in (1, 2):
                a, b = GROUPS[g]
                dve.wait_ge(l_rows[g], 16 * (b - a))
                nc.vector.tensor_copy(rows_f[:, a * 128:b * 128], rows_i[:, a * 128:b * 128]).then_inc(v_rowf, 1)
            dve.wait_ge(a_head, 2)
            nc.vector.reduce_sum(hst[:, 3:4], hw[:, :], axis=AXX).then_inc(v_head, 1)
            dve.wait_ge(v_head, 3)
            nc.vector.reciprocal(hst[:, 4:5], hst[:, 3:4]).then_inc(v_head, 1)
            dve.wait_ge(v_head, 4)
            nc.vector.tensor_tensor(hst[:, 5:6], hst[:, 4:5], hst[:, 2:3], ALU.mult).then_inc(v_head, 1)
            dve.wait_ge(v_head, 5)
            dve.wait_ge(p_gd, 4)
            nc.vector.tensor_scalar(UV[:, :], ps(4, KR, 0, D), hst[:, 5:6], None, ALU.mult).then_inc(v_head, 1)

            def one_hots(t, h, layer):
                in0 = iota_w[:, 0:W].unsqueeze(1).broadcast_to([128, C, W])
                col = flat(dst_col[:, :, :], t, C).unsqueeze(2).broadcast_to([128, C, W])
                o = oh[:, h, :].rearrange("p (j w) -> p j w", j=C)
                nc.vector.scalar_tensor_tensor(o, in0, win_first[:, bass.ds(t, 1)], col, ALU.add,
                                               ALU.is_equal).then_inc((oh_made, oh2_made)[layer], 1)

            def target_one_hots(t, i, h):
                dve.wait_ge(l_bc[h], 16 * (i + 1))
                nc.vector.tensor_scalar(ohT, dst_bc[h], node_id[0:W, bass.ds(t, 1)], None, ALU.is_equal).then_inc(oht_made, 1)

            def split_rows(t):
                zt = flat(zus[:, :, :], t, KR)
                nc.vector.tensor_copy(zu3[:, 0, :], zt).then_inc(zu3_made, 1)
                dve.wait_ge(zu3_made, 5 * t + 1)
                nc.vector.tensor_tensor(rest[:, 0, :], zt, zu3[:, 0, :], ALU.subtract).then_inc(zu3_made, 1)
                dve.wait_ge(zu3_made, 5 * t + 2)
                nc.vector.tensor_copy(zu3[:, 1, :], rest[:, 0, :]).then_inc(zu3_made, 1)
                dve.wait_ge(zu3_made, 5 * t + 3)
                nc.vector.tensor_tensor(rest[:, 1, :], rest[:, 0, :], zu3[:, 1, :], ALU.subtract).then_inc(zu3_made, 1)
                dve.wait_ge(zu3_made, 5 * t + 4)
                nc.vector.tensor_copy(zu3[:, 2, :], rest[:, 1, :]).then_inc(zu3_made, 1)

            def find_cuts(i, h):
                dve.wait_ge(l_halo[h], 16 * (i + 1))
                nc.vector.tensor_tensor(cut[:, h, 1:HALO], halo_i[:, h, 1:HALO], halo_i[:, h, 0:HALO - 1],
                                        ALU.not_equal).then_inc(cut_raw, 1)

            def relation_one_hots(t):
                kc = flat(kind_col[:, :, :], t, C).unsqueeze(2).broadcast_to([128, C, RELS])
                io = iota_w[:, 0:RELS].unsqueeze(1).broadcast_to([128, C, RELS])
                nc.vector.tensor_tensor(V[:, :, KR + K:SUMS], io, kc, ALU.is_equal).then_inc(ohk_made, 1)

            def logits(t, i, h, c):
                a, b = CHUNKS[c]
                dve.wait_ge(g_zs[h][c], 16 * (b - a) * (i + 1))
                dve.wait_ge(zd_made[c], t + 1)
                nc.vector.tensor_tensor(prod[:, a * KR:b * KR], zs[h][:, a * KR:b * KR], ps(c, 128, 0, (b - a) * KR),
                                        ALU.mult).then_inc(prod_made, 1)
                dve.wait_ge(prod_made, 3 * t + c + 1)
                nc.vector.tensor_reduce(L[:, 1 + a:1 + b, :],
                                        prod[:, a * KR:b * KR].rearrange("p (j k r) -> p j k r", k=K, r=R),
                                        AXX, ALU.add).then_inc(L_made, 1)

            def sources(t, h):
                dve.nop(nofuse=True)
                nc.vector.tensor_copy(sidx[:, h, :], flat(src_col[:, :, :], t, C)).then_inc(sidx_made[h], 1)

            def biases():
                dve.wait_ge(l_gru, 16 * 5)
                nc.vector.tensor_tensor(bfull[:, 0:2 * D], brow[:, 0, 0:2 * D], brow[:, 1, 0:2 * D], ALU.add).then_inc(v_bias, 1)
                nc.vector.tensor_copy(bfull[:, 2 * D:3 * D], brow[:, 0, 2 * D:3 * D]).then_inc(v_bias, 1)
                nc.vector.tensor_copy(bfull[:, 3 * D:4 * D], brow[:, 1, 2 * D:3 * D]).then_inc(v_bias, 1)

            def attend(t, i, h, first, last):
                logits(t, i, h, 0)
                if not first:
                    renew(t - 1)
                logits(t, i, h, 1)
                if not first:
                    shift(t - 1)
                logits(t, i, h, 2)
                dve.wait_ge(LT_made, t + 1)
                dve.wait_ge(cut_made, t + 1)
                nc.vector.tensor_tensor_scan(runs[:, 0, :], cutf[:, h, 1:2 * HALO_EDGES + 1], ps(3, K * C, 0, 256), -BIG,
                                             ALU.add, ALU.max).then_inc(runs_made, 1)
                nc.vector.tensor_tensor_scan(runs[:, 1, ::-1], cutf[:, h, HALO_EDGES + 2:HALO][:, ::-1],
                                             ps(3, K * C, 128, 384)[:, ::-1],
                                             -BIG, ALU.add, ALU.max).then_inc(runs_made, 1)
                dve.wait_ge(runs_made, 2 * t + 2)
                nc.vector.tensor_tensor(segmax[:, :], runs[:, 0, 128:256], runs[:, 1, 0:128], ALU.max).then_inc(segmax_made, 1)
                ahead = (t + 1, i + h, 1 - h)
                if not last:
                    target_one_hots(*ahead)
                dve.wait_ge(mT_made, t + 1)
                nc.vector.tensor_tensor(dif[:, :], L[:, 1:C + 1, :].rearrange("p j k -> p (j k)"),
                                        ps(4, 128, 0, K * C), ALU.subtract).then_inc(dif_made, 1)
                if not last:
                    split_rows(t + 1)
                dve.wait_ge(P_made, t + 1)
                nc.vector.tensor_tensor(V[:, :, 0:KR].rearrange("p j (k r) -> p j k r", k=K),
                                        zs[h].rearrange("p (j k r) -> p j k r", k=K, r=R),
                                        V[:, :, KR:KR + K].unsqueeze(3).broadcast_to([128, C, K, R]),
                                        ALU.mult).then_inc(V_made, 1)
                if last:
                    dve.wait_ge(V_made, NW + CREDIT)
                    sources(0, 0)
                elif not (isinstance(t, int) and t == NW - 2):
                    dve.wait_ge(V_made, t + 1 + CREDIT)
                    sources(t + 2, h)
                if not last:
                    find_cuts(i + h, 1 - h)
                    one_hots(t + 1, 1 - h, 0)
                else:
                    biases()
                dve.wait_ge(agg_made, t + 1)
                weigh(t, ps(5, W, 0, SUMS))
                if not last:
                    relation_one_hots(t + 1)
                keep_means(t)

            def weigh(t, sums):
                nc.vector.tensor_scalar(den[:, 0, :], sums[:, KR:KR + K], 1e-16, None, ALU.add).then_inc(den_made, 1)
                dve.wait_ge(den_made, 2 * t + 1)
                nc.vector.reciprocal(den[:, 1, :], den[:, 0, :]).then_inc(den_made, 1)
                dve.wait_ge(den_made, 2 * t + 2)
                nc.vector.tensor_tensor(means[:, 0:KR].rearrange("p (k r) -> p k r", k=K),
                                        sums[:, 0:KR].rearrange("p (k r) -> p k r", k=K),
                                        den[:, 1, :].unsqueeze(2).broadcast_to([W, K, R]), ALU.mult).then_inc(means_made, 1)
                nc.vector.tensor_copy(means[:, KR:KR + RELS], sums[:, KR + K:SUMS]).then_inc(means_made, 1)

            def keep_means(t):
                dve.wait_ge(turned_made, t + 1)
                dve.wait_ge(cnt_kept, t + 1)
                nc.vector.tensor_copy(meansT[:, :], ps(4, KR + RELS, 0, W)).then_inc(meansT_made, 1)

            def renew(t):
                dve.wait_ge(grad_made, t + 1)
                nc.vector.tensor_scalar(tmp[:, :], ps(6, W, 0, D), THRESH, 0.0, ALU.subtract, ALU.max).then_inc(x1_made, 1)
                dve.wait_ge(x1_made, 2 * t + 1)
                xt = flat(xs[:, :, :], t, D)
                nc.vector.tensor_tensor(xt, xt, tmp[:, :], ALU.add).then_inc(x1_made, 1)
                dve.wait_ge(x1_made, 2 * t + 2)
                dve.nop(nofuse=True)
                nc.vector.bn_stats(stat[:, :], xt).then_inc(stat_made, 1)
                dve.wait_ge(stat_made, t + 1)
                dve.nop(nofuse=True)
                nc.vector.bn_aggr(mvw[:, :], stat[:, :]).then_inc(var_made, 1)

            def shift(t):
                dve.wait_ge(ln_made, 2 * t + 2)
                nc.vector.scalar_tensor_tensor(rsw[:, 2:3], mvw[:, 0:1], -1.0, rsw[:, 1:2], ALU.mult, ALU.mult).then_inc(rsw_made, 1)

            def gru(t, i, h, ahead):
                if ahead:
                    dve.wait_ge(red_made, t + CREDIT)
                    sources(t + 1, 1 - h)
                    one_hots(t + 1, 1 - h, 1)
                mix_gates(t, h)

            def mix_gates(t, h):
                gate = (5, 3)[h]
                dve.wait_ge(rz_made, t + 1)
                nc.vector.tensor_tensor(nn[:, :], rz[:, h, 0:D], ps(gate, W, D, 2 * D), ALU.mult).then_inc(nn_pre, 1)
                dve.wait_ge(nn_pre, 2 * t + 1)
                nc.vector.tensor_tensor(nn[:, :], nn[:, :], ps(gate, W, 0, D), ALU.add).then_inc(nn_pre, 1)
                dve.wait_ge(nn_made, t + 1)
                nc.vector.tensor_tensor(dd[:, :], h2s[:, h, :], nn[:, :], ALU.subtract).then_inc(mix, 1)
                dve.wait_ge(mix, 3 * t + 1)
                nc.vector.tensor_tensor(dd[:, :], dd[:, :], rz[:, h, D:2 * D], ALU.mult).then_inc(mix, 1)
                dve.wait_ge(mix, 3 * t + 2)
                nc.vector.tensor_tensor(dd[:, :], dd[:, :], nn[:, :], ALU.add).then_inc(mix, 1)
                dve.wait_ge(mix, 3 * t + 3)
                dve.wait_ge(outs_free, t + 1)
                nc.vector.tensor_tensor(outs[:, h, :], dd[:, :], flat(xs[:, :, :], t, D), ALU.add).then_inc(out_made, 1)

            def windowed():
                target_one_hots(0, 0, 0)
                split_rows(0)
                find_cuts(0, 0)
                one_hots(0, 0, 0)
                relation_one_hots(0)
                overlapped(dve, attend)
                renew(NW - 1)
                shift(NW - 1)
                one_hots(0, 0, 1)
                with dve.Fori(0, PAIRS) as i:
                    gru(2 * i, i, 0, True)
                    gru(2 * i + 1, i, 1, True)
                gru(NW - 1, PAIRS, 0, False)

            def block_one_hots(q, t):
                in0 = iota_w[:, 0:W].unsqueeze(1).broadcast_to([128, C, W])
                col = flat(dst_col[:, :, :], q, C).unsqueeze(2).broadcast_to([128, C, W])
                nc.vector.scalar_tensor_tensor(oh[:, 0, :].rearrange("p (j w) -> p j w", j=C), in0,
                                               win_first[:, bass.ds(t, 1)], col, ALU.add, ALU.is_equal).then_inc(any_oh, 1)

            def by_blocks():
                for counted in (any_row_used, any_L_made, any_agg_kept, any_red_kept, any_most_made):
                    dve.sem_inc(counted, FREE)
                biases()
                dve.wait_ge(any_in, 48)
                nc.vector.tensor_copy(dst_col[:, 0:BLOCKS, :], any_dst_i).then_inc(any_cast, 1)
                nc.vector.tensor_copy(kind_col[:, 0:BLOCKS, :], any_kind_i).then_inc(any_cast, 1)
                dve.wait_ge(any_cast, 2)
                nc.vector.tensor_scalar(any_near, dst_col[:, 0:BLOCKS, :].rearrange("p q j -> p (q j)"), float(N - 1),
                                        None, ALU.min).then_inc(any_cast, 1)
                dve.wait_ge(any_cast, 3)
                nc.vector.tensor_copy(any_near_i, any_near).then_inc(any_cast, 1)
                nc.vector.memset(any_most[:, :, :], -BIG).then_inc(any_zero, 1)
                dve.wait_ge(a_wT, 8)
                nc.vector.memset(any_agg, 0.0).then_inc(any_zero, 1)

                with dve.Fori(0, BLOCKS) as q:
                    dve.wait_ge(any_g, 16 * 2 * C * (q + 1))
                    nc.vector.tensor_tensor(prod[:, :], zs[0], zs[1], ALU.mult).then_inc(any_prod, 1)
                    dve.wait_ge(any_prod, q + 1)
                    nc.vector.tensor_reduce(any_L[:, bass.ds(q * K * C, K * C)].rearrange("p (k j) -> p j k", k=K),
                                            prod[:, :].rearrange("p (j k r) -> p j k r", k=K, r=R),
                                            AXX, ALU.add).then_inc(any_L_made, 1)

                dve.wait_ge(any_zero, 2)
                with dve.Fori(0, BLOCKS) as q:
                    dve.wait_ge(l_any_dst, 16 * (q + 1))
                    for k in range(K):
                        dve.wait_ge(l_any_row, 16 * (q * K + k + 1))
                        dve.nop(nofuse=True)
                        with dve.Fori(0, NW) as t:
                            n = (q * K + k) * NW + t
                            nc.vector.tensor_scalar(any_mask, any_dst_row, node_id[0:W, bass.ds(t, 1)], BIG,
                                                    ALU.is_equal, ALU.mult).then_inc(any_masks, 1)
                            dve.wait_ge(any_masks, 2 * n + 1)
                            nc.vector.scalar_tensor_tensor(any_masked, any_mask, BIG, any_row, ALU.subtract,
                                                           ALU.add).then_inc(any_masks, 1)
                            dve.wait_ge(any_masks, 2 * n + 2)
                            nc.vector.reduce_max(any_top[:, :], any_masked, axis=AXX).then_inc(any_tops, 1)
                            dve.wait_ge(any_tops, n + 1)
                            dve.wait_ge(any_most_made, n + FREE)
                            dve.nop(nofuse=True)
                            most = any_most[:, :, :].rearrange("p t k -> p (t k)")[:, bass.ds(t * K + k, 1)]
                            nc.vector.tensor_tensor(most, most, any_top[:, :], ALU.max).then_inc(any_most_made, 1)
                        dve.sem_inc(any_row_used, 1)

                with dve.Fori(0, BLOCKS) as q:
                    dve.wait_ge(any_g, 16 * 2 * C * (q + 1 + BLOCKS))
                    dve.nop(nofuse=True)
                    nc.vector.tensor_tensor(dif[:, :].rearrange("p (k j) -> p k j", k=K),
                                            any_L[:, bass.ds(q * K * C, K * C)].rearrange("p (k j) -> p k j", k=K),
                                            most_e[:, :].rearrange("p (j k) -> p k j", k=K), ALU.subtract).then_inc(any_dif, 1)
                    dve.wait_ge(any_dif, 2 * q + 1)
                    nc.vector.tensor_scalar(dif[:, :], dif[:, :], 0.0, None, ALU.min).then_inc(any_dif, 1)
                    dve.wait_ge(any_P, q + 1)
                    nc.vector.tensor_tensor(V[:, :, 0:KR].rearrange("p j (k r) -> p j k r", k=K),
                                            zs[0].rearrange("p (j k r) -> p j k r", k=K, r=R),
                                            V[:, :, KR:KR + K].unsqueeze(3).broadcast_to([128, C, K, R]),
                                            ALU.mult).then_inc(any_V, 1)
                    kc = flat(kind_col[:, :, :], q, C).unsqueeze(2).broadcast_to([128, C, RELS])
                    io = iota_w[:, 0:RELS].unsqueeze(1).broadcast_to([128, C, RELS])
                    nc.vector.tensor_tensor(V[:, :, KR + K:SUMS], io, kc, ALU.is_equal).then_inc(any_ohk, 1)
                    dve.nop(nofuse=True)
                    with dve.Fori(0, NW) as t:
                        n = q * NW + t
                        dve.wait_ge(any_agg_made, n + FREE)
                        dve.nop(nofuse=True)
                        block_one_hots(q, t)
                        dve.wait_ge(any_agg_made, n + 1 + FREE)
                        dve.wait_ge(any_agg_kept, n + FREE)
                        dve.nop(nofuse=True)
                        a = any_agg[:, bass.ds(t * SUMS, SUMS)]
                        nc.vector.tensor_tensor(a, a, ps(5, W, 0, SUMS), ALU.add).then_inc(any_agg_kept, 1)
                dve.wait_ge(any_agg_kept, BLOCKS * NW + FREE)

                def finish(t, i, h):
                    weigh(t, any_agg[:, bass.ds(t * SUMS, SUMS)])
                    keep_means(t)
                    renew(t)
                    shift(t)

                windows(dve, finish)

                dve.wait_ge(rsw_made, NW)
                dve.wait_ge(l_bias, 32)
                nc.vector.memset(any_red, 0.0).then_inc(any_zero, 1)
                dve.wait_ge(any_zero, 3)
                with dve.Fori(0, BLOCKS) as q:
                    dve.nop(nofuse=True)
                    with dve.Fori(0, NW) as t:
                        n = q * NW + t
                        dve.wait_ge(any_red_made, n + FREE)
                        dve.nop(nofuse=True)
                        block_one_hots(q, t)
                        dve.wait_ge(any_red_made, n + 1 + FREE)
                        dve.wait_ge(any_red_kept, CH * n + FREE)
                        dve.nop(nofuse=True)
                        for c in range(CH):
                            a = any_red[:, bass.ds(t * W + c * N, W)]
                            nc.vector.tensor_tensor(a, a, ps(c, 128, 0, W), ALU.add).then_inc(any_red_kept, 1)
                windows(dve, lambda t, i, h: mix_gates(t, h))

            dve.sem_inc(outs_free, CREDIT)
            dve.wait_ge(c_const, 8)
            dve.wait_ge(a_col, 9)
            way(dve, windowed, by_blocks)

        @block.scalar
        def _(act):
            nc.scalar.preload_act_table_set("natural_log_exp_and_others")
            for c in range(CH):
                act.dma_start(Us[:, c, :].rearrange("p (k r) -> p k r", k=K),
                              U[:, c * 128:(c + 1) * 128, :].rearrange("k d r -> d k r")).then_inc(l_small, 16)

            act.wait_ge(l_dst, 16)
            act.wait_ge(v_half, 1)
            for t in range(SPLIT, NW):
                nc.scalar.activation(junk2, dcur, ACT.Sign, bias=half_below[:, t:t + 1], scale=-1.0,
                                     accum_out=cnt[:, t:t + 1]).then_inc(a_cnt, 1)
                act.wait_ge(a_cnt, t - SPLIT + 1)
            act.wait_ge(v_unfit, 2)
            nc.scalar.activation(unfit[:, :, :], unfit[:, :, :], ACT.Relu, accum_out=misfits[:, :]).then_inc(a_misfit, 1)
            act.wait_ge(v_mv, NW)
            act.wait_ge(c_const, 8)
            nc.scalar.activation(rstd[:, :], mv[:, :, 1], ACT.Ln, bias=eps_col[0:W, :]).then_inc(a_rstd, 1)
            act.wait_ge(a_rstd, 1)
            nc.scalar.activation(rstd[:, :], rstd[:, :], ACT.Exp, scale=-0.5).then_inc(a_rstd, 1)
            act.wait_ge(a_rstd, 2)
            act.wait_ge(v_nmr, 1)

            def normalise(t, h):
                act.wait_ge(p_hT, t + 1)
                act.nop(nofuse=True)
                nc.scalar.activation(hn[:, h, :], flat(xs[:, :, :], t, D), ACT.Relu, bias=nmr[:, bass.ds(t, 1)],
                                     scale=rstd[:, bass.ds(t, 1)]).then_inc(a_hn, 1)

            with act.Fori(0, PAIRS // 2) as i:
                for n in range(4):
                    normalise(4 * i + n, n % 2)
            normalise(NW - 1, 0)

            def keep_columns(g):
                a, b = GROUPS[g]
                act.wait_ge(p_col, g + 1)
                v = ps(5 + g, 128, 0, (b - a) * 3 * C).rearrange("p (t n j) -> p t n j", n=3, j=C)
                for n, to in enumerate((src_col, dst_col, kind_col)):
                    nc.scalar.activation(to[:, a:b, :], v[:, :, n, :], ACT.Copy).then_inc(a_col, 1)

            a, b = GROUPS[0]
            act.wait_ge(l_rows[0], 16 * b)
            nc.scalar.activation(rows_f[:, 0:b * 128], rows_i[:, 0:b * 128], ACT.Copy).then_inc(a_rowf, 1)
            keep_columns(0)
            act.wait_ge(v_head, 2)
            nc.scalar.activation(hw[:, :], hw[:, :], ACT.Exp, bias=hst[:, 1:2]).then_inc(a_head, 1)
            nc.scalar.activation(hst[:, 2:3], hwcol[:, :], ACT.Exp, bias=hst[:, 1:2]).then_inc(a_head, 1)
            keep_columns(1)
            keep_columns(2)

            def keep_weights(groups=range(8)):
                for g in groups:
                    n, c, half = g // 4, g // 2 % 2, g % 2
                    act.wait_ge(p_wT, g + 1)
                    to = (wihT, whhT)[n]
                    nc.scalar.activation(to[:, c, half * G3 // 2:(half + 1) * G3 // 2], ps((7, 3)[g % 2], 128, 0, G3 // 2),
                                         ACT.Copy).then_inc(a_wT, 1)

            def keep_relations():
                act.wait_ge(p_relT, 1)
                nc.scalar.activation(relT[:, :], ps(5, 128, 0, CH * RELS), ACT.Copy).then_inc(a_relT, 1)
                act.wait_ge(p_relw, 1)
                nc.scalar.activation(relw_low[:, 0:2 * D], ps(7, RELS, 0, 2 * D), ACT.Copy).then_inc(a_relw, 1)
                nc.scalar.activation(relw_low[:, 2 * D:3 * D], ps(4, RELS, 0, D), ACT.Copy).then_inc(a_relw, 1)

            act.sem_inc(h2s_free, CREDIT)
            act.sem_inc(cnt_kept, 1)

            def cuts(t, h):
                act.wait_ge(cut_raw, t + 1)
                nc.scalar.activation(cutf[:, h, 1:HALO], cut[:, h, 1:HALO], ACT.Copy, scale=-BIG).then_inc(cut_made, 1)

            def attend(t, i, h, first, last):
                if last:
                    keep_weights(range(0, 2))
                if not first:
                    normalise_rows(t - 1, 1 - h)
                keep_turned(t)
                act.wait_ge(dif_made, t + 1)
                nc.scalar.activation(V[:, :, KR:KR + K], dif[:, :].rearrange("p (j k) -> p j k", k=K), ACT.Exp,
                                     scale=float(R) ** -0.5).then_inc(P_made, 1)
                if not last:
                    cuts(t + 1, 1 - h)
                else:
                    keep_weights(range(2, 8))
                keep_counts(t)
                if not last:
                    dense_row(t + 1)

            def dense_row(t):
                if not (isinstance(t, int) and t == 0):
                    act.wait_ge(hrow_turned, t)
                    act.nop(nofuse=True)
                nc.scalar.activation(hrow, flat(xs[:, :, :], t, D), ACT.Relu, bias=nmr[:, bass.ds(t, 1)],
                                     scale=rstd[:, bass.ds(t, 1)]).then_inc(hrow_made, 1)

            def keep_turned(t):
                act.wait_ge(hrow_turned, t + 1)
                nc.scalar.activation(hTw, ps(5, 128, 0, CH * W), ACT.Copy).then_inc(hTw_kept, 1)

            def keep_counts(t):
                act.wait_ge(meansT_made, t + 1)
                act.nop(nofuse=True)
                nc.scalar.activation(cnt_rows[KR:KR + RELS, bass.ds(t * W, W)], meansT[KR:KR + RELS, :],
                                     ACT.Copy).then_inc(cnt_kept, 1)

            def normalise_rows(t, h):
                act.wait_ge(var_made, t + 1)
                nc.scalar.activation(rsw[:, 0:1], mvw[:, 1:2], ACT.Ln, bias=eps_col[0:W, :]).then_inc(ln_made, 1)
                act.wait_ge(ln_made, 2 * t + 1)
                nc.scalar.activation(rsw[:, 1:2], rsw[:, 0:1], ACT.Exp, scale=-0.5).then_inc(ln_made, 1)
                act.wait_ge(h2s_free, t + 1)
                act.wait_ge(rsw_made, t + 1)
                act.nop(nofuse=True)
                nc.scalar.activation(h2s[:, h, :], flat(xs[:, :, :], t, D), ACT.Relu, bias=rsw[:, 2:3],
                                     scale=rsw[:, 1:2]).then_inc(h2_made, 1)

            def gru(t, i, h):
                update(t, h, [ps(c, 128, 0, W) for c in range(CH)])

            def update(t, h, sums):
                nc.scalar.activation(cntT[KR:, h, :], cnt_rows[KR:, bass.ds(t * W, W)], ACT.Copy).then_inc(cntT_kept, 1)
                act.wait_ge(h2T_made, t + 1)
                nc.scalar.activation(h2T[:, :], ps(6, 128, 0, CH * W), ACT.Copy).then_inc(h2T_kept, 1)
                act.wait_ge(red_made, t + 1 + CREDIT)
                act.nop(nofuse=True)
                for c in range(CH):
                    nc.scalar.activation(redT[:, c * W:(c + 1) * W], sums[c], ACT.Copy).then_inc(red_kept, 1)
                act.wait_ge(gates_made, t + 1)
                nc.scalar.activation(rz[:, h, :], ps((4, 2)[h], W, 0, 2 * D), ACT.Sigmoid).then_inc(rz_made, 1)
                act.wait_ge(nn_pre, 2 * t + 2)
                nc.scalar.activation(nn[:, :], nn[:, :], ACT.Tanh).then_inc(nn_made, 1)

            def windowed():
                cuts(0, 0)
                dense_row(0)
                overlapped(act, attend)
                normalise_rows(NW - 1, 0)
                keep_relations()
                act.wait_ge(cnt_kept, NW + 1)
                windows(act, gru)

            def by_blocks():
                keep_weights()
                keep_relations()
                with act.Fori(0, BLOCKS) as q:
                    act.wait_ge(any_dif, 2 * q + 2)
                    nc.scalar.activation(V[:, :, KR:KR + K].rearrange("p j k -> p k j"),
                                         dif[:, :].rearrange("p (k j) -> p k j", k=K), ACT.Exp,
                                         scale=float(R) ** -0.5).then_inc(any_P, 1)

                def finish(t, i, h):
                    keep_turned(t)
                    keep_counts(t)
                    normalise_rows(t, h)

                dense_row(0)
                with act.Fori(0, PAIRS) as i:
                    finish(2 * i, i, 0)
                    dense_row(2 * i + 1)
                    finish(2 * i + 1, i, 1)
                    dense_row(2 * i + 2)
                finish(NW - 1, PAIRS, 0)
                act.wait_ge(cnt_kept, NW + 1)
                act.wait_ge(any_red_kept, CH * BLOCKS * NW + FREE)
                windows(act, lambda t, i, h: update(t, h, [any_red[:, bass.ds(t * W + c * N, W)] for c in range(CH)]))

            way(act, windowed, by_blocks)

        @block.tensor
        def _(pe):
            pe.sem_inc(p_hT, CREDIT)
            mm, tr = nc.tensor.matmul, nc.tensor.transpose
            pe.wait_ge(v_cnt, SPLIT)
            pe.wait_ge(a_cnt, NW - SPLIT)
            pe.wait_ge(c_const, 8)
            mm(ps(7, 1, 0, NW), ones[0:W, :], cnt[:, :], start=True, stop=True).then_inc(p_tot, 1)
            pe.wait_ge(a_misfit, 1)
            mm(ps(5, 1, 0, 1), ones[0:W, :], misfits[:, :], start=True, stop=True).then_inc(p_flag, 1)
            pe.wait_ge(l_dense, 48)
            for a in range(CH):
                for c in range(CH):
                    last = mm(ps(4, 128, a * D, (a + 1) * D), Ds[:, c, a * 128:(a + 1) * 128], Ds[:, c, :],
                              start=c == 0, stop=c == CH - 1)
            last.then_inc(p_gd, 1)
            pe.wait_ge(l_small, 16 * CH)
            pe.wait_ge(c_ident, 1)

            def turn_h(t, h):
                pe.wait_ge(a_hn, t + 1)
                for c in range(CH):
                    last = tr(ps(h, 128, c * W, (c + 1) * W), hn[:, h, c * 128:(c + 1) * 128], ident[0:W, 0:W])
                last.then_inc(p_hT, 1)

            def project(t, h, ahead=True):
                if ahead:
                    turn_h(t + 1, 1 - h)
                pe.wait_ge(v_hT, t + 1)
                pe.wait_ge(v_zu, t + 1)
                for c in range(CH):
                    last = mm(ps(2 + h, W, 0, KR), hTs[:, h, c * W:(c + 1) * W], Us[:, c, :],
                              start=c == 0, stop=c == CH - 1)
                last.then_inc(p_zub, 1)

            turn_h(0, 0)
            with pe.Fori(0, PAIRS // 2) as i:
                for n in range(4):
                    project(4 * i + n, n % 2)
            project(NW - 1, 0, False)

            def turn_rows_of_edges(g):
                a, b = GROUPS[g]
                for t in range(a, b):
                    last = tr(ps(5 + g, 128, (t - a) * 3 * C, (t - a + 1) * 3 * C), rows_f[:, t * 128:(t + 1) * 128],
                              ident[0:3 * C, 0:3 * C])
                last.then_inc(p_col, 1)

            pe.wait_ge(a_rowf, 1)
            pe.wait_ge(v_chk, 4)
            turn_rows_of_edges(0)
            pe.wait_ge(v_zu, NW + CREDIT)
            pe.wait_ge(v_gd, 1)
            for a in range(CH):
                for c in range(CH):
                    last = mm(ps(2 + a, 128, 0, D), DD[:, c, a * 128:(a + 1) * 128], Ds[:, c, :],
                              start=c == 0, stop=c == CH - 1)
                last.then_inc(p_gd, 1)
            pe.wait_ge(v_gd, 6)
            for c in range(CH):
                last = mm(ps(4, KR, 0, D), Us[:, c, :], VV[:, c, :], start=c == 0, stop=c == CH - 1)
            last.then_inc(p_gd, 1)
            for g in (1, 2):
                pe.wait_ge(v_rowf, g)
                turn_rows_of_edges(g)

            def turn_weights(groups=range(8)):
                pe.wait_ge(l_gru, 16 * 5)
                for g in groups:
                    n, c, half = g // 4, g // 2 % 2, g % 2
                    if g >= 2:
                        pe.wait_ge(a_wT, g - 1)
                    for m in range(WC // 2):
                        last = tr(ps((7, 3)[g % 2], 128, m * 128, (m + 1) * 128),
                                  wrow[:, n * WC + half * WC // 2 + m, c * 128:(c + 1) * 128], ident[:, :])
                    last.then_inc(p_wT, 1)

            def relation_products():
                for c in range(CH):
                    last = tr(ps(5, 128, c * RELS, (c + 1) * RELS), rels[:, c * 128:(c + 1) * 128], ident[0:RELS, 0:RELS])
                last.then_inc(p_relT, 1)
                pe.wait_ge(a_relT, 1)
                pe.wait_ge(a_wT, 8)
                for b, lo, hi in ((7, 0, 2 * D), (4, 2 * D, 3 * D)):
                    for c in range(CH):
                        last = mm(ps(b, RELS, 0, hi - lo), relT[:, c * RELS:(c + 1) * RELS], wihT[:, c, lo:hi],
                                  start=c == 0, stop=c == CH - 1)
                last.then_inc(p_relw, 1)
                pe.wait_ge(a_relw, 2)

            def target_rows(t):
                pe.wait_ge(oht_made, t + 1)
                pe.wait_ge(zu3_made, 5 * t + 5)
                for c, (a, b) in enumerate(CHUNKS):
                    for j in range(a, b):
                        for m in range(3):
                            last = mm(ps(c, 128, (j - a) * KR, (j - a + 1) * KR), ohT[:, j * 128:(j + 1) * 128],
                                      zu3[:, m, :], start=m == 0, stop=m == 2)
                    last.then_inc(zd_made[c], 1)

            def attend(t, h, ahead):
                turn_row(t)
                if not ahead:
                    turn_weights(range(0, 2))
                    pe.wait_ge(a_wT, 2)
                pe.wait_ge(L_made, 3 * t + 3)
                for s in range(3):
                    last = tr(ps(3, K * C, s * 128, (s + 1) * 128), L[:, s:s + C, :].rearrange("p j k -> p (j k)"), ident[:, :])
                last.then_inc(LT_made, 1)
                pe.wait_ge(segmax_made, t + 1)
                tr(ps(4, 128, 0, K * C), segmax[:, :], ident[0:K * C, 0:K * C]).then_inc(mT_made, 1)
                dense_part(t)
                if ahead:
                    target_rows(t + 1)
                else:
                    turn_weights(range(2, 8))
                pe.wait_ge(oh_made, t + 1)
                pe.wait_ge(ohk_made, t + 1)
                pe.wait_ge(V_made, t + 1 + CREDIT)
                for j in range(C):
                    last = mm(ps(5, W, 0, SUMS), oh[:, h, j * W:(j + 1) * W], V[:, j, :], start=j == 0, stop=j == C - 1)
                last.then_inc(agg_made, 1)
                step_rows(t)

            def turn_row(t):
                pe.wait_ge(hrow_made, t + 1)
                for c in range(CH):
                    last = tr(ps(5, 128, c * W, (c + 1) * W), hrow[:, c * 128:(c + 1) * 128], ident[0:W, 0:W])
                last.then_inc(hrow_turned, 1)

            def dense_part(t):
                pe.wait_ge(hTw_kept, t + 1)
                for c in range(CH):
                    mm(ps(6, W, 0, D), hTw[:, c * W:(c + 1) * W], VV[:, c, :], start=c == 0, stop=False)

            def step_rows(t):
                pe.wait_ge(means_made, 2 * t + 2)
                tr(ps(4, KR + RELS, 0, W), means[:, :], ident[0:W, 0:W]).then_inc(turned_made, 1)
                pe.wait_ge(meansT_made, t + 1)
                mm(ps(6, W, 0, D), meansT[0:KR, :], UV[:, :], start=False, stop=True).then_inc(grad_made, 1)

            pe.sem_inc(red_made, CREDIT)

            def gru(t, i, h):
                own_first = isinstance(t, int)
                turn_rows(t, i, h)
                pe.wait_ge(oh2_made, t + 1)
                for q, (a, b) in enumerate(CHUNKS2):
                    if q == (0 if own_first else 1):
                        own_gates(t, h)
                    pe.wait_ge(g_h[h][q], 16 * (b - a) * (i + 1))
                    for j in range(a, b):
                        for c in range(CH):
                            last = mm(ps(c, 128, 0, W), hg[h][:, j, c * 128:(c + 1) * 128], oh[:, h, j * W:(j + 1) * W],
                                      start=j == 0, stop=j == C - 1)
                last.then_inc(red_made, 1)
                gates(t, h)

            def turn_rows(t, i, h):
                pe.wait_ge(l_h2[h], 16 * (i + 1))
                for c in range(CH):
                    last = tr(ps(6, 128, c * W, (c + 1) * W), h2s[:, h, c * 128:(c + 1) * 128], ident[0:W, 0:W])
                last.then_inc(h2T_made, 1)

            def own_gates(t, h):
                rzb, nb = ((4, 5), (2, 3))[h]
                pe.wait_ge(cntT_kept, t + 1)
                mm(ps(rzb, W, 0, 2 * D), cntT[KR:, h, :], relw[KR:, 0:2 * D], start=True, stop=False)
                mm(ps(nb, W, 0, 2 * D), cntT[KR:, h, :], relw[KR:, 2 * D:4 * D], start=True, stop=False)
                pe.wait_ge(h2T_kept, t + 1)
                for c in range(CH):
                    mm(ps(rzb, W, 0, 2 * D), h2T[:, c * W:(c + 1) * W], whhT[:, c, 0:2 * D], start=False, stop=False)
                    mm(ps(nb, W, D, 2 * D), h2T[:, c * W:(c + 1) * W], whhT[:, c, 2 * D:3 * D], start=False, stop=False)

            def gates(t, h):
                rzb, nb = ((4, 5), (2, 3))[h]
                pe.wait_ge(red_kept, 2 * t + 2)
                for c in range(CH):
                    mm(ps(rzb, W, 0, 2 * D), redT[:, c * W:(c + 1) * W], wihT[:, c, 0:2 * D], start=False, stop=c == CH - 1)
                    last = mm(ps(nb, W, 0, D), redT[:, c * W:(c + 1) * W], wihT[:, c, 2 * D:3 * D], start=False, stop=c == CH - 1)
                last.then_inc(gates_made, 1)

            def windowed():
                target_rows(0)
                with pe.Fori(0, PAIRS) as i:
                    attend(2 * i, 0, True)
                    attend(2 * i + 1, 1, True)
                attend(NW - 1, 0, False)
                relation_products()
                pe.wait_ge(l_bias, 32)
                windows(pe, gru)

            def block_gru(t, i, h):
                turn_rows(t, i, h)
                own_gates(t, h)
                pe.sem_inc(red_made, 1)
                gates(t, h)

            def by_blocks():
                turn_weights()
                relation_products()
                for counted in (any_agg_made, any_red_made):
                    pe.sem_inc(counted, FREE)
                with pe.Fori(0, BLOCKS) as q:
                    pe.wait_ge(any_V, q + 1)
                    pe.wait_ge(any_ohk, q + 1)
                    pe.nop(nofuse=True)
                    with pe.Fori(0, NW) as t:
                        n = q * NW + t
                        pe.wait_ge(any_oh, n + 1)
                        pe.wait_ge(any_agg_kept, n + FREE)
                        for j in range(C):
                            last = mm(ps(5, W, 0, SUMS), oh[:, 0, j * W:(j + 1) * W], V[:, j, :], start=j == 0, stop=j == C - 1)
                        last.then_inc(any_agg_made, 1)

                pe.wait_ge(any_agg_kept, BLOCKS * NW + FREE)

                def finish(t, i, h):
                    turn_row(t)
                    dense_part(t)
                    step_rows(t)

                windows(pe, finish)
                with pe.Fori(0, BLOCKS) as q:
                    pe.wait_ge(any_g, 16 * C * (4 * BLOCKS + q + 1))
                    pe.nop(nofuse=True)
                    with pe.Fori(0, NW) as t:
                        n = q * NW + t
                        pe.wait_ge(any_oh, BLOCKS * NW + n + 1)
                        pe.wait_ge(any_red_kept, CH * n + FREE)
                        for j in range(C):
                            for c in range(CH):
                                last = mm(ps(c, 128, 0, W), hg[0][:, j, c * 128:(c + 1) * 128], oh[:, 0, j * W:(j + 1) * W],
                                          start=j == 0, stop=j == C - 1)
                        last.then_inc(any_red_made, 1)
                pe.wait_ge(any_red_kept, CH * BLOCKS * NW + FREE)
                pe.wait_ge(l_bias, 32)
                windows(pe, block_gru)

            way(pe, windowed, by_blocks)


def kernel(**inputs):
    import numpy as _np
    import concourse.bacc as _bacc
    from concourse import mybir as _mybir
    from concourse.bass_utils import run_bass_kernel_spmd as _run

    names = ["x", "edges", "L0_gnn_U", "L0_gnn_Dmat", "L0_gnn_head_w", "L1_gnn_relvectors",
             "L1_gnn_w_ih", "L1_gnn_w_hh", "L1_gnn_b_ih", "L1_gnn_b_hh"]
    nc = _bacc.Bacc("TRN2", target_bir_lowering=False, num_devices=1)
    behind = TILES * 128 + 256
    rows = []
    for name, before, after in (("src", 0, 0), ("dst", -1, PAD_NODE), ("edge_type_16", 0, 0)):
        a = _np.asarray(inputs[name])
        rows.append(_np.concatenate([_np.full(FRONT, before, a.dtype), a, _np.full(behind, after, a.dtype)]))
    arrays, args = {}, []
    for name in names:
        a = _np.stack(rows) if name == "edges" else _np.ascontiguousarray(inputs[name])
        arrays[f"in_{name}"] = a
        args.append(nc.dram_tensor(f"in_{name}", a.shape, _mybir.dt.from_np(a.dtype), kind="ExternalInput").ap())
    shape = inputs["x"].shape
    args.append(nc.dram_tensor("out_dram", shape, _mybir.dt.float32, kind="ExternalOutput").ap())
    gnn_kernel(nc, *args)
    return _run(nc, [arrays], core_ids=[0]).results[0]["out_dram"]
```
